# Optimizing a Trainium2 kernel written in Bass

```python
import numpy as np
import jax
import jax.numpy as jnp

def _softmax(x, axis=-1):
    return jax.nn.softmax(x, axis=axis)

def _gelu(x):
    return jax.nn.gelu(x, approximate=True)

def _silu(x):
    return jax.nn.silu(x)

def _sigmoid(x):
    return jax.nn.sigmoid(x)

def _layernorm(x, axis=-1, eps=1e-05):
    m = jnp.mean(x, axis=axis, keepdims=True)
    v = jnp.var(x, axis=axis, keepdims=True)
    return (x - m) / jnp.sqrt(v + eps)

def _scatter_add(tgt, idx, src, axis=0):
    return tgt.at[idx].add(src)

def _segment_sum(src, seg, n):
    return jax.ops.segment_sum(src, seg, n)
kernel_name = 'mk_seq_postln_d1_jaxref_r4_c0cd9e'

def setup_inputs(seed: int=0):
    np.random.seed(seed)
    _w = jnp.asarray

    def _L0_attn_setup():
        import jax, jax.numpy as jnp
        import numpy as np
        DIM = 256
        N_HEADS = 16
        HEAD_DIM = DIM // N_HEADS
        B, T = (2, 512)
        ROPE_THETA = 32.0
        EPS = 1e-06

        def precompute_freqs_1d(dim, seq_len, theta):
            freqs = theta ** (-jnp.arange(0, dim, 2, dtype=jnp.float32) / dim)
            t = jnp.arange(seq_len, dtype=jnp.float32)
            ang = t[:, None] * freqs[None, :]
            return (jnp.cos(ang), jnp.sin(ang))

        def _rms_norm(t, w):
            var = jnp.mean(t * t, axis=-1, keepdims=True)
            return t * jax.lax.rsqrt(var + EPS) * w

        def _rope(q, k, cos, sin):
            cos = cos[None, None]
            sin = sin[None, None]
            q1, q2 = jnp.split(q, 2, axis=-1)
            k1, k2 = jnp.split(k, 2, axis=-1)
            q_out = jnp.concatenate([q1 * cos - q2 * sin, q2 * cos + q1 * sin], axis=-1)
            k_out = jnp.concatenate([k1 * cos - k2 * sin, k2 * cos + k1 * sin], axis=-1)
            return (q_out, k_out)
        key = jax.random.key(seed)
        k1, k2, k3, k4, k5 = jax.random.split(key, 5)
        x = jax.random.normal(k1, (B, T, DIM), dtype=jnp.float32)
        w_qkv = jax.random.normal(k2, (3 * DIM, DIM), dtype=jnp.float32) * DIM ** (-0.5)
        w_proj = jax.random.normal(k3, (DIM, DIM), dtype=jnp.float32) * DIM ** (-0.5)
        q_norm_w = 1.0 + 0.1 * jax.random.normal(k4, (HEAD_DIM,), dtype=jnp.float32)
        k_norm_w = 1.0 + 0.1 * jax.random.normal(k5, (HEAD_DIM,), dtype=jnp.float32)
        return {'x': x, 'w_qkv': w_qkv, 'w_proj': w_proj, 'q_norm_w': q_norm_w, 'k_norm_w': k_norm_w}
    _L0_attn_in = _L0_attn_setup()

    def _L0_ffn_setup():
        import jax, jax.numpy as jnp
        import numpy as np
        D, H, O, E, TOPK = (256, 1024, 256, 8, 2)
        B, S = (4, 256)
        key = jax.random.key(seed)
        ks = jax.random.split(key, 12)
        std = 0.02
        return {'hidden_states': jax.random.normal(ks[0], (B, S, D), dtype=jnp.float32), 'norm_weight': jnp.ones((D,), dtype=jnp.float32), 'router_w': jax.random.normal(ks[1], (E, D), dtype=jnp.float32) * std, 'sw1': jax.random.normal(ks[2], (D, H), dtype=jnp.float32) * (1.0 / np.sqrt(D)), 'sb1': jnp.zeros((H,), dtype=jnp.float32), 'sw2': jax.random.normal(ks[3], (H, O), dtype=jnp.float32) * (1.0 / np.sqrt(H)), 'sb2': jnp.zeros((O,), dtype=jnp.float32), 'ew1': jax.random.normal(ks[4], (E, D, H), dtype=jnp.float32) * (1.0 / np.sqrt(D)), 'eb1': jnp.zeros((E, H), dtype=jnp.float32), 'ew2': jax.random.normal(ks[5], (E, H, O), dtype=jnp.float32) * (1.0 / np.sqrt(H)), 'eb2': jnp.zeros((E, O), dtype=jnp.float32)}
    _L0_ffn_in = _L0_ffn_setup()
    _d = {'L0_attn_x': _L0_attn_in['x'], 'L0_attn_w_qkv': _L0_attn_in['w_qkv'], 'L0_attn_w_proj': _L0_attn_in['w_proj'], 'L0_attn_q_norm_w': _L0_attn_in['q_norm_w'], 'L0_attn_k_norm_w': _L0_attn_in['k_norm_w'], 'L0_ffn_norm_weight': _L0_ffn_in['norm_weight'], 'L0_ffn_router_w': _L0_ffn_in['router_w'], 'L0_ffn_sw1': _L0_ffn_in['sw1'], 'L0_ffn_sb1': _L0_ffn_in['sb1'], 'L0_ffn_sw2': _L0_ffn_in['sw2'], 'L0_ffn_sb2': _L0_ffn_in['sb2'], 'L0_ffn_ew1': _L0_ffn_in['ew1'], 'L0_ffn_eb1': _L0_ffn_in['eb1'], 'L0_ffn_ew2': _L0_ffn_in['ew2'], 'L0_ffn_eb2': _L0_ffn_in['eb2']}
    _x0 = _d['L0_attn_x']
    _d['L0_attn_x'] = jax.random.normal(jax.random.fold_in(jax.random.key(seed), 1), (8, 512, 256), dtype=_x0.dtype)
    del _x0
    return _d

def reference(L0_attn_x, L0_attn_w_qkv, L0_attn_w_proj, L0_attn_q_norm_w, L0_attn_k_norm_w, L0_ffn_norm_weight, L0_ffn_router_w, L0_ffn_sw1, L0_ffn_sb1, L0_ffn_sw2, L0_ffn_sb2, L0_ffn_ew1, L0_ffn_eb1, L0_ffn_ew2, L0_ffn_eb2):

    def _L0_attn_ref(x, w_qkv, w_proj, q_norm_w, k_norm_w):
        import jax, jax.numpy as jnp
        import numpy as np
        DIM = 256
        N_HEADS = 16
        HEAD_DIM = DIM // N_HEADS
        B, T = (2, 512)
        ROPE_THETA = 32.0
        EPS = 1e-06

        def precompute_freqs_1d(dim, seq_len, theta):
            freqs = theta ** (-jnp.arange(0, dim, 2, dtype=jnp.float32) / dim)
            t = jnp.arange(seq_len, dtype=jnp.float32)
            ang = t[:, None] * freqs[None, :]
            return (jnp.cos(ang), jnp.sin(ang))

        def _rms_norm(t, w):
            var = jnp.mean(t * t, axis=-1, keepdims=True)
            return t * jax.lax.rsqrt(var + EPS) * w

        def _rope(q, k, cos, sin):
            cos = cos[None, None]
            sin = sin[None, None]
            q1, q2 = jnp.split(q, 2, axis=-1)
            k1, k2 = jnp.split(k, 2, axis=-1)
            q_out = jnp.concatenate([q1 * cos - q2 * sin, q2 * cos + q1 * sin], axis=-1)
            k_out = jnp.concatenate([k1 * cos - k2 * sin, k2 * cos + k1 * sin], axis=-1)
            return (q_out, k_out)
        Bc, Tc, C = x.shape
        scale = HEAD_DIM ** (-0.5)
        qkv = x @ w_qkv.T
        qkv = qkv.reshape(Bc, Tc, 3, N_HEADS, HEAD_DIM).transpose(2, 0, 3, 1, 4)
        q, k, v = (qkv[0], qkv[1], qkv[2])
        q = _rms_norm(q, q_norm_w)
        k = _rms_norm(k, k_norm_w)
        cos, sin = precompute_freqs_1d(HEAD_DIM, Tc, ROPE_THETA)
        q, k = _rope(q, k, cos, sin)
        attn = jnp.einsum('bhqd,bhkd->bhqk', q, k) * scale
        causal = jnp.triu(jnp.ones((Tc, Tc), dtype=bool), k=1)
        attn = jnp.where(causal, -jnp.inf, attn)
        attn = jax.nn.softmax(attn, axis=-1)
        out = jnp.einsum('bhqk,bhkd->bhqd', attn, v)
        out = out.transpose(0, 2, 1, 3).reshape(Bc, Tc, C)
        return out @ w_proj.T

    def _L0_ffn_ref(hidden_states, norm_weight, router_w, sw1, sb1, sw2, sb2, ew1, eb1, ew2, eb2):
        import jax, jax.numpy as jnp
        import numpy as np
        D, H, O, E, TOPK = (256, 1024, 256, 8, 2)
        B, S = (4, 256)
        b, s, d = hidden_states.shape
        var = jnp.mean(jnp.square(hidden_states), axis=-1, keepdims=True)
        normed = hidden_states * jax.lax.rsqrt(var + 1e-08) * norm_weight
        shared = jnp.maximum(normed @ sw1 + sb1, 0.0) @ sw2 + sb2
        flat = normed.reshape(-1, d)
        T = flat.shape[0]
        probs = jax.nn.sigmoid(flat @ router_w.T)
        scores, idx = jax.lax.top_k(probs, TOPK)
        w = scores / (jnp.sum(scores, axis=-1, keepdims=True) + 1e-06)
        comb = jnp.zeros((T, E), dtype=flat.dtype)
        comb = comb.at[jnp.arange(T)[:, None], idx].add(w)
        h = jnp.maximum(jnp.einsum('td,edh->teh', flat, ew1) + eb1[None, :, :], 0.0)
        eo = jnp.einsum('teh,eho->teo', h, ew2) + eb2[None, :, :]
        routed = jnp.einsum('teo,te->to', eo, comb)
        return shared + routed.reshape(b, s, -1)
    x = L0_attn_x
    x = _layernorm(x + _L0_attn_ref(x, L0_attn_w_qkv, L0_attn_w_proj, L0_attn_q_norm_w, L0_attn_k_norm_w), axis=-1)
    x = _layernorm(x + _L0_ffn_ref(x, L0_ffn_norm_weight, L0_ffn_router_w, L0_ffn_sw1, L0_ffn_sb1, L0_ffn_sw2, L0_ffn_sb2, L0_ffn_ew1, L0_ffn_eb1, L0_ffn_ew2, L0_ffn_eb2), axis=-1)
    return x

_drawn_inputs = setup_inputs


def setup_inputs(seed=0):
    import zlib

    import numpy as np

    out = dict(_drawn_inputs(seed))
    spreads = {'L0_ffn_norm_weight': (1.0, 0.2),
     'L0_ffn_sb1': (0.0, 0.1),
     'L0_ffn_sb2': (0.0, 0.1),
     'L0_ffn_eb1': (0.0, 0.1),
     'L0_ffn_eb2': (0.0, 0.1)}
    factors = {}
    for name, (base, spread) in spreads.items():
        noise = np.random.default_rng([zlib.crc32(name.encode()), seed]).standard_normal(out[name].shape)
        drawn = base * np.exp(spread * noise) if base else spread * noise
        out[name] = jnp.asarray(drawn.astype(out[name].dtype))
    for name, factor in factors.items():
        out[name] = (out[name] * factor).astype(out[name].dtype)
    return out
```

```python
from contextlib import ExitStack

import numpy as np

import concourse.bass as bass
from concourse import mybir

ALU = mybir.AluOpType
ACT = mybir.ActivationFunctionType
AX = mybir.AxisListType
F32 = mybir.dt.float32
F16 = mybir.dt.float16
BF16 = mybir.dt.bfloat16
I32 = mybir.dt.int32
U32 = mybir.dt.uint32

P = 128
NB, T, D = 8, 512, 256
NH, HD = 16, 16
NT = T // P
DC = D // P
NTOK = NB * T
NTILE = NTOK // P
ROPE_THETA = 32.0
RMS_EPS = 1e-6
LN_EPS = 1e-5
FFN_EPS = 1e-8
ATT_SCALE = HD ** -0.5
WS = 16.0
RS = 64.0
SEG = (0, 512, 1024, 896)
PW = 1280

NE, H = 8, 1024
HC = H // P
SHARED = NE
REGION = NTOK
TT = 256
TOPK = 2
N_SHARED = NTOK // TT
N_ROUTED = (TOPK * NTOK) // TT + NE - 1
SPARE = (NE + 1) * REGION
N_ROWS = SPARE + (NE - 1) * TT
WE = DC * H


def rope_tables():
    freqs = np.float32(ROPE_THETA) ** (-np.arange(0, HD, 2, dtype=np.float32) / np.float32(HD))
    ang = np.arange(T, dtype=np.float32)[:, None] * freqs[None, :].astype(np.float32)
    return np.stack([np.cos(ang), np.sin(ang)], axis=1).astype(np.float32)



def order(*jobs):
    by = sorted((p, k, name, t) for k, (name, pos) in enumerate(jobs) for t, p in enumerate(pos))
    return {(name, t): i for i, (_, _, name, t) in enumerate(by)}


P_QK = (1, 3, 6, 9)
P_V = (2, 4, 7, 10)
P_T = (5, 8, 11, 14)
P_NAT = (1, 3, 5, 7)
P_AT = tuple(p + 1 for p in P_NAT)
P_PROJ = tuple(p + 2 for p in P_NAT)
P_XN = tuple(p + 4 for p in P_NAT)
P_LG = tuple(p + 5 for p in P_NAT)
P_RANK = tuple(p + 7 for p in P_NAT)
P_BIAS = tuple(p + 8 for p in P_NAT)
POSITIONS = 17
MA = order(("qk", P_QK), ("v", P_V), ("t", P_T))
MB = order(("nat", P_NAT), ("at", P_AT), ("proj", P_PROJ))
MC = order(("xn", P_XN), ("lg", P_LG), ("rank", P_RANK), ("bias", P_BIAS))


def at(positions, p):
    return [t for t in range(NT) if positions[t] == p]


def wait_apart(eng, S, name, count):
    eng.wait_ge(S(name), count)
    eng.sem_inc(S("passed"), 1)


def tiles(b, t):
    return b * NT + t + 1


def attention_block(nc, a, S, keep):
    with ExitStack() as ctx:
        def sb(name, shape, dt):
            return ctx.enter_context(nc.sbuf_tensor(name, shape, dt))

        def ps(name, cols):
            return ctx.enter_context(nc.psum_tensor(name, [P, cols], F32))

        stage = sb("stage", [P, DC, 4 * D + NE], F32)
        wqkv = sb("wqkv", [P, 2, DC, 3 * D], F16)
        wproj = sb("wproj", [P, 2, DC, D], F16)
        wrout = sb("wrout", [P, 2, DC, NE], F16)
        ident_f = sb("ident_f", [P, P], F32)
        ident_h = keep["ident"]
        ident_b = sb("ident_b", [P, P], BF16)
        mask_b = sb("mask_b", [P, P], BF16)
        tri_h = sb("tri_h", [P, P], F16)
        ones_h = sb("ones_h", [P, P], F16)
        iota_i = sb("iota_i", [P, 2, NE], I32)
        iota_e = sb("iota_e", [P, 2, NE], F32)
        trig = sb("trig", [P, NT, 2, HD // 2], F32)
        nw = sb("nw", [P, 2, HD], F32)
        ctab = sb("ctab", [P, NT, 2, HD], F32)
        stab = sb("stab", [P, NT, 2, HD], F32)
        ffn_nw = sb("ffn_nw", [P, D], F32)
        bias2 = sb("bias2", [NE + 1, D], F32)
        mhalf = sb("mhalf", [P, NH], F32)
        zeros_i = sb("zeros_i", [P, SHARED * REGION // P], I32)
        tokid = sb("tokid", [P, NTILE], I32)
        in_order = sb("in_order", [P, NTILE], I32)
        xTf = sb("xTf", [P, DC, T], F32)
        xTh = sb("xTh", [P, 2, DC, T], F16)
        sq = sb("sq", [P, 2 * D], F32)
        ms = sb("ms", [P, NT, 2 * NH], F32)
        rn = sb("rn", [P, NT, 2 * NH], F32)
        rot = sb("rot", [P, 2, 2 * D], F32)
        rsum = sb("rsum", [P, 2, 2 * D], F32)
        qn = sb("qn", [P, 2 * D], F32)
        nat = sb("nat", [P, NT, 2, 2 * D], F16)
        qkT = sb("qkT", [P, 8, T], F16)
        stk = sb("stk", [P, 2, 2, 8, T], F16)
        vst = sb("vst", [P, 2, NT, NH, 32], F32)
        prob = sb("prob", [P, 2, 4, PW], F32)
        raw = sb("raw", [P, 2, 4, T], F32)
        xin = sb("xin", [P, NT, D], F32)
        rcp = sb("rcp", [P, NT, NH], F32)
        an = sb("an", [P, D], F32)
        anh = sb("anh", [P, NT, 2, D], F16)
        aT = sb("aT", [P, NT, 4, P], F16)
        y0 = sb("y0", [P, NT, D], F32)
        st6 = sb("st6", [P, NT, 6], F32)
        mv = sb("mv", [P, NT, 2], F32)
        vv = sb("vv", [P, NT, 6], F32)
        x1 = sb("x1", [P, NT, D], F32)
        xnf = sb("xnf", [P, D], F32)
        xnh = sb("xnh", [P, NT, 2, D], F16)
        xnT = sb("xnT", [P, NT, 4, P], F16)
        lg = sb("lg", [P, NT, NE], F32)
        mx = sb("mx", [P, NT, 8], F32)
        ix = sb("ix", [P, NT, 8], U32)
        ixf = sb("ixf", [P, NT, 2], F32)
        oh = sb("oh", [P, NT, 2, NE], F32)
        mh = sb("mh", [P, NT, NE], F16)
        msum = keep["msum"]
        ex = sb("ex", [P, NT, 2], F32)
        pr = sb("pr", [P, NT, 2], F32)
        pr1 = sb("pr1", [P, NT, 2], F32)
        tot = sb("tot", [P, NT, 2], F32)
        wt = sb("wt", [P, NT, 2], F32)
        comb = sb("comb", [P, NT, NE + 1], F32)
        comb1 = sb("comb1", [P, NT, NE], F32)
        combT = sb("combT", [NE + 1, NT, P], F32)
        sl = sb("sl", [P, NT, NE], F32)
        slm = sb("slm", [P, NT, 2, NE], F32)
        slf = sb("slf", [P, NT, 2], F32)
        sl_i = sb("sl_i", [P, NT, 2], I32)
        tok_i = sb("tok_i", [P, NT], I32)
        res = sb("res", [P, NT, D], F32)

        slots = (ps("slot0", 1024), ps("slot1", 1024))
        pv_bank = ps("pv_bank", T)
        ma = ps("ma", T)
        mb = ps("mb", T)
        mc = ps("mc", T)

        def turns(eng, turn):
            turn(-1, 1, True, False, False)
            turn(0, 0, True, True, False)
            with eng.Fori(0, (NB - 2) // 2) as it:
                turn(it * 2 + 1, 1, True, True, True)
                turn(it * 2 + 2, 0, True, True, True)
            turn(NB - 1, 1, False, True, True)
            turn(NB, 0, False, False, True)

        with nc.Block() as block:
            @block.sync
            def _(sp):
                w = 3 * D
                for c in range(DC):
                    for lo, hi, src in ((0, w, "wqkvT"), (w, w + D, "wprojT"), (w + D, w + D + NE, "routT")):
                        sp.dma_start(stage[:, c, lo:hi], a[src][c * P:(c + 1) * P, :]).then_inc(S("w_loaded"), 16)
                sp.dma_start(trig[:], a["trig"].rearrange("(t p) s f -> p t s f", p=P)).then_inc(S("c_loaded"), 16)
                sp.dma_start(nw[:, 0, :], a["qnw"].partition_broadcast(P)).then_inc(S("c_loaded"), 16)
                sp.dma_start(nw[:, 1, :], a["knw"].partition_broadcast(P)).then_inc(S("c_loaded"), 16)
                sp.dma_start(ffn_nw[:], a["ffn_nw"].partition_broadcast(P)).then_inc(S("c_loaded"), 16)
                sp.dma_start(bias2[:], a["b2all"]).then_inc(S("c_loaded"), 16)

                def load_xT(b):
                    sp.dma_start(xTf[:], a["xT"][bass.ds(b * D, D), :].rearrange("(c p) t -> p c t", p=P)
                                 ).then_inc(S("xT_loaded"), 16)

                load_xT(0)
                sp.wait_ge(S("const_ready"), 1)
                sp.dma_start(a["table"][0:SHARED * REGION, :].rearrange("(p c) o -> p (c o)", p=P),
                             zeros_i[:, :]).then_inc(S("table_init"), 16)
                sp.dma_start(a["table"][SPARE:N_ROWS, :].rearrange("(p c) o -> p (c o)", p=P),
                             zeros_i[:, 0:(N_ROWS - SPARE) // P]).then_inc(S("table_init"), 16)
                sp.dma_start(a["table"][SHARED * REGION:SPARE, :].rearrange("(p c) o -> p (c o)", p=P),
                             in_order[:, :]).then_inc(S("table_init"), 16)

                def turn(b, par, front, attend, back):
                    for p in range(POSITIONS):
                        if p == 1 and front and not (isinstance(b, int) and b + 2 >= NB):
                            wait_apart(sp, S, "xT_split", b + 2)
                            load_xT((b + 2) % NB)
                        for t in at(P_T, p):
                            if front and t % 2:
                                h0 = (t - 1) * P
                                half = slice(h0, h0 + 2 * P)
                                sp.wait_ge(S("ma_free"), (b + 1) * 12 + MA["t", t] + 2)
                                sp.dma_start(a["qk_dram"][:, :, half].rearrange("k p t -> p k t"),
                                             qkT[:, :, half]).then_inc(S("qk_out"), 16)
                                sp.wait_ge(S("qk_out"), ((b + 1) * 2 + (t // 2) + 1) * 16)
                                for qk in range(2):
                                    for cc in range(DC):
                                        for s in range(4):
                                            hl = s // 2 if qk == 0 else s % 2
                                            row = 64 * cc + HD * s
                                            sp.dma_start(
                                                stk[row:row + HD, 1 - par, qk, :, half],
                                                a["qk_dram"][hl * 4 + qk * 2 + cc, :, half]
                                                .rearrange("(i d) t -> d i t", d=HD)).then_inc(S("stk_in"), 16)
                        for t in at(P_XN, p):
                            if back:
                                wait_apart(sp, S, "xn_lo", tiles(b - 1, t))
                                sp.dma_start(a["xn_rows"][bass.ds(((b - 1) * NT + t) * P, P), :],
                                             xnh[:, t, :, :].rearrange("p h d -> p (h d)")
                                             ).then_inc(S("xn_stored"), 16)
                        for t in at(P_BIAS, p):
                            if back:
                                wait_apart(sp, S, "res_ready", tiles(b - 1, t))
                                sp.dma_start(a["resid"][bass.ds(((b - 1) * NT + t) * P, P), :],
                                             res[:, t, :]).then_inc(S("res_stored"), 16)
                    if attend:
                        if back:
                            wait_apart(sp, S, "y0_done", tiles(b - 1, NT - 1))
                        sp.dma_start(xin[:], a["x"][bass.ds(b * T, T), :].rearrange("(t p) d -> p t d", p=P)
                                     ).then_inc(S("xin_loaded"), 16)
                    if back:
                        sp.wait_ge(S("xn_stored"), b * (NT * 16))
                        sp.wait_ge(S("res_stored"), b * (NT * 16))
                    sp.sem_inc(S("stores_out"), 1)

                turns(sp, turn)
                sp.wait_ge(S("stk_in"), 16 * 32 * NB)
                sp.wait_ge(S("xT_loaded"), 16 * (NB + 1))

            @block.gpsimd
            def _(pool):
                pool.memset(ident_f[:], 0.0).then_inc(S("made"), 1)
                pool.memset(mask_b[:], 0.0).then_inc(S("made"), 1)
                pool.memset(tri_h[:], 1.0).then_inc(S("made"), 1)
                pool.memset(zeros_i[:], 0).then_inc(S("made"), 1)
                pool.iota(tokid[:], pattern=[[P, NTILE]], base=0, channel_multiplier=1).then_inc(S("made"), 1)
                pool.memset(mhalf[:], -0.5).then_inc(S("made"), 1)
                pool.iota(iota_i[:, 0, :], pattern=[[1, NE]], base=0, channel_multiplier=0).then_inc(S("made"), 1)
                pool.iota(iota_i[:, 1, :], pattern=[[REGION, NE]], base=0, channel_multiplier=0).then_inc(S("made"), 1)
                pool.iota(in_order[:], pattern=[[1, NTILE]], base=0, channel_multiplier=NTILE).then_inc(S("made"), 1)
                pool.memset(ones_h[:], 1.0).then_inc(S("made"), 1)
                pool.wait_ge(S("made"), 10)
                pool.affine_select(out=ident_f[:], in_=ident_f[:], compare_op=ALU.not_equal, fill=1.0, base=0,
                                   pattern=[[-1, P]], channel_multiplier=1).then_inc(S("made"), 1)
                pool.affine_select(out=mask_b[:], in_=mask_b[:], compare_op=ALU.is_ge, fill=-1e30, base=0,
                                   pattern=[[1, P]], channel_multiplier=-1).then_inc(S("made"), 1)
                pool.affine_select(out=tri_h[:], in_=tri_h[:], compare_op=ALU.is_gt, fill=0.0, base=0,
                                   pattern=[[1, P]], channel_multiplier=-1).then_inc(S("made"), 1)
                pool.wait_ge(S("made"), 13)
                pool.tensor_copy(ident_h[:], ident_f[:]).then_inc(S("made"), 1)
                pool.tensor_copy(ident_b[:], ident_f[:]).then_inc(S("made"), 1)
                pool.wait_ge(S("made"), 15)
                pool.sem_inc(S("const_ready"), 1)
                pool.wait_ge(S("table_init"), 48)

                def turn(b, par, front, attend, back):
                    for p in range(POSITIONS):
                        for t in at(P_PROJ, p):
                            if back:
                                k = tiles(b - 1, t)
                                pool.wait_ge(S("var_ready"), k)
                                pool.tensor_tensor(vv[:, t, 1:2], vv[:, t, 0:1], mhalf[:, 0:1], ALU.pow).then_inc(S("rstd"), 1)
                                pool.wait_ge(S("rstd"), k)
                                pool.tensor_tensor(vv[:, t, 2:3], vv[:, t, 1:2], vv[:, t, 1:2], ALU.mult).then_inc(S("rstd_sq"), 1)
                                pool.wait_ge(S("rstd_sq"), k)
                                pool.tensor_tensor(vv[:, t, 3:4], vv[:, t, 2:3], mv[:, t, 1:2], ALU.mult).then_inc(S("msq"), 1)
                                wait_apart(pool, S, "msq", k)
                                pool.tensor_scalar(vv[:, t, 4:5], vv[:, t, 3:4], FFN_EPS, None, ALU.add).then_inc(S("msq_eps"), 1)
                                pool.wait_ge(S("msq_eps"), k)
                                pool.tensor_tensor(vv[:, t, 5:6], vv[:, t, 4:5], mhalf[:, 0:1], ALU.pow).then_inc(S("norms_ready"), 1)
                        for t in at(P_BIAS, p):
                            if back:
                                wait_apart(pool, S, "slots_ready", tiles(b - 1, t))
                                for k in range(TOPK):
                                    pool.indirect_dma_start(
                                        a["table"], bass.IndirectOffsetOnAxis(ap=sl_i[:, t, k:k + 1], axis=0),
                                        tok_i[:, t:t + 1], None).then_inc(S("scattered"), 16)
                        for t in range(NT):
                            for q in range(4):
                                if front and p == P_QK[t] + min(q, 2):
                                    pool.wait_ge(S("ms_ready"), tiles(b + 1, t))
                                    h = slice(q * NH // 2, (q + 1) * NH // 2)
                                    pool.tensor_tensor(rn[:, t, h], ms[:, t, h], mhalf[:, 0:NH // 2],
                                                       ALU.pow).then_inc(S("rn_ready"), 1)
                    if back:
                        pool.wait_ge(S("scattered"), b * (NT * TOPK * 16))
                    pool.sem_inc(S("ids_out"), 1)

                turns(pool, turn)

            @block.scalar
            def _(act):
                act.wait_ge(S("w_loaded"), 16 * 3 * DC)
                w = 3 * D
                act.activation(wqkv[:, 0, :, :], stage[:, :, 0:w], ACT.Copy, scale=WS).then_inc(S("w_hi"), 1)
                act.activation(wproj[:, 0, :, :], stage[:, :, w:w + D], ACT.Copy, scale=WS).then_inc(S("w_hi"), 1)
                act.activation(wrout[:, 0, :, :], stage[:, :, w + D:], ACT.Copy, scale=RS).then_inc(S("w_hi"), 1)
                act.wait_ge(S("tables_ready"), 1)

                def turn(b, par, front, attend, back):
                    if front:
                        act.wait_ge(S("xT_loaded"), (b + 2) * 16)
                        if not isinstance(b, int) or b >= 0:
                            act.wait_ge(S("v_done"), tiles(b, NT - 1))
                        act.activation(xTh[:, 0, :, :], xTf[:, :, :], ACT.Copy).then_inc(S("xT_hi"), 1)
                    for p in range(POSITIONS):
                        g = p // 4
                        if attend and p < 16:
                            for u in ((0, 1), (2,), (3,), (4, 5))[p % 4]:
                                act.wait_ge(S("unit_ready"), b * 24 + g * 6 + u + 1)
                                if u == 0 and (not isinstance(b, int) or b * 4 + g >= 2):
                                    act.wait_ge(S("pv_done"), b * 4 + g - 1)
                                slot = slots[u % 2]
                                pp = prob[:, g % 2]
                                if u in (2, 5):
                                    r = 0 if u == 2 else 2
                                    act.activation(pp[:, r:r + 2, 1024:PW],
                                                   slot[:, 0:512].rearrange("p (r q) -> p r q", r=2),
                                                   ACT.Exp, scale=ATT_SCALE).then_inc(S("exp_done"), 1)
                                else:
                                    r = (0, 1, None, 2, 3)[u]
                                    act.activation(pp[:, r, 0:1024], slot[:, 0:1024], ACT.Exp,
                                                   scale=ATT_SCALE).then_inc(S("exp_done"), 1)
                        if p % 4 == 0 and ((p == 0 and back) or (0 < p < 16 and attend)):
                            s = b * 4 + g
                            act.wait_ge(S("pv_done"), s)
                            act.activation(raw[:, (1 - par) if p == 0 else par, (g - 1) % 4, :], pv_bank[:, :],
                                           ACT.Copy).then_inc(S("raw_done"), 1)
                        for t in at(P_QK, p):
                            if front:
                                act.wait_ge(S("qk_done"), tiles(b + 1, t))
                                act.activation(sq[:], ma[:, :], ACT.Square).then_inc(S("sq_ready"), 1)
                        for t in at(P_V, p):
                            if front:
                                act.wait_ge(S("v_done"), tiles(b + 1, t))
                                act.activation(vst[:, 1 - par, t, :, 0:HD],
                                               ma[:, 0:D].rearrange("p (h d) -> p h d", d=HD), ACT.Copy,
                                               scale=1.0 / WS).then_inc(S("ma_free"), 1)
                        for t in at(P_T, p):
                            if front:
                                act.wait_ge(S("t_done"), tiles(b + 1, t))
                                act.activation(qkT[:, :, t * P:(t + 1) * P],
                                               ma[:, :].bitcast(F16).rearrange("p (k t) -> p k t", k=8),
                                               ACT.Copy).then_inc(S("ma_free"), 1)
                        for t in at(P_AT, p):
                            if back:
                                act.wait_ge(S("at_done"), tiles(b - 1, t))
                                act.activation(aT[:, t, :, :].rearrange("p k t -> p (k t)"),
                                               mb[:, 0:2 * P].bitcast(F16), ACT.Copy).then_inc(S("mb_free"), 1)
                        for t in at(P_XN, p):
                            if back:
                                act.wait_ge(S("xnT_done"), tiles(b - 1, t))
                                act.activation(xnT[:, t, :, :].rearrange("p k t -> p (k t)"),
                                               mc[:, 0:2 * P].bitcast(F16), ACT.Copy).then_inc(S("mc_free"), 1)
                        for t in at(P_LG, p):
                            if back:
                                act.wait_ge(S("top_ready"), tiles(b - 1, t))
                                act.activation(ex[:, t, :], mx[:, t, 0:2], ACT.Exp, scale=-1.0).then_inc(S("ex_ready"), 1)

                turns(act, turn)

            @block.vector
            def _(dve):
                def then(ins, name, count):
                    ins.then_inc(S(name), 1)
                    dve.wait_ge(S(name), count)

                def then_apart(ins, name, count):
                    ins.then_inc(S(name), 1)
                    wait_apart(dve, S, name, count)

                for bank in ("ma_free", "mb_free", "mc_free"):
                    dve.sem_inc(S(bank), 1)
                dve.memset(vst[:].rearrange("p a t h d -> p (a t h d)"), 0.0).then_inc(S("vst_zero"), 1)
                dve.memset(comb[:], 1.0).then_inc(S("vst_zero"), 1)
                dve.memset(msum[:], 0.0).then_inc(S("msum_free"), 1)
                dve.wait_ge(S("vst_zero"), 2)
                dve.memset(vst[:].rearrange("p a t h d -> p (a t h) d")[:, :, HD:HD + 1], 1.0).then_inc(S("vst_one"), 1)
                dve.wait_ge(S("const_ready"), 1)
                dve.tensor_copy(iota_e[:], iota_i[:]).then_inc(S("vst_one"), 1)
                dve.wait_ge(S("w_hi"), 3)
                w = 3 * D
                for k, (dst, lo, hi, scale) in enumerate(((wqkv, 0, w, WS), (wproj, w, w + D, WS),
                                                          (wrout, w + D, w + D + NE, RS))):
                    dve.scalar_tensor_tensor(dst[:, 1, :, :], stage[:, :, lo:hi], scale, dst[:, 0, :, :],
                                             ALU.mult, ALU.subtract).then_inc(S("w_lo"), 1)
                dve.wait_ge(S("c_loaded"), 80)
                hh = HD // 2
                for qk in range(2):
                    for half in range(2):
                        here = slice(half * hh, half * hh + hh)
                        other = slice(hh - half * hh, HD - half * hh)
                        wb = nw[:, qk, here].unsqueeze(1).broadcast_to([P, NT, hh])
                        wo = nw[:, qk, other].unsqueeze(1).broadcast_to([P, NT, hh])
                        dve.scalar_tensor_tensor(ctab[:, :, qk, here], trig[:, :, 0, :], 1.0 / WS, wb,
                                                 ALU.mult, ALU.mult).then_inc(S("rope_made"), 1)
                        dve.scalar_tensor_tensor(stab[:, :, qk, here], trig[:, :, 1, :], (2 * half - 1) / WS, wo,
                                                 ALU.mult, ALU.mult).then_inc(S("rope_made"), 1)
                dve.wait_ge(S("rope_made"), 8)
                dve.wait_ge(S("vst_one"), 2)
                dve.wait_ge(S("w_lo"), 3)
                dve.sem_inc(S("tables_ready"), 1)

                def turn(b, par, front, attend, back):
                    if front:
                        dve.wait_ge(S("xT_hi"), b + 2)
                        dve.tensor_tensor(xTh[:, 1, :, :], xTf[:, :, :], xTh[:, 0, :, :],
                                          ALU.subtract).then_inc(S("xT_split"), 1)
                    for p in range(POSITIONS):
                        for t in at(P_XN, p):
                            if back:
                                k = tiles(b - 1, t)
                                dve.wait_ge(S("norms_ready"), k)
                                then(dve.tensor_scalar(x1[:, t, :], y0[:, t, :], mv[:, t, 0:1], vv[:, t, 1:2],
                                                       ALU.subtract, ALU.mult), "x1_done", k)
                                then(dve.scalar_tensor_tensor(xnf[:], x1[:, t, :], vv[:, t, 5:6], ffn_nw[:],
                                                              ALU.mult, ALU.mult), "xnf_done", k)
                                dve.wait_ge(S("stores_out"), b + 1)
                                then(dve.tensor_copy(xnh[:, t, 0, :], xnf[:]), "xn_hi", k)
                                then(dve.tensor_tensor(xnh[:, t, 1, :], xnf[:], xnh[:, t, 0, :],
                                                       ALU.subtract), "xn_lo", k)
                        for t in range(NT):
                            if back and p == P_LG[t] + 1:
                                k = tiles(b - 1, t)
                                dve.wait_ge(S("ex_ready"), k)
                                then(dve.tensor_scalar(pr1[:, t, :], ex[:, t, :], 1.0, None, ALU.add), "sig_den", k)
                                then(dve.reciprocal(pr[:, t, :], pr1[:, t, :]), "sig", k)
                                then(dve.scalar_tensor_tensor(tot[:, t, 0:1], pr[:, t, 0:1], 1e-6, pr[:, t, 1:2],
                                                              ALU.add, ALU.add), "sig_sum", k)
                                then(dve.reciprocal(tot[:, t, 1:2], tot[:, t, 0:1]), "sig_rcp", k)
                                then(dve.tensor_scalar(wt[:, t, :], pr[:, t, :], tot[:, t, 1:2], None, ALU.mult), "wt_done", k)
                                dve.tensor_copy(keep["weights"][:, bass.ds(((b - 1) * NT + t) * 2, 2)], wt[:, t, :]
                                                ).then_inc(S("kept"), 1)
                                then(dve.tensor_scalar(comb1[:, t, :], oh[:, t, 1, :], wt[:, t, 1:2], None, ALU.mult), "comb1", k)
                                dve.scalar_tensor_tensor(comb[:, t, 0:NE], oh[:, t, 0, :], wt[:, t, 0:1], comb1[:, t, :],
                                                         ALU.mult, ALU.add).then_inc(S("comb_ready"), 1)
                            if front and p == P_T[t] - 1:
                                k = tiles(b + 1, t)
                                dve.wait_ge(S("rn_ready"), k * 4)
                                then(dve.tensor_tensor(qn[:].rearrange("p (h d) -> p h d", d=HD),
                                                       rsum[:, t % 2, :].rearrange("p (h d) -> p h d", d=HD),
                                                       rn[:, t, :].unsqueeze(2).broadcast_to([P, 2 * NH, HD]),
                                                       ALU.mult), "qn_done", k)
                                then(dve.tensor_copy(nat[:, t, 0, :], qn[:]), "nat_hi", k)
                                then(dve.tensor_tensor(nat[:, t, 1, :], qn[:], nat[:, t, 0, :],
                                                       ALU.subtract), "nat_ready", k)
                        for t in at(P_QK, p):
                            if front:
                                k = tiles(b + 1, t)
                                dve.wait_ge(S("sq_ready"), k)
                                then(dve.tensor_reduce(ms[:, t, :], sq[:].rearrange("p (h d) -> p h d", d=HD),
                                                       AX.X, ALU.add), "ss_done", k)
                                dve.tensor_scalar(ms[:, t, :], ms[:, t, :], 1.0 / (HD * WS * WS), RMS_EPS,
                                                  ALU.mult, ALU.add).then_inc(S("ms_ready"), 1)
                                q4 = ma[:, :].rearrange("p (k h d) -> p k h d", k=2, d=HD)
                                r0 = rot[:, 0, :].rearrange("p (k h d) -> p k h d", k=2, d=HD)
                                r1 = rot[:, 1, :].rearrange("p (k h d) -> p k h d", k=2, d=HD)
                                dve.tensor_tensor(r0, q4, ctab[:, t].unsqueeze(2).broadcast_to([P, 2, NH, HD]),
                                                  ALU.mult).then_inc(S("rot_done"), 1)
                                dve.tensor_tensor(r1[:, :, :, 0:hh], q4[:, :, :, hh:HD],
                                                  stab[:, t, :, 0:hh].unsqueeze(2).broadcast_to([P, 2, NH, hh]),
                                                  ALU.mult).then_inc(S("rot_done"), 1)
                                dve.tensor_tensor(r1[:, :, :, hh:HD], q4[:, :, :, 0:hh],
                                                  stab[:, t, :, hh:HD].unsqueeze(2).broadcast_to([P, 2, NH, hh]),
                                                  ALU.mult).then_inc(S("ma_free"), 1)
                                dve.wait_ge(S("ma_free"), (b + 1) * 12 + MA["qk", t] + 2)
                                dve.wait_ge(S("rot_done"), k * 2)
                                then(dve.tensor_tensor(rsum[:, t % 2, :], rot[:, 0, :], rot[:, 1, :], ALU.add), "rsum_done", k)
                        for t in at(P_NAT, p):
                            if back:
                                k = tiles(b - 1, t)
                                dve.wait_ge(S("nat_done"), k)
                                o3 = mb[:, :].rearrange("p (h d) -> p h d", d=32)
                                then(dve.reciprocal(rcp[:, t, :], o3[:, :, HD]), "rcp_done", k)
                                dve.tensor_tensor(an[:].rearrange("p (h d) -> p h d", d=HD), o3[:, :, 0:HD],
                                                  rcp[:, t, :].unsqueeze(2).broadcast_to([P, NH, HD]),
                                                  ALU.mult).then_inc(S("mb_free"), 1)
                                dve.wait_ge(S("mb_free"), (b - 1) * 12 + MB["nat", t] + 2)
                                then(dve.tensor_copy(anh[:, t, 0, :], an[:]), "an_hi", k)
                                then(dve.tensor_tensor(anh[:, t, 1, :], an[:], anh[:, t, 0, :],
                                                       ALU.subtract), "an_ready", k)
                        for t in at(P_PROJ, p):
                            if back:
                                k = tiles(b - 1, t)
                                dve.wait_ge(S("proj_done"), k)
                                dve.wait_ge(S("xin_loaded"), b * 16)
                                dve.scalar_tensor_tensor(y0[:, t, :], mb[:, 0:D], 1.0 / WS, xin[:, t, :],
                                                         ALU.mult, ALU.add).then_inc(S("mb_free"), 1)
                                dve.wait_ge(S("mb_free"), (b - 1) * 12 + MB["proj", t] + 2)
                                then_apart(dve.bn_stats(st6[:, t, :], y0[:, t, :]), "y0_done", k)
                                then(dve.bn_aggr(mv[:, t, :], st6[:, t, :]), "mv_done", k)
                                dve.tensor_scalar(vv[:, t, 0:1], mv[:, t, 1:2], LN_EPS, None,
                                                  ALU.add).then_inc(S("var_ready"), 1)
                        for t in at(P_LG, p):
                            if back:
                                k = tiles(b - 1, t)
                                dve.wait_ge(S("lg_done"), k)
                                dve.tensor_scalar(lg[:, t, :], mc[:, 0:NE], 1.0 / RS, None, ALU.mult).then_inc(S("mc_free"), 1)
                                wait_apart(dve, S, "mc_free", (b - 1) * 16 + MC["lg", t] + 2)
                                then_apart(dve.max(mx[:, t, :], lg[:, t, :]), "top_ready", k)
                                then(dve.max_index(ix[:, t, :], mx[:, t, :], lg[:, t, :]), "ix_done", k)
                                then(dve.tensor_copy(ixf[:, t, :], ix[:, t, 0:2]), "ixf_done", k)
                                then(dve.tensor_tensor(oh[:, t, :, :], iota_e[:, 0, :].unsqueeze(1).broadcast_to([P, 2, NE]),
                                                       ixf[:, t, :].unsqueeze(2).broadcast_to([P, 2, NE]),
                                                       ALU.is_equal), "oh_done", k)
                                dve.tensor_tensor(mh[:, t, :], oh[:, t, 0, :], oh[:, t, 1, :], ALU.add).then_inc(S("mh_ready"), 1)
                        for t in at(P_RANK, p):
                            if back:
                                k = tiles(b - 1, t)
                                dve.wait_ge(S("rank_done"), k)
                                dve.tensor_tensor(sl[:, t, :], mc[:, 0:NE], iota_e[:, 1, :], ALU.add).then_inc(S("sl_done"), 1)
                                dve.tensor_copy(combT[:, t, :], mc[0:NE + 1, P:2 * P]).then_inc(S("mc_free"), 1)
                                dve.tensor_tensor(msum[:], msum[:], mh[:, t, :], ALU.add).then_inc(S("msum_free"), 1)
                                dve.wait_ge(S("sl_done"), k)
                                then(dve.tensor_tensor(slm[:, t, :, :], oh[:, t, :, :],
                                                       sl[:, t, :].unsqueeze(1).broadcast_to([P, 2, NE]),
                                                       ALU.mult), "slm_done", k)
                                then(dve.tensor_reduce(slf[:, t, :], slm[:, t, :, :], AX.X, ALU.add), "slf_done", k)
                                dve.tensor_copy(keep["slots"][:, bass.ds(((b - 1) * NT + t) * 2, 2)], slf[:, t, :]
                                                ).then_inc(S("kept"), 1)
                                dve.wait_ge(S("ids_out"), b + 1)
                                dve.tensor_copy(tok_i[:, t:t + 1], tokid[:, bass.ds((b - 1) * NT + t, 1)]
                                                ).then_inc(S("tok_ready"), 1)
                                dve.wait_ge(S("tok_ready"), k)
                                dve.tensor_copy(sl_i[:, t, :], slf[:, t, :]).then_inc(S("slots_ready"), 1)
                        for t in at(P_BIAS, p):
                            if back:
                                k = tiles(b - 1, t)
                                dve.wait_ge(S("bias_done"), k)
                                dve.tensor_tensor(res[:, t, :], mc[:, 0:D], x1[:, t, :], ALU.add).then_inc(S("mc_free"), 1)
                                dve.wait_ge(S("mc_free"), (b - 1) * 16 + MC["bias", t] + 2)
                                dve.sem_inc(S("res_ready"), 1)

                turns(dve, turn)

            @block.tensor
            def _(pe):
                pe.wait_ge(S("tables_ready"), 1)
                pe.wait_ge(S("const_ready"), 1)

                def scores(b, par, g, u):
                    i = b * 24 + g * 6 + u
                    if not isinstance(b, int) or i >= 2:
                        pe.wait_ge(S("exp_done"), i - 1)
                    slot = slots[u % 2]
                    if u in (2, 5):
                        jobs = [(4 * g + (0 if u == 2 else 2) + r, 2, 256 * r, r == 0) for r in range(2)]
                    else:
                        h = 4 * g + (0, 1, None, 2, 3)[u]
                        jobs = [(h, 0, 0, True), (h, 1, 512, True), (h, 3, 896, False)]
                    for h, j, col, first in jobs:
                        rows = slice(64 * (h // 8), 64 * (h // 8) + 64)
                        pe.matmul(slot[:, col:col + T - P * j],
                                  stk[rows, par, 1, h % 8, P * j:P * j + P],
                                  stk[rows, par, 0, h % 8, P * j:T], start=first, stop=False, skip_group_check=True)
                    for h, j, col, first in jobs:
                        last = pe.matmul(slot[:, col:col + P], ident_b[:], mask_b[:], start=False, stop=True,
                                         skip_group_check=True)
                    last.then_inc(S("unit_ready"), 1)

                def turn(b, par, front, attend, back):
                    for p in range(POSITIONS):
                        g = p // 4
                        if attend and p < 16:
                            if p == 0:
                                pe.wait_ge(S("stk_in"), (b + 1) * (32 * 16))
                            for u in ((0, 1), (2,), (3,), (4, 5))[p % 4]:
                                scores(b, par, g, u)
                        if p % 4 == 0 and ((p == 0 and back) or (0 < p < 16 and attend)):
                            s = b * 4 + g
                            pe.wait_ge(S("exp_done"), s * 6)
                            pe.wait_ge(S("ma_free"), (b + (0 if p == 0 else 1)) * 12 + 1)
                            if not isinstance(b, int) or s >= 2:
                                pe.wait_ge(S("raw_done"), s - 1)
                            vp = (1 - par) if p == 0 else par
                            gg = (g - 1) % 4
                            for j in range(NT):
                                for r in range(4):
                                    last = pe.matmul(pv_bank[32 * r:32 * r + 32, P * j:T],
                                                     vst[:, vp, j, 4 * gg + r, :],
                                                     prob[:, (g - 1) % 2, r, SEG[j]:SEG[j] + T - P * j],
                                                     start=(j == 0), stop=(j == NT - 1), skip_group_check=True)
                            last.then_inc(S("pv_done"), 1)
                        if front:
                            for t in at(P_QK, p):
                                pe.wait_ge(S("xT_split"), b + 2)
                                pe.wait_ge(S("ma_free"), (b + 1) * 12 + MA["qk", t] + 1)
                                product(ma[:, 0:2 * D], xTh, t, wqkv, slice(0, 2 * D)).then_inc(S("qk_done"), 1)
                            for t in at(P_V, p):
                                pe.wait_ge(S("ma_free"), (b + 1) * 12 + MA["v", t] + 1)
                                product(ma[:, 0:D], xTh, t, wqkv, slice(2 * D, 3 * D)).then_inc(S("v_done"), 1)
                            for t in at(P_T, p):
                                pe.wait_ge(S("nat_ready"), tiles(b + 1, t))
                                pe.wait_ge(S("ma_free"), (b + 1) * 12 + MA["t", t] + 1)
                                for k in range(8):
                                    last = pe.transpose(ma[:, 64 * k:64 * k + 64].bitcast(F16),
                                                        nat[:, t, k // 4, P * (k % 4):P * (k % 4) + P], ident_h[:])
                                last.then_inc(S("t_done"), 1)
                        if back:
                            for t in at(P_NAT, p):
                                pe.wait_ge(S("raw_done"), b * 4)
                                pe.wait_ge(S("mb_free"), (b - 1) * 12 + MB["nat", t] + 1)
                                for q in range(4):
                                    last = pe.transpose(mb[:, P * q:P * q + P], raw[:, 1 - par, q, P * t:P * t + P],
                                                        ident_f[:])
                                last.then_inc(S("nat_done"), 1)
                            for t in at(P_AT, p):
                                pe.wait_ge(S("an_ready"), tiles(b - 1, t))
                                pe.wait_ge(S("mb_free"), (b - 1) * 12 + MB["at", t] + 1)
                                for k in range(4):
                                    last = pe.transpose(mb[:, 64 * k:64 * k + 64].bitcast(F16),
                                                        anh[:, t, k // 2, P * (k % 2):P * (k % 2) + P], ident_h[:])
                                last.then_inc(S("at_done"), 1)
                            for t in at(P_PROJ, p):
                                pe.wait_ge(S("mb_free"), (b - 1) * 12 + max(MB["proj", t], MB["at", t] + 1) + 1)
                                pieces = [(x, w, c) for c in range(DC) for x, w in ((0, 0), (0, 1), (1, 0))]
                                for n, (x, w, c) in enumerate(pieces):
                                    last = pe.matmul(mb[:, 0:D], aT[:, t, x * DC + c, :], wproj[:, w, c, :],
                                                     start=(n == 0), stop=(n == len(pieces) - 1))
                                last.then_inc(S("proj_done"), 1)
                            for t in at(P_XN, p):
                                pe.wait_ge(S("xn_lo"), tiles(b - 1, t))
                                pe.wait_ge(S("mc_free"), (b - 1) * 16 + MC["xn", t] + 1)
                                for k in range(4):
                                    last = pe.transpose(mc[:, 64 * k:64 * k + 64].bitcast(F16),
                                                        xnh[:, t, k // 2, P * (k % 2):P * (k % 2) + P], ident_h[:])
                                last.then_inc(S("xnT_done"), 1)
                            for t in at(P_LG, p):
                                pe.wait_ge(S("mc_free"), (b - 1) * 16 + MC["lg", t] + 1)
                                pieces = [(x, w, c) for c in range(DC) for x in range(2) for w in range(2)]
                                for n, (x, w, c) in enumerate(pieces):
                                    last = pe.matmul(mc[:, 0:NE], xnT[:, t, x * DC + c, :], wrout[:, w, c, :],
                                                     start=(n == 0), stop=(n == len(pieces) - 1))
                                last.then_inc(S("lg_done"), 1)
                            for t in at(P_RANK, p):
                                pe.wait_ge(S("comb_ready"), tiles(b - 1, t))
                                pe.wait_ge(S("mh_ready"), tiles(b - 1, t))
                                pe.wait_ge(S("msum_free"), tiles(b - 1, t))
                                pe.wait_ge(S("mc_free"), (b - 1) * 16 + MC["rank", t] + 1)
                                pe.transpose(mc[0:NE + 1, P:2 * P], comb[:, t, :], ident_f[:])
                                pe.matmul(mc[:, 0:NE], tri_h[:], mh[:, t, :], start=True, stop=False)
                                pe.matmul(mc[:, 0:NE], ones_h[:], msum[:], start=False, stop=True
                                          ).then_inc(S("rank_done"), 1)
                            for t in at(P_BIAS, p):
                                pe.wait_ge(S("mc_free"), (b - 1) * 16 + max(MC["bias", t], MC["rank", t] + 1) + 1)
                                pe.matmul(mc[:, 0:D], combT[:, t, :], bias2[:], start=True, stop=True
                                          ).then_inc(S("bias_done"), 1)

                def product(out, xh, t, w, cols):
                    pieces = [(x, y, c) for c in range(DC) for x, y in ((0, 0), (0, 1), (1, 0))]
                    for n, (x, y, c) in enumerate(pieces):
                        last = pe.matmul(out, xh[:, x, c, P * t:P * t + P], w[:, y, c, cols],
                                         start=(n == 0), stop=(n == len(pieces) - 1))
                    return last

                turns(pe, turn)


N_TILES = N_SHARED + N_ROUTED
UNIT_COLS = DC * H
N_UNITS = 2 * (NE + 1)
UNITS_FIRST = 4


def expert_block(nc, a, S, keep):
    with ExitStack() as ctx:
        def sb(name, shape, dt):
            return ctx.enter_context(nc.sbuf_tensor(name, shape, dt))

        def ps(name, cols):
            return ctx.enter_context(nc.psum_tensor(name, [P, cols], F32))

        w_hi = sb("w_hi", [P, N_UNITS * UNIT_COLS], F16)
        w_lo = sb("w_lo", [P, N_UNITS * UNIT_COLS], F16)
        w_raw = sb("w_raw", [P, 2, UNIT_COLS], F32)
        b1 = sb("b1", [P, (NE + 1) * HC], F32)
        ident = sb("ident2", [P, P], F16)
        idx = sb("idx", [P, 2, 2], I32)
        xg = sb("xg", [P, 2, 2, 2 * D], F16)
        xgT = sb("xgT", [P, 2, 4, TT], F16)
        hf = sb("hf", [P, HC, TT], F32)
        hh = sb("hh", [P, 2, 2, HC, TT], F16)
        yb = sb("yb", [P, 2, 2, D], F32)
        ge = sb("ge", [P, NE, N_SHARED], F32)
        io_i = sb("io_i", [P, N_TILES + N_SHARED], I32)
        io_f = sb("io_f", [P, N_TILES + N_SHARED], F32)
        cum = sb("cum", [P, 3, NE], F32)
        past = sb("past", [1, 2, N_ROUTED, NE], F32)
        te = sb("te", [1, 4, N_ROUTED], F32)
        shift = sb("shift", [P, NE], F32)
        yrow = sb("yrow", [P, 2, 2 * NTILE], F32)
        tab = sb("tab", [1, 2, N_TILES], I32)
        ones = sb("ones2", [P, P], F16)
        tr = [ps(f"tr{i}", 512) for i in range(2)]
        hb = [ps(f"hb{i}", 512) for i in range(4)]
        ybank = [ps(f"yb{i}", 512) for i in range(2)]

        with nc.Block() as block:
            @block.gpsimd
            def _(pool):
                pool.iota(io_i[:, 0:N_TILES], pattern=[[1, N_TILES]], base=0, channel_multiplier=0).then_inc(S("io_made"), 1)
                pool.iota(io_i[:, N_TILES:], pattern=[[TT, N_SHARED]], base=0, channel_multiplier=0).then_inc(S("io_made"), 1)

                def gather(h, par):
                    wait_apart(pool, S, f"idx_loaded{par}", (h + 1) * 16)
                    if not isinstance(h, int) or h >= 1:
                        wait_apart(pool, S, "tr_done", h * 2 + par - 1)
                    for j in range(2):
                        pool.indirect_dma_start(xg[:, par, j, :], None, a["xn_rows"],
                                                bass.IndirectOffsetOnAxis(ap=idx[:, par, j:j + 1], axis=0)
                                                ).then_inc(S(f"gathered{par}"), 16)

                gather(0, 0)
                gather(0, 1)
                with pool.Fori(1, N_TILES // 2) as h:
                    gather(h, 0)
                    gather(h, 1)
                gather(N_TILES // 2, 0)

            @block.sync
            def _(sp):
                def load_ids(h, par):
                    i = h * 2 + par
                    row = sp.value_load(tab[0:1, 1, bass.ds(i, 1)], min_val=0, max_val=N_ROWS - TT)
                    if not isinstance(h, int) or h >= 1:
                        wait_apart(sp, S, f"gathered{par}", h * 32)
                    sp.dma_start(idx[:, par, :], a["table"][bass.ds(row, TT), :].rearrange("(p j) o -> p (j o)", j=2)
                                 ).then_inc(S(f"idx_loaded{par}"), 16)

                def store(h, par):
                    i = h * 2 + par
                    wait_apart(sp, S, "y_ready", i + 1)
                    sp.dma_start(a["y_rows"][bass.ds(i * TT, TT), :].rearrange("(p j) d -> p j d", j=2), yb[:, par, :, :]
                                 ).then_inc(S(f"y_stored{par}"), 16)

                sp.wait_ge(S("tab_ready"), 1)
                load_ids(0, 0)
                load_ids(0, 1)
                load_ids(1, 0)
                load_ids(1, 1)
                with sp.Fori(0, (N_TILES - 5) // 2) as h:
                    store(h, 0)
                    load_ids(h + 2, 0)
                    store(h, 1)
                    load_ids(h + 2, 1)
                k = (N_TILES - 5) // 2
                store(k, 0)
                load_ids(k + 2, 0)
                store(k, 1)
                store(k + 1, 0)
                store(k + 1, 1)
                store(k + 2, 0)
                sp.wait_ge(S("y_stored0"), 16 * ((N_TILES + 1) // 2))
                sp.wait_ge(S("y_stored1"), 16 * (N_TILES // 2))

            def weight_unit(k):
                return (k + 2 * NE) % N_UNITS

            def tiles_of(eng, step, split):
                def two(h, units):
                    for par in range(2):
                        step(h, par, True, True)
                        if units:
                            split(par, h + UNITS_FIRST // 2)

                two(0, True)
                with eng.Fori(1, (N_UNITS - UNITS_FIRST) // 2) as h:
                    two(h, True)
                with eng.Fori((N_UNITS - UNITS_FIRST) // 2, (N_TILES - 3) // 2) as h:
                    two(h, False)
                k = (N_TILES - 3) // 2
                step(k, 0, True, True)
                step(k, 1, False, True)
                step(k + 1, 0, False, False)

            @block.scalar
            def _(act):
                def split(par, h):
                    u = ((h + NE) % (NE + 1)) * 2 + par if isinstance(h, int) else (h - 1) * 2 + par
                    act.wait_ge(S(f"w_in{par}"), (h + 1) * 16)
                    act.activation(w_hi[:, bass.ds(u * UNIT_COLS, UNIT_COLS)], w_raw[:, par, :], ACT.Copy,
                                   scale=WS).then_inc(S("w_hi_done"), 1)

                def split_and_load(par, h):
                    split(par, h)
                    act.wait_ge(S("w_lo_done"), h * 2 + par + 1)
                    u = (h + 1 + NE) % (NE + 1) * 2 + par if isinstance(h, int) else (h % NE) * 2 + par
                    act.dma_start(w_raw[:, par, :], a["w_all"][bass.ds(u * P, P), :]).then_inc(S(f"w_in{par}"), 16)

                act.dma_start(b1[:], a["b1"]).then_inc(S("b1_in"), 16)
                for par in range(2):
                    act.dma_start(w_raw[:, par, :], a["w_all"][weight_unit(par) * P:(weight_unit(par) + 1) * P, :]
                                  ).then_inc(S(f"w_in{par}"), 16)
                for h in range(UNITS_FIRST // 2):
                    for par in range(2):
                        split_and_load(par, h)
                act.wait_ge(S("b1_in"), 16)
                act.wait_ge(S("tab_ready"), 1)

                def hidden(h, par):
                    i = h * 2 + par
                    e = act.value_load(tab[0:1, 0, bass.ds(i, 1)], min_val=0, max_val=NE)
                    if not isinstance(h, int) or i >= 1:
                        act.wait_ge(S("h_lo"), i * 2)
                    for c in range(HC):
                        if c % 2 == 0:
                            act.wait_ge(S("h_done"), i * (HC // 2) + c // 2 + 1)
                        act.activation(hf[:, c, :], hb[c // 2][:, (c % 2) * TT:(c % 2) * TT + TT], ACT.Relu,
                                       bias=b1[:, bass.ds(e * HC + c, 1)], scale=1.0 / WS).then_inc(S("relu_done"), 1)

                def step(h, par, has2, has1):
                    if has1:
                        hidden(h + par, 1 - par)

                hidden(0, 0)
                tiles_of(act, step, split_and_load)
                act.wait_ge(S("w_in0"), 16 * (NE + 2))
                act.wait_ge(S("w_in1"), 16 * (NE + 2))

            @block.vector
            def _(dve):
                def then(ins, name, count):
                    ins.then_inc(S(name), 1)
                    dve.wait_ge(S(name), count)

                dve.memset(ones[:], 1.0).then_inc(S("ones_made"), 1)
                dve.tensor_copy(ident[:], keep["ident"][:]).then_inc(S("ones_made"), 1)
                dve.wait_ge(S("io_made"), 2)
                then(dve.tensor_copy(io_f[:], io_i[:]), "io_f_made", 1)
                dve.wait_ge(S("counted"), 1)
                then(dve.tensor_copy(cum[:, 0, :], tr[0][:, 0:NE]), "tb", 1)
                then(dve.tensor_tensor(ge[:], cum[:, 0, :].unsqueeze(2).broadcast_to([P, NE, N_SHARED]),
                                       io_f[:, N_TILES:].unsqueeze(1).broadcast_to([P, NE, N_SHARED]), ALU.is_gt), "tb", 2)
                then(dve.tensor_reduce(cum[:, 1, :], ge[:], AX.X, ALU.add), "tb", 3)
                then(dve.tensor_copy(cum[:, 2, 0:1], cum[:, 1, 0:1]), "tb", 4)
                for e in range(1, NE):
                    then(dve.tensor_tensor(cum[:, 2, e:e + 1], cum[:, 2, e - 1:e], cum[:, 1, e:e + 1], ALU.add), "tb", 4 + e)
                k39 = io_f[0:1, 0:N_ROUTED]
                then(dve.tensor_tensor(past[:, 0], k39.unsqueeze(2).broadcast_to([1, N_ROUTED, NE]),
                                       cum[0:1, 2, :].unsqueeze(1).broadcast_to([1, N_ROUTED, NE]), ALU.is_ge), "tb", 12)
                dve.tensor_reduce(te[:, 0, :], past[:, 0], AX.X, ALU.add).then_inc(S("tb"), 1)
                then(dve.tensor_tensor(past[:, 1], past[:, 0],
                                       cum[0:1, 1, :].unsqueeze(1).broadcast_to([1, N_ROUTED, NE]), ALU.mult), "tb", 14)
                then(dve.tensor_reduce(te[:, 1, :], past[:, 1], AX.X, ALU.add), "tb", 15)
                then(dve.scalar_tensor_tensor(te[:, 2, :], te[:, 0, :], float(NE), te[:, 0, :], ALU.is_equal, ALU.add), "tb", 16)
                then(dve.tensor_tensor(te[:, 3, :], k39, te[:, 1, :], ALU.subtract), "tb", 17)
                then(dve.tensor_scalar(te[:, 3, :], te[:, 3, :], float(TT), None, ALU.mult), "tb", 18)
                then(dve.scalar_tensor_tensor(te[:, 2, :], te[:, 2, :], float(REGION), te[:, 3, :], ALU.mult, ALU.add), "tb", 19)
                dve.tensor_copy(tab[:, 0, N_SHARED:], te[:, 0, :]).then_inc(S("tb"), 1)
                dve.tensor_copy(tab[:, 1, N_SHARED:], te[:, 2, :]).then_inc(S("tb"), 1)
                dve.tensor_scalar(tab[:, 0, 0:N_SHARED], io_f[0:1, 0:N_SHARED], 0.0, float(SHARED),
                                  ALU.mult, ALU.add).then_inc(S("tb"), 1)
                dve.tensor_scalar(tab[:, 1, 0:N_SHARED], io_f[0:1, N_TILES:], float(SHARED * REGION), None,
                                  ALU.add).then_inc(S("tb"), 1)
                dve.wait_ge(S("tb"), 23)
                dve.sem_inc(S("tab_ready"), 1)
                then(dve.tensor_scalar(shift[:], cum[:, 1, :], float(TT), float(-REGION), ALU.mult, ALU.add), "yr", 1)
                then(dve.tensor_scalar(yrow[:, 0, :], keep["slots"][:], float(N_SHARED * TT), None, ALU.add), "yr", 2)
                for e in range(1, NE):
                    then(dve.tensor_scalar(yrow[:, 1, :], keep["slots"][:], float(e * REGION), shift[:, e - 1:e],
                                           ALU.is_ge, ALU.mult), "yr", 1 + 2 * e)
                    then(dve.tensor_tensor(yrow[:, 0, :], yrow[:, 0, :], yrow[:, 1, :], ALU.add), "yr", 2 + 2 * e)
                dve.tensor_copy(keep["rows"][:], yrow[:, 0, :]).then_inc(S("yr"), 1)

                def split(par, h):
                    u = ((h + NE) % (NE + 1)) * 2 + par if isinstance(h, int) else (h - 1) * 2 + par
                    dve.wait_ge(S("w_hi_done"), h * 2 + par + 1)
                    cols = bass.ds(u * UNIT_COLS, UNIT_COLS)
                    dve.scalar_tensor_tensor(w_lo[:, cols], w_raw[:, par, :], WS, w_hi[:, cols],
                                             ALU.mult, ALU.subtract).then_inc(S("w_lo_done"), 1)

                for h in range(UNITS_FIRST // 2):
                    for par in range(2):
                        split(par, h)

                def turned(h, par):
                    dve.wait_ge(S("tr_done"), h * 2 + par + 1)
                    dve.tensor_copy(xgT[:, par].rearrange("p k t -> p (k t)"),
                                    tr[par][:, :].bitcast(F16)).then_inc(S("xgT_ready"), 1)

                def split_hidden(h, par):
                    i = h * 2 + par
                    for half in range(2):
                        cs = slice(half * HC // 2, (half + 1) * HC // 2)
                        dve.wait_ge(S("relu_done"), i * HC + (half + 1) * HC // 2)
                        then(dve.tensor_copy(hh[:, par, 0, cs, :], hf[:, cs, :]), "h_hi", i * 2 + half + 1)
                        dve.tensor_tensor(hh[:, par, 1, cs, :], hf[:, cs, :], hh[:, par, 0, cs, :],
                                          ALU.subtract).then_inc(S("h_lo"), 1)

                def output(h, par):
                    i = h * 2 + par
                    dve.wait_ge(S("y_done"), i + 1)
                    if not isinstance(h, int) or h >= 1:
                        dve.wait_ge(S(f"y_stored{par}"), h * 16)
                    dve.tensor_scalar(yb[:, par].rearrange("p j d -> p (j d)"), ybank[par][:, :], 1.0 / WS, None,
                                      ALU.mult).then_inc(S("y_ready"), 1)

                def step(h, par, has2, has1):
                    if has2:
                        turned(h + 1, par)
                    if has1:
                        split_hidden(h + par, 1 - par)
                    output(h, par)

                turned(0, 0)
                turned(0, 1)
                split_hidden(0, 0)
                tiles_of(dve, step, split)

            @block.tensor
            def _(pe):
                pe.wait_ge(S("ones_made"), 2)
                pe.matmul(tr[0][:, 0:NE], ones[:], keep["msum"][:], start=True, stop=True).then_inc(S("counted"), 1)
                pe.wait_ge(S("tab_ready"), 1)

                def turn_rows(h, par):
                    pe.wait_ge(S(f"gathered{par}"), (h + 1) * 32)
                    if not isinstance(h, int) or h >= 1:
                        pe.wait_ge(S("xgT_ready"), h * 2 + par - 1)
                    for k in range(4):
                        for j in range(2):
                            c = (2 * k + j) * 64
                            last = pe.transpose(tr[par][:, c:c + 64].bitcast(F16), xg[:, par, j, P * k:P * k + P], ident[:])
                    last.then_inc(S("tr_done"), 1)

                PIECES = ((0, 0), (0, 1), (1, 0))
                ws = (w_hi, w_lo)

                def hidden(h, par, ready):
                    i = h * 2 + par
                    e = pe.value_load(tab[0:1, 0, bass.ds(i, 1)], min_val=0, max_val=NE)
                    pe.wait_ge(S("w_lo_done"), ready)
                    pe.wait_ge(S("xgT_ready"), i + 1)
                    for hc in range(HC):
                        if hc % 2 == 0 and (not isinstance(h, int) or i >= 1):
                            pe.wait_ge(S("relu_done"), (i - 1) * HC + hc + 2)
                        n = 0
                        for c in range(DC):
                            for x, w in PIECES:
                                last = pe.matmul(hb[hc // 2][:, (hc % 2) * TT:(hc % 2) * TT + TT],
                                                 ws[w][:, bass.ds(e * (2 * UNIT_COLS) + (c * H + hc * P), P)],
                                                 xgT[:, par, x * DC + c, :], start=(n == 0), stop=(n == 5))
                                n += 1
                        if hc % 2:
                            last.then_inc(S("h_done"), 1)

                def output(h, par):
                    i = h * 2 + par
                    e = pe.value_load(tab[0:1, 0, bass.ds(i, 1)], min_val=0, max_val=NE)
                    pe.wait_ge(S("h_lo"), (i + 1) * 2)
                    if not isinstance(h, int) or h >= 1:
                        pe.wait_ge(S("y_ready"), i - 1)
                    for j in range(2):
                        n = 0
                        for hc in range(HC):
                            for x, w in PIECES:
                                last = pe.matmul(ybank[par][:, j * D:(j + 1) * D],
                                                 hh[:, par, x, hc, P * j:P * j + P],
                                                 ws[w][:, bass.ds(e * (2 * UNIT_COLS) + (UNIT_COLS + hc * D), D)],
                                                 start=(n == 0), stop=(n == 3 * HC - 1))
                                n += 1
                    last.then_inc(S("y_done"), 1)

                turn_rows(0, 0)
                turn_rows(0, 1)
                hidden(0, 0, UNITS_FIRST)

                def two(h, shared):
                    for par in range(2):
                        turn_rows(h + 1, par)
                        hidden(h + par, 1 - par, UNITS_FIRST if shared else N_UNITS)
                        output(h, par)

                half = (N_UNITS - UNITS_FIRST) // 2
                two(0, True)
                with pe.Fori(1, half) as h:
                    two(h, True)
                with pe.Fori(half, (N_TILES - 3) // 2) as h:
                    two(h, False)
                k = (N_TILES - 3) // 2
                turn_rows(k + 1, 0)
                hidden(k, 1, N_UNITS)
                output(k, 0)
                hidden(k + 1, 0, N_UNITS)
                output(k, 1)
                output(k + 1, 0)


def combine_block(nc, a, S, keep):
    with ExitStack() as ctx:
        def sb(name, shape, dt):
            return ctx.enter_context(nc.sbuf_tensor(name, shape, dt))

        R = 4
        sidx = sb("sidx", [P, R, 2], I32)
        y1 = sb("y1", [P, R, D], F32)
        y2 = sb("y2", [P, R, D], F32)
        ys = sb("ys", [P, R, D], F32)
        rs = sb("rs", [P, R, D], F32)
        acc = sb("acc", [P, R, D], F32)
        st = sb("st", [P, R, 6], F32)
        mean_var = sb("mean_var", [P, R, 2], F32)
        var_eps = sb("var_eps", [P, R], F32)
        rstd = sb("rstd_f", [P, R], F32)
        half = sb("half_f", [P, 1], F32)
        ob = sb("ob", [P, R, D], F32)

        def rounds(eng, job):
            for r in range(R):
                job(0, r)
            with eng.Fori(1, NTILE // R) as h:
                for r in range(R):
                    job(h, r)

        with nc.Block() as block:
            @block.sync
            def _(sp):
                def load(h, r):
                    if not isinstance(h, int) or h >= 1:
                        wait_apart(sp, S, "acc_done", (h - 1) * R + r + 1)
                    rows = (h * R + r) * P
                    sp.dma_start(rs[:, r, :], a["resid"][bass.ds(rows, P), :]).then_inc(S(f"f_in{r}"), 16)
                    sp.dma_start(ys[:, r, :], a["y_rows"][bass.ds(rows, P), :]).then_inc(S(f"f_in{r}"), 16)

                rounds(sp, load)

            @block.scalar
            def _(act):
                def store(h, r):
                    act.wait_ge(S("out_ready"), h * R + r + 1)
                    act.dma_start(a["out"][bass.ds((h * R + r) * P, P), :], ob[:, r, :]).then_inc(S(f"out_stored{r}"), 16)

                rounds(act, store)
                for r in range(R):
                    act.wait_ge(S(f"out_stored{r}"), 16 * (NTILE // R))

            @block.gpsimd
            def _(pool):
                def job(h, r):
                    i = h * R + r
                    wait_apart(pool, S, "sidx_ready", i + 2)
                    for y, k in ((y1, 0), (y2, 1)):
                        pool.indirect_dma_start(y[:, r, :], None, a["y_rows"],
                                                bass.IndirectOffsetOnAxis(ap=sidx[:, r, k:k + 1], axis=0)
                                                ).then_inc(S(f"f_gathered{r}"), 16)

                def rsqrt(h, r):
                    i = h * R + r
                    pool.wait_ge(S("f_var"), i + 1)
                    pool.tensor_tensor(rstd[:, r:r + 1], var_eps[:, r:r + 1], half[:], ALU.pow).then_inc(S("f_rstd"), 1)

                for r in range(R):
                    job(0, r)
                with pool.Fori(1, NTILE // R) as h:
                    for r in range(R):
                        rsqrt(h - 1, r)
                        job(h, r)
                for r in range(R):
                    rsqrt(NTILE // R - 1, r)

            @block.vector
            def _(dve):
                def then(ins, name, count):
                    ins.then_inc(S(name), 1)
                    dve.wait_ge(S(name), count)

                def then_apart(ins, name, count):
                    ins.then_inc(S(name), 1)
                    wait_apart(dve, S, name, count)

                dve.memset(half[:], -0.5).then_inc(S("sidx_ready"), 1)

                def pick(h, r):
                    dve.tensor_copy(sidx[:, r, :], keep["rows"][:, bass.ds((h * R + r) * 2, 2)]).then_inc(S("sidx_ready"), 1)

                def rsqrt(h, r):
                    i = h * R + r
                    dve.wait_ge(S("f_rstd"), i + 1)
                    if not isinstance(h, int) or h >= 1:
                        dve.wait_ge(S(f"out_stored{r}"), h * 16)
                    dve.tensor_scalar(ob[:, r, :], acc[:, r, :], mean_var[:, r, 0:1], rstd[:, r:r + 1],
                                      ALU.subtract, ALU.mult).then_inc(S("out_ready"), 1)

                def sums(h, r, more):
                    i = h * R + r
                    dve.wait_ge(S(f"f_in{r}"), (h + 1) * 32)
                    dve.wait_ge(S(f"f_gathered{r}"), (h + 1) * 32)
                    w = keep["weights"]
                    then(dve.scalar_tensor_tensor(acc[:, r, :], y1[:, r, :], w[:, bass.ds(i * 2, 1)], ys[:, r, :],
                                                  ALU.mult, ALU.add), "f_a", i + 1)
                    then(dve.scalar_tensor_tensor(acc[:, r, :], y2[:, r, :], w[:, bass.ds(i * 2 + 1, 1)], acc[:, r, :],
                                                  ALU.mult, ALU.add), "f_b", i + 1)
                    then(dve.tensor_tensor(acc[:, r, :], acc[:, r, :], rs[:, r, :], ALU.add), "acc_done", i + 1)
                    if more:
                        pick(h + 1, r)
                    then_apart(dve.bn_stats(st[:, r, :], acc[:, r, :]), "f_st", i + 1)
                    then(dve.bn_aggr(mean_var[:, r, :], st[:, r, :]), "f_mv", i + 1)
                    dve.tensor_scalar(var_eps[:, r:r + 1], mean_var[:, r, 1:2], LN_EPS, None, ALU.add).then_inc(S("f_var"), 1)

                for r in range(R):
                    pick(0, r)
                last_round = NTILE // R - 1
                sums(0, 0, True)
                for r in range(1, R):
                    sums(0, r, True)
                    rsqrt(0, r - 1)
                with dve.Fori(1, last_round) as h:
                    for r in range(R):
                        sums(h, r, True)
                        rsqrt(h - 1, R - 1) if r == 0 else rsqrt(h, r - 1)
                for r in range(R):
                    sums(last_round, r, False)
                    rsqrt(last_round - 1, R - 1) if r == 0 else rsqrt(last_round, r - 1)
                rsqrt(last_round, R - 1)


def layer(nc, a):
    with ExitStack() as ctx:
        named = {}

        def S(name):
            if name not in named:
                named[name] = ctx.enter_context(nc.semaphore(name))
            return named[name]

        keep = {
            "slots": ctx.enter_context(nc.sbuf_tensor("keep_slots", [P, 2 * NTILE], F32)),
            "rows": ctx.enter_context(nc.sbuf_tensor("keep_rows", [P, 2 * NTILE], I32)),
            "weights": ctx.enter_context(nc.sbuf_tensor("keep_weights", [P, 2 * NTILE], F32)),
            "msum": ctx.enter_context(nc.sbuf_tensor("keep_msum", [P, NE], F16)),
            "ident": ctx.enter_context(nc.sbuf_tensor("keep_ident", [P, P], F16)),
        }
        attention_block(nc, a, S, keep)
        expert_block(nc, a, S, keep)
        combine_block(nc, a, S, keep)


def kernel(**inputs):
    import concourse.bacc as _bacc
    from concourse import mybir as _mybir
    from concourse.bass_utils import run_bass_kernel_spmd as _run

    v = {k.replace("L0_", ""): np.asarray(x) for k, x in inputs.items()}
    cat = lambda routed, shared: np.concatenate([v[routed], v[shared][None]], axis=0)
    w1 = cat("ffn_ew1", "ffn_sw1").reshape(NE + 1, DC, P, H).transpose(0, 2, 1, 3).reshape(NE + 1, 1, P, UNIT_COLS)
    w2 = cat("ffn_ew2", "ffn_sw2").reshape(NE + 1, HC, P, D).transpose(0, 2, 1, 3).reshape(NE + 1, 1, P, UNIT_COLS)
    arrays = {
        "x": v["attn_x"].reshape(NTOK, D),
        "xT": v["attn_x"].transpose(0, 2, 1).reshape(NB * D, T),
        "wqkvT": v["attn_w_qkv"].T,
        "wprojT": v["attn_w_proj"].T,
        "qnw": v["attn_q_norm_w"],
        "knw": v["attn_k_norm_w"],
        "ffn_nw": v["ffn_norm_weight"],
        "routT": v["ffn_router_w"].T,
        "w_all": np.concatenate([w1, w2], axis=1).reshape(N_UNITS * P, UNIT_COLS),
        "b1": cat("ffn_eb1", "ffn_sb1").reshape(NE + 1, HC, P).transpose(2, 0, 1).reshape(P, (NE + 1) * HC),
        "b2all": cat("ffn_eb2", "ffn_sb2"),
        "trig": rope_tables(),
    }
    arrays = {k: np.ascontiguousarray(x) for k, x in arrays.items()}
    nc = _bacc.Bacc("TRN2", target_bir_lowering=False, num_devices=1)
    a = {k: nc.dram_tensor("in_" + k, x.shape, _mybir.dt.from_np(x.dtype), kind="ExternalInput").ap()
         for k, x in arrays.items()}
    for name, shape, dt in (("qk_dram", (8, P, T), F16), ("xn_rows", (NTOK, 2 * D), F16), ("resid", (NTOK, D), F32),
                            ("table", (N_ROWS, 1), I32), ("y_rows", (N_TILES * TT, D), F32)):
        a[name] = nc.dram_tensor(name, shape, dt, kind="Internal").ap()
    a["out"] = nc.dram_tensor("out", (NTOK, D), F32, kind="ExternalOutput").ap()
    layer(nc, a)
    r = _run(nc, [{"in_" + k: x for k, x in arrays.items()}], core_ids=[0])
    return r.results[0]["out"].reshape(NB, T, D)
```

```python
from contextlib import ExitStack

import numpy as np

import concourse.bass as bass
from concourse import mybir

ALU = mybir.AluOpType
ACT = mybir.ActivationFunctionType
AX = mybir.AxisListType
F32 = mybir.dt.float32
F16 = mybir.dt.float16
BF16 = mybir.dt.bfloat16
I32 = mybir.dt.int32
U32 = mybir.dt.uint32

P = 128
NB, T, D = 8, 512, 256
NH, HD = 16, 16
NT = T // P
DC = D // P
NTOK = NB * T
NTILE = NTOK // P
ROPE_THETA = 32.0
RMS_EPS = 1e-6
LN_EPS = 1e-5
FFN_EPS = 1e-8
ATT_SCALE = HD ** -0.5
WS = 16.0
RS = 64.0
SEG = (0, 512, 1024, 896)
PW = 1280

NE, H = 8, 1024
HC = H // P
SHARED = NE
REGION = NTOK
TT = 256
TOPK = 2
N_SHARED = NTOK // TT
N_ROUTED = (TOPK * NTOK) // TT + NE - 1
SPARE = NE * REGION
N_ROWS = SPARE + (NE - 1) * TT


def rope_tables():
    freqs = np.float32(ROPE_THETA) ** (-np.arange(0, HD, 2, dtype=np.float32) / np.float32(HD))
    ang = np.arange(T, dtype=np.float32)[:, None] * freqs[None, :].astype(np.float32)
    return np.stack([np.cos(ang), np.sin(ang)], axis=1).astype(np.float32)



def order(*jobs):
    by = sorted((p, k, name, t) for k, (name, pos) in enumerate(jobs) for t, p in enumerate(pos))
    return {(name, t): i for i, (_, _, name, t) in enumerate(by)}


P_QK = (1, 3, 5, 8)
P_V = (3, 8)
P_T = (5, 6, 10, 14)
P_QN = (4, 5, 8, 12)
P_NAT = (0, 1, 2, 5)
P_AT = (3, 6)
P_PROJ = (3, 7)
P_XN = (5, 10)
P_LG = (6, 11)
P_W = (8, 12)
P_RANK = (8, 13)
P_BIAS = (9, 16)
P_LOAD = (0, 2, 6, 8, 10, 13)
P_SPLIT = (1, 4, 6, 9, 11, 14)
P_STORE = (2, 4, 7, 10, 12, 15)
POSITIONS = 17
CHUNKS = 6
MA = order(("qk", P_QK), ("v", P_V), ("t", P_T))
MB = order(("nat", P_NAT), ("at", P_AT), ("proj", P_PROJ))
MC = order(("xn", P_XN), ("rank", P_RANK), ("bias", P_BIAS), ("lg", P_LG))
N_MA, N_MB, N_MC = len(MA), len(MB), len(MC)


def at(positions, p):
    return [t for t in range(len(positions)) if positions[t] == p]


def wait_apart(eng, S, name, count):
    eng.wait_ge(S(name), count)
    eng.sem_inc(S("passed"), 1)


def pairs(b, u):
    return b * (NT // 2) + u + 1


def pair(u):
    return slice(2 * u, 2 * u + 2)


def tiles(b, t):
    return b * NT + t + 1


def attention_block(nc, a, S, keep):
    with ExitStack() as ctx:
        def sb(name, shape, dt):
            return ctx.enter_context(nc.sbuf_tensor(name, shape, dt))

        def ps(name, cols):
            return ctx.enter_context(nc.psum_tensor(name, [P, cols], F32))

        stage = sb("stage", [P, DC, 4 * D + NE], F32)
        chunk = stage[:, 0, 0:H]
        chunk_hl = stage[:, 1, 0:H].bitcast(F16)
        wqkv = sb("wqkv", [P, 2, DC, 3 * D], F16)
        wproj = sb("wproj", [P, 2, DC, D], F16)
        wrout = sb("wrout", [P, 2, DC, NE], F16)
        ident_f = sb("ident_f", [P, P], F32)
        ident_h = keep["ident"]
        ident_b = sb("ident_b", [P, P], BF16)
        mask_b = sb("mask_b", [P, P], BF16)
        tri_h = sb("tri_h", [P, P], F16)
        ones_h = sb("ones_h", [P, P], F16)
        iota_i = sb("iota_i", [P, 2, NE], I32)
        iota_e = sb("iota_e", [P, 2, NE], F32)
        trig = sb("trig", [P, NT, 2, HD // 2], F32)
        nw = sb("nw", [P, 2, HD], F32)
        ctab = sb("ctab", [P, NT, 2, HD], F32)
        stab = sb("stab", [P, NT, 2, HD], F32)
        ffn_nw = sb("ffn_nw", [P, D], F32)
        bias2 = sb("bias2", [NE + 1, D], F32)
        mhalf = sb("mhalf", [P, NH], F32)
        zeros_i = sb("zeros_i", [P, NE * REGION // P], I32)
        tokid = sb("tokid", [P, NTILE], I32)
        xTf = sb("xTf", [P, DC, T], F32)
        xTh = sb("xTh", [P, 2, DC, T], F16)
        sq = sb("sq", [P, 2 * D], F32)
        ms = sb("ms", [P, NT, 2 * NH], F32)
        rn = sb("rn", [P, NT, 2 * NH], F32)
        qk_raw = sb("qk_raw", [P, 2, 2 * D], F32)
        rot = sb("rot", [P, 2 * D], F32)
        rsum = sb("rsum", [P, 2, 2 * D], F32)
        nat = sb("nat", [P, NT, 2, 2 * D], F16)
        qkT = sb("qkT", [P, 8, T], F16)
        stk = sb("stk", [P, 2, 2, 8, T], F16)
        vst = sb("vst", [P, 2, NT, NH, 32], F32)
        prob = sb("prob", [P, 2, 4, PW], F32)
        raw = sb("raw", [P, 2, 4, T], F32)
        xin = sb("xin", [P, NT, D], F32)
        rcp = sb("rcp", [P, NT, NH], F32)
        an = sb("an", [P, 2, D], F32)
        anh = sb("anh", [P, NT, 2, D], F16)
        aT = sb("aT", [P, 2, 2, 4, P], F16)
        y0 = sb("y0", [P, NT, D], F32)
        st6 = sb("st6", [P, NT, 6], F32)
        mv = sb("mv", [P, NT, 2], F32)
        vv = sb("vv", [P, NT, 6], F32)
        x1 = sb("x1", [P, NT, D], F32)
        xnf = sb("xnf", [P, 2, D], F32)
        xnh = sb("xnh", [P, NT, 2, D], F16)
        xnT = sb("xnT", [P, 2, 2, 4, P], F16)
        lg = sb("lg", [P, NT, NE], F32)
        mx = sb("mx", [P, NT, 8], F32)
        ix = sb("ix", [P, NT, 8], U32)
        ixf = sb("ixf", [P, NT, 2], F32)
        oh = sb("oh", [P, NT, 2, NE], F32)
        mh = sb("mh", [P, NT, NE], F16)
        msum = keep["msum"]
        ex = sb("ex", [P, NT, 2], F32)
        pr = sb("pr", [P, NT, 2], F32)
        pr1 = sb("pr1", [P, NT, 2], F32)
        tot = sb("tot", [P, NT, 2], F32)
        wt = sb("wt", [P, NT, 2], F32)
        comb = sb("comb", [P, NT, NE + 1], F32)
        cw = sb("cw", [P, NT, 2, NE], F32)
        combT = sb("combT", [NE + 1, NT, P], F32)
        sl = sb("sl", [P, NT, NE], F32)
        slm = sb("slm", [P, NT, 2, NE], F32)
        slf = sb("slf", [P, NT, 2], F32)
        sl_i = sb("sl_i", [P, NT, 2], I32)
        tok_i = sb("tok_i", [P, NT], I32)
        res = sb("res", [P, NT, D], F32)

        slots = (ps("slot0", 1024), ps("slot1", 1024))
        pv_bank = ps("pv_bank", T)
        ma = ps("ma", T)
        mb = ps("mb", T)
        mc = ps("mc", T)

        def turns(eng, turn):
            turn(-1, 1, True, False, False)
            turn(0, 0, True, True, False)
            with eng.Fori(0, (NB - 2) // 2) as it:
                turn(it * 2 + 1, 1, True, True, True)
                turn(it * 2 + 2, 0, True, True, True)
            turn(NB - 1, 1, False, True, True)
            turn(NB, 0, False, False, True)

        with nc.Block() as block:
            @block.sync
            def _(sp):
                w = 3 * D
                for c in range(DC):
                    for lo, hi, src in ((0, w, "wqkvT"), (w, w + D, "wprojT"), (w + D, w + D + NE, "routT")):
                        sp.dma_start(stage[:, c, lo:hi], a[src][c * P:(c + 1) * P, :]).then_inc(S("w_loaded"), 16)
                sp.dma_start(trig[:], a["trig"].rearrange("(t p) s f -> p t s f", p=P)).then_inc(S("c_loaded"), 16)
                sp.dma_start(nw[:, 0, :], a["qnw"].partition_broadcast(P)).then_inc(S("c_loaded"), 16)
                sp.dma_start(nw[:, 1, :], a["knw"].partition_broadcast(P)).then_inc(S("c_loaded"), 16)
                sp.dma_start(ffn_nw[:], a["ffn_nw"].partition_broadcast(P)).then_inc(S("c_loaded"), 16)
                sp.dma_start(bias2[:], a["b2all"]).then_inc(S("c_loaded"), 16)

                def load_xT(b):
                    sp.dma_start(xTf[:], a["xT"][bass.ds(b * D, D), :].rearrange("(c p) t -> p c t", p=P)
                                 ).then_inc(S("xT_loaded"), 16)

                load_xT(0)
                sp.wait_ge(S("const_ready"), 1)
                sp.dma_start(a["table"][0:SPARE, :].rearrange("(p c) o -> p (c o)", p=P),
                             zeros_i[:, :]).then_inc(S("table_init"), 16)
                sp.dma_start(a["table"][SPARE:N_ROWS, :].rearrange("(p c) o -> p (c o)", p=P),
                             zeros_i[:, 0:(N_ROWS - SPARE) // P]).then_inc(S("table_init"), 16)

                def turn(b, par, front, attend, back):
                    for p in range(POSITIONS):
                        if p == 1 and front and not (isinstance(b, int) and b + 2 >= NB):
                            wait_apart(sp, S, "xT_split", b + 2)
                            load_xT((b + 2) % NB)
                        for j in at(P_STORE, p):
                            if front and back:
                                k = (b - 1) * CHUNKS + j
                                wait_apart(sp, S, "chunk_lo", k + 1)
                                sp.dma_start(a["w_split"][bass.ds(k * P, P), :], chunk_hl).then_inc(S("chunk_stored"), 16)
                                sp.wait_ge(S("chunk_stored"), (k + 1) * 16)
                                sp.sem_inc(S("chunk_free"), 1)
                        for j in at(P_LOAD, p):
                            if front and back:
                                k = (b - 1) * CHUNKS + j
                                wait_apart(sp, S, "chunk_free", k + 1)
                                sp.dma_start(chunk, a["w_all"][bass.ds(k * P, P), :]).then_inc(S("chunk_in"), 16)
                        for t in at(P_T, p):
                            if front and t % 2:
                                h0 = (t - 1) * P
                                half = slice(h0, h0 + 2 * P)
                                sp.wait_ge(S("ma_free"), (b + 1) * N_MA + MA["t", t] + 2)
                                sp.dma_start(a["qk_dram"][:, :, :, half].rearrange("k s p t -> p (k s) t"),
                                             qkT[:, :, half]).then_inc(S("qk_out"), 16)
                                sp.wait_ge(S("qk_out"), ((b + 1) * 2 + (t // 2) + 1) * 16)
                                for cc in range(DC):
                                    for qk, r, hl, n in ((0, 0, 0, 2), (1, 0, 0, 2), (1, 2, 0, 2), (0, 2, 1, 1), (0, 3, 0, 1)):
                                        row = 64 * cc + HD * r
                                        k = qk * DC + cc
                                        sp.dma_start(
                                            stk[row:row + HD * n, 1 - par, qk, :, half],
                                            a["qk_dram"][k, hl:hl + n, :, half]
                                            .rearrange("s (d i) t -> (s d) i t", d=HD)).then_inc(S(f"stk_in{cc}"), 16)
                        for u in at(P_BIAS, p):
                            if back:
                                wait_apart(sp, S, "res_ready", pairs(b - 1, u))
                                sp.dma_start(a["resid"][bass.ds((b - 1) * T + u * 2 * P, 2 * P), :]
                                             .rearrange("(t p) d -> p t d", p=P),
                                             res[:, pair(u), :]).then_inc(S("res_stored"), 16)
                        for u in at(P_XN, p):
                            if back:
                                wait_apart(sp, S, "xn_lo", pairs(b - 1, u))
                                sp.dma_start(a["xn_rows"][bass.ds((b - 1) * T + u * 2 * P, 2 * P), :]
                                             .rearrange("(t p) d -> p t d", p=P),
                                             xnh[:, pair(u), :, :].rearrange("p t h d -> p t (h d)")
                                             ).then_inc(S("xn_stored"), 16)
                    if attend:
                        if back:
                            wait_apart(sp, S, "y0_done", b * NT)
                        sp.dma_start(xin[:], a["x"][bass.ds(b * T, T), :].rearrange("(t p) d -> p t d", p=P)
                                     ).then_inc(S("xin_loaded"), 16)
                    if back:
                        sp.wait_ge(S("xn_stored"), b * (NT // 2 * 16))
                        sp.wait_ge(S("res_stored"), b * (NT // 2 * 16))
                    sp.sem_inc(S("stores_out"), 1)

                turns(sp, turn)
                for cc in range(DC):
                    sp.wait_ge(S(f"stk_in{cc}"), 16 * 10 * NB)
                sp.wait_ge(S("xT_loaded"), 16 * (NB + 1))
                sp.wait_ge(S("chunk_stored"), 16 * N_CHUNKS)

            @block.gpsimd
            def _(pool):
                pool.memset(ident_f[:], 0.0).then_inc(S("made"), 1)
                pool.memset(mask_b[:], 0.0).then_inc(S("made"), 1)
                pool.memset(tri_h[:], 1.0).then_inc(S("made"), 1)
                pool.memset(zeros_i[:], 0).then_inc(S("made"), 1)
                pool.iota(tokid[:], pattern=[[P, NTILE]], base=0, channel_multiplier=1).then_inc(S("made"), 1)
                pool.memset(mhalf[:], -0.5).then_inc(S("made"), 1)
                pool.iota(iota_i[:, 0, :], pattern=[[1, NE]], base=0, channel_multiplier=0).then_inc(S("made"), 1)
                pool.iota(iota_i[:, 1, :], pattern=[[REGION, NE]], base=0, channel_multiplier=0).then_inc(S("made"), 1)
                pool.memset(ones_h[:], 1.0).then_inc(S("made"), 1)
                pool.wait_ge(S("made"), 9)
                pool.affine_select(out=ident_f[:], in_=ident_f[:], compare_op=ALU.not_equal, fill=1.0, base=0,
                                   pattern=[[-1, P]], channel_multiplier=1).then_inc(S("made"), 1)
                pool.affine_select(out=mask_b[:], in_=mask_b[:], compare_op=ALU.is_ge, fill=-1e30, base=0,
                                   pattern=[[1, P]], channel_multiplier=-1).then_inc(S("made"), 1)
                pool.affine_select(out=tri_h[:], in_=tri_h[:], compare_op=ALU.is_gt, fill=0.0, base=0,
                                   pattern=[[1, P]], channel_multiplier=-1).then_inc(S("made"), 1)
                pool.wait_ge(S("made"), 12)
                pool.tensor_copy(ident_h[:], ident_f[:]).then_inc(S("made"), 1)
                pool.tensor_copy(ident_b[:], ident_f[:]).then_inc(S("made"), 1)
                pool.wait_ge(S("made"), 14)
                pool.sem_inc(S("const_ready"), 1)
                pool.wait_ge(S("table_init"), 32)

                def turn(b, par, front, attend, back):
                    for p in range(POSITIONS):
                        for t in range(NT):
                            for q in range(4):
                                if front and p == P_QK[t] + min(q, 2):
                                    pool.wait_ge(S("ms_ready"), tiles(b + 1, t))
                                    h = slice(q * NH // 2, (q + 1) * NH // 2)
                                    pool.tensor_tensor(rn[:, t, h], ms[:, t, h], mhalf[:, 0:NH // 2],
                                                       ALU.pow).then_inc(S("rn_ready"), 1)
                        for u in at(P_BIAS, p):
                            if back:
                                wait_apart(pool, S, "slots_ready", pairs(b - 1, u))
                                for t in range(2 * u, 2 * u + 2):
                                    for k in range(TOPK):
                                        pool.indirect_dma_start(
                                            a["table"], bass.IndirectOffsetOnAxis(ap=sl_i[:, t, k:k + 1], axis=0),
                                            tok_i[:, t:t + 1], None).then_inc(S("scattered"), 16)
                        for u in at(P_PROJ, p):
                            if back:
                                k = pairs(b - 1, u)
                                v = [vv[:, pair(u), c] for c in range(6)]
                                pool.wait_ge(S("var_ready"), k)
                                pool.tensor_tensor(v[1], v[0], mhalf[:, 0:2], ALU.pow).then_inc(S("rstd"), 1)
                                pool.wait_ge(S("rstd"), k)
                                pool.tensor_tensor(v[2], v[1], v[1], ALU.mult).then_inc(S("rstd_sq"), 1)
                                pool.wait_ge(S("rstd_sq"), k)
                                pool.tensor_tensor(v[3], v[2], mv[:, pair(u), 1], ALU.mult).then_inc(S("msq"), 1)
                                wait_apart(pool, S, "msq", k)
                                pool.tensor_scalar(v[4], v[3], FFN_EPS, None, ALU.add).then_inc(S("msq_eps"), 1)
                                pool.wait_ge(S("msq_eps"), k)
                                pool.tensor_tensor(v[5], v[4], mhalf[:, 0:2], ALU.pow).then_inc(S("norms_ready"), 1)
                    if back:
                        pool.wait_ge(S("scattered"), b * (NT * TOPK * 16))
                    pool.sem_inc(S("ids_out"), 1)

                turns(pool, turn)

            @block.scalar
            def _(act):
                act.wait_ge(S("w_loaded"), 16 * 3 * DC)
                w = 3 * D
                act.activation(wqkv[:, 0, :, :], stage[:, :, 0:w], ACT.Copy, scale=WS).then_inc(S("w_hi"), 1)
                act.activation(wproj[:, 0, :, :], stage[:, :, w:w + D], ACT.Copy, scale=WS).then_inc(S("w_hi"), 1)
                act.activation(wrout[:, 0, :, :], stage[:, :, w + D:], ACT.Copy, scale=RS).then_inc(S("w_hi"), 1)
                act.wait_ge(S("tables_ready"), 1)

                def turn(b, par, front, attend, back):
                    if front:
                        act.wait_ge(S("xT_loaded"), (b + 2) * 16)
                        if not isinstance(b, int) or b >= 0:
                            act.wait_ge(S("v_done"), pairs(b, 1))
                        act.activation(xTh[:, 0, :, :], xTf[:, :, :], ACT.Copy).then_inc(S("xT_hi"), 1)
                    for p in range(POSITIONS):
                        g = p // 4
                        if attend and p < 16:
                            for u in ((0, 1), (2,), (3,), (4, 5))[p % 4]:
                                act.wait_ge(S("unit_ready"), b * 24 + g * 6 + u + 1)
                                if u == 0 and (not isinstance(b, int) or b * 4 + g >= 2):
                                    act.wait_ge(S("pv_done"), b * 4 + g - 1)
                                slot = slots[u % 2]
                                pp = prob[:, g % 2]
                                if u in (2, 5):
                                    r = 0 if u == 2 else 2
                                    act.activation(pp[:, r:r + 2, 1024:PW],
                                                   slot[:, 0:512].rearrange("p (r q) -> p r q", r=2),
                                                   ACT.Exp, scale=ATT_SCALE).then_inc(S("exp_done"), 1)
                                else:
                                    r = (0, 1, None, 2, 3)[u]
                                    act.activation(pp[:, r, 0:1024], slot[:, 0:1024], ACT.Exp,
                                                   scale=ATT_SCALE).then_inc(S("exp_done"), 1)
                        if p % 4 == 0 and ((p == 0 and back) or (0 < p < 16 and attend)):
                            s = b * 4 + g
                            act.wait_ge(S("pv_done"), s)
                            act.activation(raw[:, (1 - par) if p == 0 else par, (g - 1) % 4, :], pv_bank[:, :],
                                           ACT.Copy).then_inc(S("raw_done"), 1)
                        for t in at(P_QK, p):
                            if front:
                                k = tiles(b + 1, t)
                                act.wait_ge(S("qk_done"), k)
                                if not isinstance(b, int) or k > 2:
                                    act.wait_ge(S("rot_done"), (k - 2) * 3)
                                act.activation(qk_raw[:, t % 2, :], ma[:, :], ACT.Copy).then_inc(S("ma_free"), 1)
                                if not isinstance(b, int) or k > 1:
                                    act.wait_ge(S("ss_done"), k - 1)
                                act.wait_ge(S("ma_free"), (b + 1) * N_MA + MA["qk", t] + 2)
                                act.activation(sq[:], qk_raw[:, t % 2, :], ACT.Square).then_inc(S("sq_ready"), 1)
                        for u in at(P_V, p):
                            if front:
                                act.wait_ge(S("v_done"), pairs(b + 1, u))
                                act.activation(vst[:, 1 - par, pair(u), :, 0:HD],
                                               ma[:, :].rearrange("p (t h d) -> p t h d", t=2, d=HD), ACT.Copy,
                                               scale=1.0 / WS).then_inc(S("ma_free"), 1)
                        for t in at(P_T, p):
                            if front:
                                act.wait_ge(S("t_done"), tiles(b + 1, t))
                                act.activation(qkT[:, :, t * P:(t + 1) * P],
                                               ma[:, :].bitcast(F16).rearrange("p (k t) -> p k t", k=8),
                                               ACT.Copy).then_inc(S("ma_free"), 1)
                        for u in at(P_AT, p):
                            if back:
                                act.wait_ge(S("at_done"), pairs(b - 1, u))
                                act.activation(aT[:, u].rearrange("p t k q -> p (t k q)"),
                                               mb[:, :].bitcast(F16), ACT.Copy).then_inc(S("mb_free"), 1)
                        for u in at(P_XN, p):
                            if back:
                                act.wait_ge(S("xnT_done"), pairs(b - 1, u))
                                act.activation(xnT[:, u].rearrange("p t k q -> p (t k q)"),
                                               mc[:, :].bitcast(F16), ACT.Copy).then_inc(S("mc_free"), 1)
                        for u in at(P_LG, p):
                            if back:
                                act.wait_ge(S("top_ready"), tiles(b - 1, 2 * u + 1))
                                act.activation(ex[:, pair(u), :], mx[:, pair(u), 0:2], ACT.Exp, scale=-1.0).then_inc(S("ex_ready"), 1)
                        for j in at(P_SPLIT, p):
                            if front and back:
                                k = (b - 1) * CHUNKS + j
                                act.wait_ge(S("chunk_in"), (k + 1) * 16)
                                act.activation(chunk_hl[:, 0:H], chunk, ACT.Copy, scale=WS).then_inc(S("chunk_hi"), 1)

                turns(act, turn)

            @block.vector
            def _(dve):
                def then(ins, name, count):
                    ins.then_inc(S(name), 1)
                    dve.wait_ge(S(name), count)

                def then_apart(ins, name, count):
                    ins.then_inc(S(name), 1)
                    wait_apart(dve, S, name, count)

                for bank in ("ma_free", "mb_free", "mc_free"):
                    dve.sem_inc(S(bank), 1)
                dve.memset(vst[:].rearrange("p a t h d -> p (a t h d)"), 0.0).then_inc(S("vst_zero"), 1)
                dve.memset(comb[:], 1.0).then_inc(S("vst_zero"), 1)
                dve.memset(msum[:], 0.0).then_inc(S("msum_free"), 1)
                dve.wait_ge(S("vst_zero"), 2)
                dve.memset(vst[:].rearrange("p a t h d -> p (a t h) d")[:, :, HD:HD + 1], 1.0).then_inc(S("vst_one"), 1)
                dve.wait_ge(S("const_ready"), 1)
                dve.tensor_copy(iota_e[:], iota_i[:]).then_inc(S("vst_one"), 1)
                dve.wait_ge(S("w_hi"), 3)
                w = 3 * D
                for k, (dst, lo, hi, scale) in enumerate(((wqkv, 0, w, WS), (wproj, w, w + D, WS),
                                                          (wrout, w + D, w + D + NE, RS))):
                    dve.scalar_tensor_tensor(dst[:, 1, :, :], stage[:, :, lo:hi], scale, dst[:, 0, :, :],
                                             ALU.mult, ALU.subtract).then_inc(S("w_lo"), 1)
                dve.wait_ge(S("c_loaded"), 80)
                hh = HD // 2
                for qk in range(2):
                    for half in range(2):
                        here = slice(half * hh, half * hh + hh)
                        other = slice(hh - half * hh, HD - half * hh)
                        wb = nw[:, qk, here].unsqueeze(1).broadcast_to([P, NT, hh])
                        wo = nw[:, qk, other].unsqueeze(1).broadcast_to([P, NT, hh])
                        dve.scalar_tensor_tensor(ctab[:, :, qk, here], trig[:, :, 0, :], 1.0 / WS, wb,
                                                 ALU.mult, ALU.mult).then_inc(S("rope_made"), 1)
                        dve.scalar_tensor_tensor(stab[:, :, qk, here], trig[:, :, 1, :], (2 * half - 1) / WS, wo,
                                                 ALU.mult, ALU.mult).then_inc(S("rope_made"), 1)
                dve.wait_ge(S("rope_made"), 8)
                dve.wait_ge(S("vst_one"), 2)
                dve.wait_ge(S("w_lo"), 3)
                dve.sem_inc(S("tables_ready"), 1)
                dve.sem_inc(S("chunk_free"), 1)

                def turn(b, par, front, attend, back):
                    if front:
                        dve.wait_ge(S("xT_hi"), b + 2)
                        dve.tensor_tensor(xTh[:, 1, :, :], xTf[:, :, :], xTh[:, 0, :, :],
                                          ALU.subtract).then_inc(S("xT_split"), 1)
                    for p in range(POSITIONS):
                        for u in at(P_XN, p):
                            if back:
                                k = pairs(b - 1, u)
                                dve.wait_ge(S("norms_ready"), k)
                                for t in range(2 * u, 2 * u + 2):
                                    dve.tensor_scalar(x1[:, t, :], y0[:, t, :], mv[:, t, 0:1], vv[:, t, 1:2],
                                                      ALU.subtract, ALU.mult).then_inc(S("x1_done"), 1)
                                for t in range(2 * u, 2 * u + 2):
                                    dve.wait_ge(S("x1_done"), tiles(b - 1, t))
                                    dve.scalar_tensor_tensor(xnf[:, t % 2, :], x1[:, t, :], vv[:, t, 5:6], ffn_nw[:],
                                                             ALU.mult, ALU.mult).then_inc(S("xnf_done"), 1)
                                dve.wait_ge(S("xnf_done"), tiles(b - 1, 2 * u + 1))
                                dve.wait_ge(S("stores_out"), b + 1)
                                then(dve.tensor_copy(xnh[:, pair(u), 0, :], xnf[:]), "xn_hi", k)
                                then(dve.tensor_tensor(xnh[:, pair(u), 1, :], xnf[:], xnh[:, pair(u), 0, :],
                                                       ALU.subtract), "xn_lo", k)
                        for u in at(P_W, p):
                            if back:
                                k = pairs(b - 1, u)
                                q = pair(u)
                                dve.wait_ge(S("ex_ready"), k)
                                then(dve.tensor_scalar(pr1[:, q, :], ex[:, q, :], 1.0, None, ALU.add), "sig_den", k)
                                then(dve.reciprocal(pr[:, q, :], pr1[:, q, :]), "sig", k)
                                then(dve.scalar_tensor_tensor(tot[:, q, 0:1], pr[:, q, 0:1], 1e-6, pr[:, q, 1:2],
                                                              ALU.add, ALU.add), "sig_sum", k)
                                then(dve.reciprocal(tot[:, q, 1:2], tot[:, q, 0:1]), "sig_rcp", k)
                                then(dve.tensor_tensor(wt[:, q, :], pr[:, q, :], tot[:, q, 1:2].broadcast_to([P, 2, 2]),
                                                       ALU.mult), "wt_done", k)
                                dve.tensor_copy(keep["weights"][:, bass.ds(((b - 1) * NT + 2 * u) * 2, 4)],
                                                wt[:, q, :].rearrange("p t k -> p (t k)")).then_inc(S("kept"), 1)
                                then(dve.tensor_tensor(cw[:, q].rearrange("p t k e -> p (t k) e"),
                                                       oh[:, q].rearrange("p t k e -> p (t k) e"),
                                                       wt[:, q, :].rearrange("p t k -> p (t k)").unsqueeze(2)
                                                       .broadcast_to([P, 4, NE]), ALU.mult), "cw_done", k)
                                dve.tensor_tensor(comb[:, q, 0:NE], cw[:, q, 0, :], cw[:, q, 1, :],
                                                  ALU.add).then_inc(S("comb_ready"), 1)
                        for t in at(P_QN, p):
                            if front:
                                k = tiles(b + 1, t)
                                dve.wait_ge(S("rn_ready"), k * 4)
                                then(dve.tensor_tensor(rot[:].rearrange("p (c d i) -> p c i d", c=2 * DC, d=HD),
                                                       rsum[:, t % 2, :].rearrange("p (c i d) -> p c i d", c=2 * DC, d=HD),
                                                       rn[:, t, :].rearrange("p (c i) -> p c i", c=2 * DC).unsqueeze(3)
                                                       .broadcast_to([P, 2 * DC, NH // DC, HD]), ALU.mult), "qn_done", k)
                                then(dve.tensor_copy(nat[:, t, 0, :], rot[:]), "nat_hi", k)
                                then(dve.tensor_tensor(nat[:, t, 1, :], rot[:], nat[:, t, 0, :],
                                                       ALU.subtract), "nat_ready", k)
                        for t in at(P_QK, p):
                            if front:
                                k = tiles(b + 1, t)
                                dve.wait_ge(S("ma_free"), (b + 1) * N_MA + MA["qk", t] + 2)
                                q4 = qk_raw[:, t % 2, :].rearrange("p (k h d) -> p k h d", k=2, d=HD)
                                r0 = rot[:].rearrange("p (k h d) -> p k h d", k=2, d=HD)
                                r1 = rsum[:, t % 2, :].rearrange("p (k h d) -> p k h d", k=2, d=HD)
                                dve.tensor_tensor(r0, q4, ctab[:, t].unsqueeze(2).broadcast_to([P, 2, NH, HD]),
                                                  ALU.mult).then_inc(S("rot_done"), 1)
                                dve.tensor_tensor(r1[:, :, :, 0:hh], q4[:, :, :, hh:HD],
                                                  stab[:, t, :, 0:hh].unsqueeze(2).broadcast_to([P, 2, NH, hh]),
                                                  ALU.mult).then_inc(S("rot_done"), 1)
                                dve.tensor_tensor(r1[:, :, :, hh:HD], q4[:, :, :, 0:hh],
                                                  stab[:, t, :, hh:HD].unsqueeze(2).broadcast_to([P, 2, NH, hh]),
                                                  ALU.mult).then_inc(S("rot_done"), 1)
                                dve.wait_ge(S("sq_ready"), k)
                                then(dve.tensor_reduce(ms[:, t, :], sq[:].rearrange("p (h d) -> p h d", d=HD),
                                                       AX.X, ALU.add), "ss_done", k)
                                dve.tensor_scalar(ms[:, t, :], ms[:, t, :], 1.0 / (HD * WS * WS), RMS_EPS,
                                                  ALU.mult, ALU.add).then_inc(S("ms_ready"), 1)
                                dve.wait_ge(S("rot_done"), k * 3)
                                then(dve.tensor_tensor(rsum[:, t % 2, :], rot[:], rsum[:, t % 2, :], ALU.add), "rsum_done", k)
                        for t in at(P_NAT, p):
                            if back:
                                k = tiles(b - 1, t)
                                dve.wait_ge(S("nat_done"), k)
                                o3 = mb[:, :].rearrange("p (h d) -> p h d", d=32)
                                then(dve.reciprocal(rcp[:, t, :], o3[:, :, HD]), "rcp_done", k)
                                dve.tensor_tensor(an[:, t % 2, :].rearrange("p (h d) -> p h d", d=HD), o3[:, :, 0:HD],
                                                  rcp[:, t, :].unsqueeze(2).broadcast_to([P, NH, HD]),
                                                  ALU.mult).then_inc(S("mb_free"), 1)
                                dve.wait_ge(S("mb_free"), (b - 1) * N_MB + MB["nat", t] + 2)
                                if t % 2:
                                    u = t // 2
                                    k = pairs(b - 1, u)
                                    then(dve.tensor_copy(anh[:, pair(u), 0, :], an[:]), "an_hi", k)
                                    then(dve.tensor_tensor(anh[:, pair(u), 1, :], an[:], anh[:, pair(u), 0, :],
                                                           ALU.subtract), "an_ready", k)
                        for u in at(P_PROJ, p):
                            if back:
                                dve.wait_ge(S("proj_done"), pairs(b - 1, u))
                                dve.wait_ge(S("xin_loaded"), b * 16)
                                dve.scalar_tensor_tensor(y0[:, pair(u), :].rearrange("p t d -> p (t d)"), mb[:, :], 1.0 / WS,
                                                         xin[:, pair(u), :].rearrange("p t d -> p (t d)"),
                                                         ALU.mult, ALU.add).then_inc(S("mb_free"), 1)
                                dve.wait_ge(S("mb_free"), (b - 1) * N_MB + MB["proj", u] + 2)
                                for t in range(2 * u, 2 * u + 2):
                                    dve.bn_stats(st6[:, t, :], y0[:, t, :]).then_inc(S("y0_done"), 1)
                                for t in range(2 * u, 2 * u + 2):
                                    wait_apart(dve, S, "y0_done", tiles(b - 1, t))
                                    dve.bn_aggr(mv[:, t, :], st6[:, t, :]).then_inc(S("mv_done"), 1)
                                dve.wait_ge(S("mv_done"), tiles(b - 1, 2 * u + 1))
                                dve.tensor_scalar(vv[:, pair(u), 0], mv[:, pair(u), 1], LN_EPS, None,
                                                  ALU.add).then_inc(S("var_ready"), 1)
                        for u in at(P_LG, p):
                            if back:
                                k = pairs(b - 1, u)
                                q = pair(u)
                                dve.wait_ge(S("lg_done"), k)
                                dve.tensor_scalar(lg[:, q, :], mc[:, 0:2 * NE].rearrange("p (t e) -> p t e", t=2), 1.0 / RS,
                                                  None, ALU.mult).then_inc(S("mc_free"), 1)
                                wait_apart(dve, S, "mc_free", (b - 1) * N_MC + MC["lg", u] + 2)
                                for t in range(2 * u, 2 * u + 2):
                                    dve.max(mx[:, t, :], lg[:, t, :]).then_inc(S("top_ready"), 1)
                                for t in range(2 * u, 2 * u + 2):
                                    wait_apart(dve, S, "top_ready", tiles(b - 1, t))
                                    dve.max_index(ix[:, t, :], mx[:, t, :], lg[:, t, :]).then_inc(S("ix_done"), 1)
                                dve.wait_ge(S("ix_done"), tiles(b - 1, 2 * u + 1))
                                then(dve.tensor_copy(ixf[:, q, :], ix[:, q, 0:2]), "ixf_done", k)
                                then(dve.tensor_tensor(oh[:, q].rearrange("p t k e -> p (t k) e"),
                                                       iota_e[:, 0, :].unsqueeze(1).broadcast_to([P, 4, NE]),
                                                       ixf[:, q, :].rearrange("p t k -> p (t k)").unsqueeze(2)
                                                       .broadcast_to([P, 4, NE]), ALU.is_equal), "oh_done", k)
                                dve.tensor_tensor(mh[:, q, :], oh[:, q, 0, :], oh[:, q, 1, :], ALU.add).then_inc(S("mh_ready"), 1)
                        for u in at(P_RANK, p):
                            if back:
                                k = pairs(b - 1, u)
                                q = pair(u)
                                dve.wait_ge(S("rank_done"), k)
                                dve.tensor_tensor(sl[:, q, :], mc[:, 0:2 * NE].rearrange("p (t e) -> p t e", t=2),
                                                  iota_e[:, 1, :].unsqueeze(1).broadcast_to([P, 2, NE]), ALU.add
                                                  ).then_inc(S("sl_done"), 1)
                                dve.tensor_copy(combT[:, q, :], mc[0:NE + 1, P:3 * P].rearrange("p (t q) -> p t q", t=2)
                                                ).then_inc(S("mc_free"), 1)
                                for t in range(2 * u, 2 * u + 2):
                                    dve.wait_ge(S("msum_free"), tiles(b - 1, t))
                                    dve.tensor_tensor(msum[:], msum[:], mh[:, t, :], ALU.add).then_inc(S("msum_free"), 1)
                                dve.wait_ge(S("sl_done"), k)
                                for t in range(2 * u, 2 * u + 2):
                                    dve.tensor_tensor(slm[:, t, :, :], oh[:, t, :, :],
                                                      sl[:, t, :].unsqueeze(1).broadcast_to([P, 2, NE]),
                                                      ALU.mult).then_inc(S("slm_done"), 1)
                                dve.wait_ge(S("slm_done"), tiles(b - 1, 2 * u + 1))
                                then(dve.tensor_reduce(slf[:, q, :], slm[:, q, :, :], AX.X, ALU.add), "slf_done", k)
                                dve.tensor_copy(keep["slots"][:, bass.ds(((b - 1) * NT + 2 * u) * 2, 4)],
                                                slf[:, q, :].rearrange("p t k -> p (t k)")).then_inc(S("kept"), 1)
                                dve.wait_ge(S("ids_out"), b + 1)
                                dve.tensor_copy(tok_i[:, q], tokid[:, bass.ds((b - 1) * NT + 2 * u, 2)]
                                                ).then_inc(S("tok_ready"), 1)
                                dve.wait_ge(S("tok_ready"), k)
                                dve.tensor_copy(sl_i[:, q, :], slf[:, q, :]).then_inc(S("slots_ready"), 1)
                        for u in at(P_BIAS, p):
                            if back:
                                dve.wait_ge(S("bias_done"), pairs(b - 1, u))
                                dve.tensor_tensor(res[:, pair(u), :].rearrange("p t d -> p (t d)"), mc[:, :],
                                                  x1[:, pair(u), :].rearrange("p t d -> p (t d)"), ALU.add
                                                  ).then_inc(S("mc_free"), 1)
                                dve.wait_ge(S("mc_free"), (b - 1) * N_MC + MC["bias", u] + 2)
                                dve.sem_inc(S("res_ready"), 1)
                        for j in at(P_SPLIT, p):
                            if front and back:
                                k = (b - 1) * CHUNKS + j
                                dve.wait_ge(S("chunk_hi"), k + 1)
                                dve.scalar_tensor_tensor(chunk_hl[:, H:2 * H], chunk, WS, chunk_hl[:, 0:H],
                                                         ALU.mult, ALU.subtract).then_inc(S("chunk_lo"), 1)

                turns(dve, turn)

            @block.tensor
            def _(pe):
                pe.wait_ge(S("tables_ready"), 1)
                pe.wait_ge(S("const_ready"), 1)

                def scores(b, par, g, u):
                    i = b * 24 + g * 6 + u
                    if not isinstance(b, int) or i >= 2:
                        pe.wait_ge(S("exp_done"), i - 1)
                    slot = slots[u % 2]
                    if u in (2, 5):
                        jobs = [(4 * g + (0 if u == 2 else 2) + r, 2, 256 * r, r == 0) for r in range(2)]
                    else:
                        h = 4 * g + (0, 1, None, 2, 3)[u]
                        jobs = [(h, 0, 0, True), (h, 1, 512, True), (h, 3, 896, False)]
                    for h, j, col, first in jobs:
                        rows = slice(64 * (h // 8), 64 * (h // 8) + 64)
                        pe.matmul(slot[:, col:col + T - P * j],
                                  stk[rows, par, 1, h % 8, P * j:P * j + P],
                                  stk[rows, par, 0, h % 8, P * j:T], start=first, stop=False, skip_group_check=True)
                    for h, j, col, first in jobs:
                        last = pe.matmul(slot[:, col:col + P], ident_b[:], mask_b[:], start=False, stop=True,
                                         skip_group_check=True)
                    last.then_inc(S("unit_ready"), 1)

                def turn(b, par, front, attend, back):
                    for p in range(POSITIONS):
                        g = p // 4
                        if attend and p < 16:
                            if p % 8 == 0:
                                pe.wait_ge(S(f"stk_in{p // 8}"), (b + 1) * (10 * 16))
                            for u in ((0, 1), (2,), (3,), (4, 5))[p % 4]:
                                scores(b, par, g, u)
                        if p % 4 == 0 and ((p == 0 and back) or (0 < p < 16 and attend)):
                            s = b * 4 + g
                            pe.wait_ge(S("exp_done"), s * 6)
                            pe.wait_ge(S("ma_free"), (b + (0 if p == 0 else 1)) * N_MA + 1)
                            if not isinstance(b, int) or s >= 2:
                                pe.wait_ge(S("raw_done"), s - 1)
                            vp = (1 - par) if p == 0 else par
                            gg = (g - 1) % 4
                            for j in range(NT):
                                for r in range(4):
                                    last = pe.matmul(pv_bank[32 * r:32 * r + 32, P * j:T],
                                                     vst[:, vp, j, 4 * gg + r, :],
                                                     prob[:, (g - 1) % 2, r, SEG[j]:SEG[j] + T - P * j],
                                                     start=(j == 0), stop=(j == NT - 1), skip_group_check=True)
                            last.then_inc(S("pv_done"), 1)
                        for t in at(P_QK, p):
                            if front:
                                pe.wait_ge(S("xT_split"), b + 2)
                                pe.wait_ge(S("ma_free"), (b + 1) * N_MA + MA["qk", t] + 1)
                                product(ma[:, 0:2 * D], xTh, t, wqkv, slice(0, 2 * D)).then_inc(S("qk_done"), 1)
                        for u in at(P_V, p):
                            if front:
                                pe.wait_ge(S("ma_free"), (b + 1) * N_MA + MA["v", u] + 1)
                                for j in range(2):
                                    last = product(ma[:, j * D:(j + 1) * D], xTh, 2 * u + j, wqkv, slice(2 * D, 3 * D))
                                last.then_inc(S("v_done"), 1)
                        for t in at(P_T, p):
                            if front:
                                pe.wait_ge(S("nat_ready"), tiles(b + 1, t))
                                pe.wait_ge(S("ma_free"), (b + 1) * N_MA + MA["t", t] + 1)
                                for k in range(8):
                                    last = pe.transpose(ma[:, 64 * k:64 * k + 64].bitcast(F16),
                                                        nat[:, t, k % 2, P * (k // 2):P * (k // 2) + P], ident_h[:])
                                last.then_inc(S("t_done"), 1)
                        for t in at(P_NAT, p):
                            if back:
                                pe.wait_ge(S("raw_done"), b * 4)
                                pe.wait_ge(S("mb_free"), (b - 1) * N_MB + MB["nat", t] + 1)
                                for q in range(4):
                                    last = pe.transpose(mb[:, P * q:P * q + P], raw[:, 1 - par, q, P * t:P * t + P],
                                                        ident_f[:])
                                last.then_inc(S("nat_done"), 1)
                        for u in at(P_AT, p):
                            if back:
                                pe.wait_ge(S("an_ready"), pairs(b - 1, u))
                                pe.wait_ge(S("mb_free"), (b - 1) * N_MB + MB["at", u] + 1)
                                for j in range(2):
                                    for k in range(4):
                                        c = 64 * (4 * j + k)
                                        last = pe.transpose(mb[:, c:c + 64].bitcast(F16),
                                                            anh[:, 2 * u + j, k // 2, P * (k % 2):P * (k % 2) + P], ident_h[:])
                                last.then_inc(S("at_done"), 1)
                        for u in at(P_PROJ, p):
                            if back:
                                pe.wait_ge(S("mb_free"), (b - 1) * N_MB + max(MB["proj", u], MB["at", u] + 1) + 1)
                                pieces = [(x, w, c) for c in range(DC) for x, w in ((0, 0), (0, 1), (1, 0))]
                                for j in range(2):
                                    for n, (x, w, c) in enumerate(pieces):
                                        last = pe.matmul(mb[:, j * D:(j + 1) * D], aT[:, u, j, x * DC + c, :], wproj[:, w, c, :],
                                                         start=(n == 0), stop=(n == len(pieces) - 1))
                                last.then_inc(S("proj_done"), 1)
                        for u in at(P_XN, p):
                            if back:
                                pe.wait_ge(S("xn_lo"), pairs(b - 1, u))
                                pe.wait_ge(S("mc_free"), (b - 1) * N_MC + MC["xn", u] + 1)
                                for j in range(2):
                                    for k in range(4):
                                        c = 64 * (4 * j + k)
                                        last = pe.transpose(mc[:, c:c + 64].bitcast(F16),
                                                            xnh[:, 2 * u + j, k // 2, P * (k % 2):P * (k % 2) + P], ident_h[:])
                                last.then_inc(S("xnT_done"), 1)
                        for u in at(P_RANK, p):
                            if back:
                                pe.wait_ge(S("comb_ready"), pairs(b - 1, u))
                                pe.wait_ge(S("mh_ready"), pairs(b - 1, u))
                                pe.wait_ge(S("msum_free"), tiles(b - 1, 2 * u))
                                pe.wait_ge(S("mc_free"), (b - 1) * N_MC + MC["rank", u] + 1)
                                for j in range(2):
                                    pe.transpose(mc[0:NE + 1, (j + 1) * P:(j + 2) * P], comb[:, 2 * u + j, :], ident_f[:])
                                for j in range(2):
                                    cols = slice(j * NE, (j + 1) * NE)
                                    pe.matmul(mc[:, cols], tri_h[:], mh[:, 2 * u + j, :], start=True, stop=False)
                                    if j:
                                        pe.matmul(mc[:, cols], ones_h[:], mh[:, 2 * u, :], start=False, stop=False)
                                    last = pe.matmul(mc[:, cols], ones_h[:], msum[:], start=False, stop=True)
                                last.then_inc(S("rank_done"), 1)
                        for u in at(P_BIAS, p):
                            if back:
                                pe.wait_ge(S("mc_free"), (b - 1) * N_MC + max(MC["bias", u], MC["rank", u] + 1) + 1)
                                for j in range(2):
                                    last = pe.matmul(mc[:, j * D:(j + 1) * D], combT[:, 2 * u + j, :], bias2[:], start=True, stop=True)
                                last.then_inc(S("bias_done"), 1)
                        for u in at(P_LG, p):
                            if back:
                                pe.wait_ge(S("mc_free"), (b - 1) * N_MC + max(MC["lg", u], MC["xn", u] + 1) + 1)
                                pieces = [(x, w, c) for c in range(DC) for x in range(2) for w in range(2)]
                                for j in range(2):
                                    for n, (x, w, c) in enumerate(pieces):
                                        last = pe.matmul(mc[:, j * NE:(j + 1) * NE], xnT[:, u, j, x * DC + c, :], wrout[:, w, c, :],
                                                         start=(n == 0), stop=(n == len(pieces) - 1))
                                last.then_inc(S("lg_done"), 1)

                def product(out, xh, t, w, cols):
                    pieces = [(x, y, c) for c in range(DC) for x, y in ((0, 0), (0, 1), (1, 0))]
                    for n, (x, y, c) in enumerate(pieces):
                        last = pe.matmul(out, xh[:, x, c, P * t:P * t + P], w[:, y, c, cols],
                                         start=(n == 0), stop=(n == len(pieces) - 1))
                    return last

                turns(pe, turn)


N_TILES = N_ROUTED + N_SHARED
N_CHUNKS = 4 * (NE + 1)
CH = H
EW = 4 * 2 * CH
R_LAST = N_ROUTED - 1
assert N_ROUTED % 2 == 1 and N_SHARED % 2 == 0


def expert_block(nc, a, S, keep):
    with ExitStack() as ctx:
        def sb(name, shape, dt):
            return ctx.enter_context(nc.sbuf_tensor(name, shape, dt))

        def ps(name, cols):
            return ctx.enter_context(nc.psum_tensor(name, [P, cols], F32))

        wts = sb("wts", [P, (NE + 1) * EW], F16)
        b1 = sb("b1", [P, (NE + 1) * HC], F32)
        ident = sb("ident2", [P, P], F16)
        idx = sb("idx", [P, 2, 2], I32)
        xg = sb("xg", [P, 2, 2, 2 * D], F16)
        xgT = sb("xgT", [P, 2, 4, TT], F16)
        hf = sb("hf", [P, HC, TT], F32)
        hh = sb("hh", [P, 2, 2, HC, TT], F16)
        yb = sb("yb", [P, 2, 2, D], F32)
        ge = sb("ge", [P, NE, N_SHARED], F32)
        io_i = sb("io_i", [P, N_ROUTED + N_SHARED], I32)
        io_f = sb("io_f", [P, N_ROUTED + N_SHARED], F32)
        cum = sb("cum", [P, 3, NE], F32)
        upto = sb("upto", [P, 2, NE, NE], F32)
        past = sb("past", [1, 2, N_ROUTED, NE], F32)
        te = sb("te", [1, 4, N_ROUTED], F32)
        shift = sb("shift", [P, NE], F32)
        yrow = sb("yrow", [P, 2, 2 * NTILE], F32)
        tab = sb("tab", [1, 2, N_TILES], I32)
        ones = sb("ones2", [P, P], F16)
        yidx = sb("yidx", [P, 2, 2, TOPK], I32)
        yk = sb("yk", [P, 2, TOPK, 2, D], F32)
        rs = sb("rs", [P, 2, 2, D], F32)
        acc = sb("acc", [P, 2, 2, D], F32)
        ob = sb("ob", [P, 2, 2, D], F32)
        st = sb("st", [P, 2, 2, 6], F32)
        mean_var = sb("mean_var", [P, 2, 2, 2], F32)
        var_eps = sb("var_eps", [P, 2, 2], F32)
        rstd = sb("rstd_f", [P, 2, 2], F32)
        half = sb("half_f", [P, 2], F32)
        tr = [ps(f"tr{i}", 512) for i in range(2)]
        hb = [ps(f"hb{i}", 512) for i in range(4)]
        ybank = [ps(f"yb{i}", 512) for i in range(2)]

        def first(par):
            return (R_LAST + 1 + 1 - par) // 2

        def tiles_of(eng, step):
            step(0, 0, 0)
            step(0, 1, 1)
            with eng.Fori(1, (R_LAST - 4) // 2) as h:
                step(h, 0, None)
                step(h, 1, None)
            for i in range(R_LAST - 4, R_LAST + 4):
                step(i // 2, i % 2, i)
            with eng.Fori((R_LAST + 4) // 2, (N_TILES - 3) // 2) as h:
                step(h, 0, R_LAST + 4)
                step(h, 1, R_LAST + 5)
            for i in range(N_TILES - 3, N_TILES):
                step(i // 2, i % 2, i)

        def shared(i):
            return i is not None and i > R_LAST

        with nc.Block() as block:
            @block.gpsimd
            def _(pool):
                pool.iota(io_i[:, 0:N_ROUTED], pattern=[[1, N_ROUTED]], base=0, channel_multiplier=0).then_inc(S("io_made"), 1)
                pool.iota(io_i[:, N_ROUTED:], pattern=[[TT, N_SHARED]], base=0, channel_multiplier=0).then_inc(S("io_made"), 1)
                pool.memset(half[:], -0.5).then_inc(S("half_made"), 1)

                def gather(h, par):
                    wait_apart(pool, S, f"idx_loaded{par}", (h + 1) * 16)
                    if not isinstance(h, int) or h >= 1:
                        wait_apart(pool, S, "tr_done", h * 2 + par - 1)
                    for j in range(2):
                        pool.indirect_dma_start(xg[:, par, j, :], None, a["xn_rows"],
                                                bass.IndirectOffsetOnAxis(ap=idx[:, par, j:j + 1], axis=0)
                                                ).then_inc(S(f"gathered{par}"), 16)

                def gather_routed(h, par):
                    wait_apart(pool, S, "yidx_ready", h * 2 + par - R_LAST)
                    for k in range(TOPK):
                        for j in range(2):
                            pool.indirect_dma_start(yk[:, par, k, j, :], None, a["y_rows"],
                                                    bass.IndirectOffsetOnAxis(ap=yidx[:, par, j, k:k + 1], axis=0)
                                                    ).then_inc(S(f"y_gathered{par}"), 16)

                def root(h, par):
                    pool.wait_ge(S("f_var"), h * 2 + par - R_LAST)
                    pool.tensor_tensor(rstd[:, par, :], var_eps[:, par, :], half[:], ALU.pow).then_inc(S("f_rstd"), 1)

                gather(0, 0)
                gather(0, 1)
                with pool.Fori(1, R_LAST // 2) as h:
                    gather(h, 0)
                    gather(h, 1)
                gather(R_LAST // 2, 0)
                wait_apart(pool, S, "y_stored0", 16 * ((N_ROUTED + 1) // 2))
                wait_apart(pool, S, "y_stored1", 16 * (N_ROUTED // 2))
                pool.wait_ge(S("half_made"), 1)
                h0 = R_LAST // 2
                gather_routed(h0, 1)
                with pool.Fori(h0 + 1, N_TILES // 2) as h:
                    gather_routed(h, 0)
                    root(h - 1, 1)
                    gather_routed(h, 1)
                    root(h, 0)
                gather_routed(N_TILES // 2, 0)
                root(N_TILES // 2 - 1, 1)
                root(N_TILES // 2, 0)

            @block.sync
            def _(sp):
                sp.dma_start(b1[:], a["b1"]).then_inc(S("b1_in"), 16)

                for u in range(2 * (NE + 1)):
                    sp.dma_start(wts[:, u * EW // 2:(u + 1) * EW // 2].rearrange("p (c f) -> p c f", c=2),
                                 a["w_split"][u * 2 * P:(u + 1) * 2 * P, :].rearrange("(c p) f -> p c f", p=P)
                                 ).then_inc(S("w_in"), 16)
                    if u != 0:
                        sp.wait_ge(S("w_in"), 16 * (u + 1))
                    if u % 2:
                        sp.sem_inc(S("experts_in"), 1)

                def load_shared(h, par):
                    tok = (h * 2 + par - N_ROUTED) * TT
                    wait_apart(sp, S, "tr_done", h * 2 + par - 1)
                    sp.dma_start(xg[:, par, :, :], a["xn_rows"][bass.ds(tok, TT), :].rearrange("(j p) d -> p j d", p=P)
                                 ).then_inc(S(f"rows_in{par}"), 16)

                def load_rest(h, par):
                    tok = (h * 2 + par - N_ROUTED) * TT
                    if not isinstance(h, int) or h > first(par):
                        wait_apart(sp, S, "routed_added", h * 2 + par - R_LAST - 2)
                    sp.dma_start(rs[:, par, :, :], a["resid"][bass.ds(tok, TT), :].rearrange("(j p) d -> p j d", p=P)
                                 ).then_inc(S(f"res_in{par}"), 16)

                def store(h, par):
                    tok = (h * 2 + par - N_ROUTED) * TT
                    wait_apart(sp, S, "out_ready", h * 2 + par - R_LAST)
                    sp.dma_start(a["out"][bass.ds(tok, TT), :].rearrange("(j p) d -> p j d", p=P), ob[:, par, :, :]
                                 ).then_inc(S(f"out_stored{par}"), 16)

                h0, h1 = R_LAST // 2, N_TILES // 2
                load_shared(h0, 1)
                load_rest(h0, 1)
                load_shared(h0 + 1, 0)
                load_rest(h0 + 1, 0)
                load_shared(h0 + 1, 1)
                load_shared(h0 + 2, 0)
                with sp.Fori(h0 + 1, h1 - 1) as h:
                    load_shared(h + 1, 1)
                    load_rest(h, 1)
                    store(h - 1, 1)
                    load_shared(h + 2, 0)
                    load_rest(h + 1, 0)
                    store(h, 0)
                h = h1 - 1
                load_rest(h, 1)
                store(h - 1, 1)
                load_rest(h + 1, 0)
                store(h, 0)
                store(h, 1)
                store(h + 1, 0)
                for par in range(2):
                    sp.wait_ge(S(f"out_stored{par}"), 16 * (N_SHARED // 2))

            @block.scalar
            def _(act):
                def load_ids(h, par):
                    row = act.value_load(tab[0:1, 1, bass.ds(h * 2 + par, 1)], min_val=0, max_val=N_ROWS - TT)
                    if not isinstance(h, int) or h >= 1:
                        act.wait_ge(S(f"gathered{par}"), h * 32)
                    act.dma_start(idx[:, par, :], a["table"][bass.ds(row, TT), :].rearrange("(p j) o -> p (j o)", j=2)
                                  ).then_inc(S(f"idx_loaded{par}"), 16)

                def store(h, par):
                    i = h * 2 + par
                    act.wait_ge(S("y_ready"), i + 1)
                    act.dma_start(a["y_rows"][bass.ds(i * TT, TT), :].rearrange("(p j) d -> p j d", j=2), yb[:, par, :, :]
                                  ).then_inc(S(f"y_stored{par}"), 16)

                def hidden(h, par):
                    i = h * 2 + par
                    e = act.value_load(tab[0:1, 0, bass.ds(i, 1)], min_val=0, max_val=NE)
                    if not isinstance(h, int) or h >= 1:
                        act.wait_ge(S("h_lo"), i * 2)
                        act.wait_ge(S("y_done"), i - 1)
                    elif par == 1:
                        act.wait_ge(S("h_lo"), i * 2)
                    for c in range(HC):
                        if c % 2 == 0:
                            act.wait_ge(S("h_done"), i * (HC // 2) + c // 2 + 1)
                        act.activation(hf[:, c, :], hb[c // 2][:, (c % 2) * TT:(c % 2) * TT + TT], ACT.Relu,
                                       bias=b1[:, bass.ds(e * HC + c, 1)], scale=1.0 / WS).then_inc(S("relu_done"), 1)
                        if c % (HC // 2) == HC // 2 - 1:
                            cs = slice(c + 1 - HC // 2, c + 1)
                            act.wait_ge(S("relu_done"), i * HC + c + 1)
                            act.activation(hh[:, par, 0, cs, :], hf[:, cs, :], ACT.Copy).then_inc(S("h_hi"), 1)

                act.wait_ge(S("tab_ready"), 1)
                for i in range(4):
                    load_ids(i // 2, i % 2)
                act.wait_ge(S("b1_in"), 16)
                hidden(0, 0)

                def step(h, par, i):
                    if i is None or i + 4 <= R_LAST:
                        load_ids(h + 2, par)
                    if i == R_LAST + 1:
                        store(h - 1 + par, 1 - par)
                    if i is None or i + 1 < N_TILES:
                        hidden(h + par, 1 - par)
                    if i is None or 1 <= i <= R_LAST:
                        store(h - 1 + par, 1 - par)

                tiles_of(act, step)
                act.wait_ge(S("y_stored0"), 16 * ((N_ROUTED + 1) // 2))
                act.wait_ge(S("y_stored1"), 16 * (N_ROUTED // 2))

            @block.vector
            def _(dve):
                def then(ins, name, count):
                    ins.then_inc(S(name), 1)
                    dve.wait_ge(S(name), count)

                def then_apart(ins, name, count):
                    ins.then_inc(S(name), 1)
                    wait_apart(dve, S, name, count)

                dve.memset(ones[:], 1.0).then_inc(S("ones_made"), 1)
                dve.tensor_copy(ident[:], keep["ident"][:]).then_inc(S("ones_made"), 1)
                dve.wait_ge(S("io_made"), 2)
                then(dve.tensor_copy(io_f[:], io_i[:]), "io_f_made", 1)
                then(dve.tensor_tensor(upto[:, 0], io_f[:, 0:NE].unsqueeze(2).broadcast_to([P, NE, NE]),
                                       io_f[:, 0:NE].unsqueeze(1).broadcast_to([P, NE, NE]), ALU.is_ge), "upto_made", 1)
                dve.wait_ge(S("counted"), 1)
                then(dve.tensor_copy(cum[:, 0, :], tr[0][:, 0:NE]), "tb", 1)
                then(dve.tensor_tensor(ge[:], cum[:, 0, :].unsqueeze(2).broadcast_to([P, NE, N_SHARED]),
                                       io_f[:, N_ROUTED:].unsqueeze(1).broadcast_to([P, NE, N_SHARED]), ALU.is_gt), "tb", 2)
                then(dve.tensor_reduce(cum[:, 1, :], ge[:], AX.X, ALU.add), "tb", 3)
                then(dve.tensor_tensor(upto[:, 1], upto[:, 0], cum[:, 1, :].unsqueeze(1).broadcast_to([P, NE, NE]),
                                       ALU.mult), "tb", 4)
                then(dve.tensor_reduce(cum[:, 2, :], upto[:, 1], AX.X, ALU.add), "tb", 5)
                k39 = io_f[0:1, 0:N_ROUTED]
                then(dve.tensor_tensor(past[:, 0], k39.unsqueeze(2).broadcast_to([1, N_ROUTED, NE]),
                                       cum[0:1, 2, :].unsqueeze(1).broadcast_to([1, N_ROUTED, NE]), ALU.is_ge), "tb", 6)
                dve.tensor_reduce(te[:, 0, :], past[:, 0], AX.X, ALU.add).then_inc(S("tb"), 1)
                then(dve.tensor_tensor(past[:, 1], past[:, 0],
                                       cum[0:1, 1, :].unsqueeze(1).broadcast_to([1, N_ROUTED, NE]), ALU.mult), "tb", 8)
                then(dve.tensor_reduce(te[:, 1, :], past[:, 1], AX.X, ALU.add), "tb", 9)
                then(dve.tensor_tensor(te[:, 2, :], k39, te[:, 1, :], ALU.subtract), "tb", 10)
                then(dve.tensor_scalar(te[:, 2, :], te[:, 2, :], float(TT), None, ALU.mult), "tb", 11)
                then(dve.scalar_tensor_tensor(te[:, 3, :], te[:, 0, :], float(REGION), te[:, 2, :], ALU.mult, ALU.add), "tb", 12)
                dve.tensor_copy(tab[:, 0, 0:N_ROUTED], te[:, 0, :]).then_inc(S("tb"), 1)
                dve.tensor_copy(tab[:, 1, 0:N_ROUTED], te[:, 3, :]).then_inc(S("tb"), 1)
                dve.tensor_scalar(tab[:, 0, N_ROUTED:], io_f[0:1, 0:N_SHARED], 0.0, float(SHARED),
                                  ALU.mult, ALU.add).then_inc(S("tb"), 1)
                dve.wait_ge(S("tb"), 15)
                dve.sem_inc(S("tab_ready"), 1)
                then(dve.tensor_scalar(shift[:], cum[:, 1, :], float(TT), float(-REGION), ALU.mult, ALU.add), "yr", 1)
                then(dve.tensor_copy(yrow[:, 0, :], keep["slots"][:]), "yr", 2)
                for e in range(1, NE):
                    then(dve.tensor_scalar(yrow[:, 1, :], keep["slots"][:], float(e * REGION), shift[:, e - 1:e],
                                           ALU.is_ge, ALU.mult), "yr", 1 + 2 * e)
                    then(dve.tensor_tensor(yrow[:, 0, :], yrow[:, 0, :], yrow[:, 1, :], ALU.add), "yr", 2 + 2 * e)
                then(dve.tensor_copy(keep["rows"][:], yrow[:, 0, :]), "yr", 2 * NE + 1)

                def turned(h, par):
                    dve.wait_ge(S("tr_done"), h * 2 + par + 1)
                    dve.tensor_copy(xgT[:, par].rearrange("p k t -> p (k t)"),
                                    tr[par][:, :].bitcast(F16)).then_inc(S("xgT_ready"), 1)

                def split_hidden(h, par):
                    i = h * 2 + par
                    for half in range(2):
                        cs = slice(half * HC // 2, (half + 1) * HC // 2)
                        dve.wait_ge(S("h_hi"), i * 2 + half + 1)
                        dve.tensor_tensor(hh[:, par, 1, cs, :], hf[:, cs, :], hh[:, par, 0, cs, :],
                                          ALU.subtract).then_inc(S("h_lo"), 1)

                def output(h, par):
                    i = h * 2 + par
                    dve.wait_ge(S("y_done"), i + 1)
                    if not isinstance(h, int) or h >= 1:
                        dve.wait_ge(S(f"y_stored{par}"), h * 16)
                    dve.tensor_scalar(yb[:, par].rearrange("p j d -> p (j d)"), ybank[par][:, :], 1.0 / WS, None,
                                      ALU.mult).then_inc(S("y_ready"), 1)

                def pick(h, par):
                    s = h * 2 + par - N_ROUTED
                    dve.tensor_copy(yidx[:, par, :, :].rearrange("p j k -> p (j k)"),
                                    keep["rows"][:, bass.ds(s * 2 * TOPK, 2 * TOPK)]).then_inc(S("yidx_ready"), 1)

                def add_routed(h, par):
                    n = h * 2 + par - R_LAST
                    r = h - first(par) + 1
                    dve.wait_ge(S(f"y_gathered{par}"), r * (2 * TOPK * 16))
                    dve.wait_ge(S(f"res_in{par}"), r * 16)
                    for k in range(TOPK):
                        for j in range(2):
                            w = keep["weights"][:, bass.ds((n - 1) * 2 * TOPK + j * TOPK + k, 1)]
                            dve.scalar_tensor_tensor(acc[:, par, j, :], yk[:, par, k, j, :], w,
                                                     (rs if k == 0 else acc)[:, par, j, :],
                                                     ALU.mult, ALU.add).then_inc(S("weighted"), 1)
                        dve.wait_ge(S("weighted"), n * 4 - 2 + 2 * k)
                    dve.sem_inc(S("routed_added"), 1)

                def combine(h, par):
                    i, n = h * 2 + par, h * 2 + par - R_LAST
                    dve.wait_ge(S("y_done"), i + 1)
                    flat = acc[:, par].rearrange("p j d -> p (j d)")
                    then_apart(dve.scalar_tensor_tensor(flat, ybank[par][:, :], 1.0 / WS, flat, ALU.mult, ALU.add),
                               "y_ready", i + 1)
                    for j in range(2):
                        dve.bn_stats(st[:, par, j, :], acc[:, par, j, :]).then_inc(S("f_st"), 1)
                    for j in range(2):
                        wait_apart(dve, S, "f_st", n * 2 - 1 + j)
                        dve.bn_aggr(mean_var[:, par, j, :], st[:, par, j, :]).then_inc(S("f_mv"), 1)
                    dve.wait_ge(S("f_mv"), n * 2)
                    dve.tensor_scalar(var_eps[:, par, :], mean_var[:, par, :, 1], LN_EPS, None, ALU.add).then_inc(S("f_var"), 1)

                def finish(h, par):
                    dve.wait_ge(S("f_rstd"), h * 2 + par - R_LAST)
                    if not isinstance(h, int) or h > first(par):
                        dve.wait_ge(S(f"out_stored{par}"), (h - first(par)) * 16)
                    for j in range(2):
                        ins = dve.tensor_scalar(ob[:, par, j, :], acc[:, par, j, :], mean_var[:, par, j, 0:1],
                                                rstd[:, par, j:j + 1], ALU.subtract, ALU.mult).then_inc(S("f_out"), 1)
                    dve.wait_ge(S("f_out"), (h * 2 + par - R_LAST) * 2)
                    dve.sem_inc(S("out_ready"), 1)

                def step(h, par, i):
                    if i is None or i + 2 < N_TILES:
                        turned(h + 1, par)
                    if i is None or i + 1 < N_TILES:
                        split_hidden(h + par, 1 - par)
                    if shared(i):
                        if i < N_TILES - 1:
                            pick(h + par, 1 - par)
                        add_routed(h, par)
                        if i > R_LAST + 1:
                            finish(h - 1 + par, 1 - par)
                        combine(h, par)
                    else:
                        output(h, par)
                        if i == R_LAST:
                            pick(h, 1)

                turned(0, 0)
                turned(0, 1)
                split_hidden(0, 0)
                tiles_of(dve, step)
                finish(N_TILES // 2, 0)

            @block.tensor
            def _(pe):
                pe.wait_ge(S("ones_made"), 2)
                pe.matmul(tr[0][:, 0:NE], ones[:], keep["msum"][:], start=True, stop=True).then_inc(S("counted"), 1)
                pe.wait_ge(S("tab_ready"), 1)

                def turn_rows(h, par, i):
                    if shared(i):
                        pe.wait_ge(S(f"rows_in{par}"), (h - first(par) + 1) * 16)
                    else:
                        pe.wait_ge(S(f"gathered{par}"), (h + 1) * 32)
                    if not isinstance(h, int) or h >= 1:
                        pe.wait_ge(S("xgT_ready"), h * 2 + par - 1)
                    for k in range(4):
                        for j in range(2):
                            c = (2 * k + j) * 64
                            last = pe.transpose(tr[par][:, c:c + 64].bitcast(F16), xg[:, par, j, P * k:P * k + P], ident[:])
                    last.then_inc(S("tr_done"), 1)

                PIECES = ((0, 0), (0, 1), (1, 0))

                def weights(e, chunk, w, col, n):
                    return wts[:, bass.ds(e * EW + (chunk * 2 * CH + w * CH + col), n)]

                def hidden(h, par):
                    i = h * 2 + par
                    e = pe.value_load(tab[0:1, 0, bass.ds(i, 1)], min_val=0, max_val=NE)
                    pe.wait_ge(S("experts_in"), e + 1)
                    pe.wait_ge(S("xgT_ready"), i + 1)
                    for hc in range(HC):
                        if hc % 2 == 0 and (not isinstance(h, int) or i >= 1):
                            pe.wait_ge(S("relu_done"), (i - 1) * HC + hc + 2)
                        n = 0
                        for c in range(DC):
                            for x, w in PIECES:
                                last = pe.matmul(hb[hc // 2][:, (hc % 2) * TT:(hc % 2) * TT + TT],
                                                 weights(e, c, w, hc * P, P), xgT[:, par, x * DC + c, :],
                                                 start=(n == 0), stop=(n == 5))
                                n += 1
                        if hc % 2:
                            last.then_inc(S("h_done"), 1)

                def output(h, par):
                    i = h * 2 + par
                    e = pe.value_load(tab[0:1, 0, bass.ds(i, 1)], min_val=0, max_val=NE)
                    pe.wait_ge(S("h_lo"), (i + 1) * 2)
                    if not isinstance(h, int) or h >= 1:
                        pe.wait_ge(S("y_ready"), i - 1)
                    for j in range(2):
                        n = 0
                        for hc in range(HC):
                            for x, w in PIECES:
                                last = pe.matmul(ybank[par][:, j * D:(j + 1) * D],
                                                 hh[:, par, x, hc, P * j:P * j + P],
                                                 weights(e, DC + hc * D // CH, w, hc * D % CH, D),
                                                 start=(n == 0), stop=(n == 3 * HC - 1))
                                n += 1
                    last.then_inc(S("y_done"), 1)

                turn_rows(0, 0, 0)
                turn_rows(0, 1, 1)
                hidden(0, 0)

                def step(h, par, i):
                    if i is None or i + 2 < N_TILES:
                        turn_rows(h + 1, par, None if i is None else i + 2)
                    if i is None or i + 1 < N_TILES:
                        hidden(h + par, 1 - par)
                    output(h, par)

                tiles_of(pe, step)


def layer(nc, a):
    with ExitStack() as ctx:
        named = {}

        def S(name):
            if name not in named:
                named[name] = ctx.enter_context(nc.semaphore(name))
            return named[name]

        keep = {
            "slots": ctx.enter_context(nc.sbuf_tensor("keep_slots", [P, 2 * NTILE], F32)),
            "rows": ctx.enter_context(nc.sbuf_tensor("keep_rows", [P, 2 * NTILE], I32)),
            "weights": ctx.enter_context(nc.sbuf_tensor("keep_weights", [P, 2 * NTILE], F32)),
            "msum": ctx.enter_context(nc.sbuf_tensor("keep_msum", [P, NE], F16)),
            "ident": ctx.enter_context(nc.sbuf_tensor("keep_ident", [P, P], F16)),
        }
        attention_block(nc, a, S, keep)
        expert_block(nc, a, S, keep)


def kernel(**inputs):
    import concourse.bacc as _bacc
    from concourse import mybir as _mybir
    from concourse.bass_utils import run_bass_kernel_spmd as _run

    v = {k.replace("L0_", ""): np.asarray(x) for k, x in inputs.items()}
    cat = lambda routed, shared: np.concatenate([v[routed], v[shared][None]], axis=0)
    w1 = cat("ffn_ew1", "ffn_sw1").reshape(NE + 1, DC, P, H)
    w2 = cat("ffn_ew2", "ffn_sw2").reshape(NE + 1, 2, HC // 2, P, D).transpose(0, 1, 3, 2, 4).reshape(NE + 1, 2, P, H)
    arrays = {
        "x": v["attn_x"].reshape(NTOK, D),
        "xT": v["attn_x"].transpose(0, 2, 1).reshape(NB * D, T),
        "wqkvT": v["attn_w_qkv"].T,
        "wprojT": v["attn_w_proj"].T,
        "qnw": v["attn_q_norm_w"],
        "knw": v["attn_k_norm_w"],
        "ffn_nw": v["ffn_norm_weight"],
        "routT": v["ffn_router_w"].T,
        "w_all": np.concatenate([w1, w2], axis=1).reshape(N_CHUNKS * P, H),
        "b1": cat("ffn_eb1", "ffn_sb1").reshape(NE + 1, HC, P).transpose(2, 0, 1).reshape(P, (NE + 1) * HC),
        "b2all": cat("ffn_eb2", "ffn_sb2"),
        "trig": rope_tables(),
    }
    arrays = {k: np.ascontiguousarray(x) for k, x in arrays.items()}
    nc = _bacc.Bacc("TRN2", target_bir_lowering=False, num_devices=1)
    a = {k: nc.dram_tensor("in_" + k, x.shape, _mybir.dt.from_np(x.dtype), kind="ExternalInput").ap()
         for k, x in arrays.items()}
    for name, shape, dt in (("qk_dram", (2 * DC, 2, P, T), F16), ("xn_rows", (NTOK, 2 * D), F16), ("resid", (NTOK, D), F32),
                            ("table", (N_ROWS, 1), I32), ("y_rows", (N_ROUTED * TT, D), F32), ("w_split", (N_CHUNKS * P, 2 * H), F16)):
        a[name] = nc.dram_tensor(name, shape, dt, kind="Internal").ap()
    a["out"] = nc.dram_tensor("out", (NTOK, D), F32, kind="ExternalOutput").ap()
    layer(nc, a)
    r = _run(nc, [{"in_" + k: x for k, x in arrays.items()}], core_ids=[0])
    return r.results[0]["out"].reshape(NB, T, D)
```

```python
from contextlib import ExitStack

import numpy as np

import concourse.bass as bass
from concourse import mybir

ALU = mybir.AluOpType
ACT = mybir.ActivationFunctionType
AX = mybir.AxisListType
F32 = mybir.dt.float32
F16 = mybir.dt.float16
BF16 = mybir.dt.bfloat16
I32 = mybir.dt.int32
U32 = mybir.dt.uint32

P = 128
NB, T, D = 8, 512, 256
NH, HD = 16, 16
NT = T // P
DC = D // P
NTOK = NB * T
NTILE = NTOK // P
ROPE_THETA = 32.0
RMS_EPS = 1e-6
LN_EPS = 1e-5
FFN_EPS = 1e-8
ATT_SCALE = HD ** -0.5
WS = 16.0
RS = 64.0
SEG = (0, 512, 1024, 896)
PW = 1280

NE, H = 8, 1024
HC = H // P
SHARED = NE
REGION = NTOK
TT = 256
TOPK = 2
N_SHARED = NTOK // TT
N_ROUTED = (TOPK * NTOK) // TT + NE - 1
N_TILES = N_ROUTED + N_SHARED
SPARE = NE * REGION
N_ROWS = SPARE + (NE - 1) * TT


def rope_tables():
    freqs = np.float32(ROPE_THETA) ** (-np.arange(0, HD, 2, dtype=np.float32) / np.float32(HD))
    ang = np.arange(T, dtype=np.float32)[:, None] * freqs[None, :].astype(np.float32)
    return np.stack([np.cos(ang), np.sin(ang)], axis=1).astype(np.float32)


def order(*jobs):
    by = sorted((p, k, name, t) for k, (name, pos) in enumerate(jobs) for t, p in enumerate(pos))
    return {(name, t): i for i, (_, _, name, t) in enumerate(by)}


P_QK = (1, 3, 5, 7)
P_V = (1, 8)
P_T = (5, 6, 11, 13)
P_QN = (4, 5, 9, 11)
P_NAT = (0, 2, 2, 5)
P_AT = (3, 6)
P_PROJ = (3, 7)
P_XN = (5, 11)
P_LG = (6, 11)
P_W = (7, 14)
P_RANK = (8, 14)
P_BIAS = (10, 15)
R_AFTER = (0, 0, 2, 2)
POSITIONS = 17
P_LOAD = (0, 2, 6, 8, 10, 13)
P_SPLIT = (2, 4, 6, 9, 11, 15)
P_STORE = (2, 4, 7, 9, 12, 16)
CHUNKS = len(P_LOAD)
F_QK = (2, 3, 4, 7)
F_V = (2, 8)
F_QN = (4, 6, 8, 8)
F_T = (4, 7, 8, 9)
L_NAT = (0, 1, 3, 4)
L_AT = (3, 5)
L_PROJ = (3, 8)
L_XN = (5, 10)
L_LG = (6, 10)
L_W = (7, 11)
L_RANK = (8, 11)
L_BIAS = (9, 13)
MA = order(("qk", P_QK), ("t", P_T), ("v", P_V))
MB = order(("nat", P_NAT), ("at", P_AT), ("proj", P_PROJ))
MC = order(("bias", P_BIAS), ("xn", P_XN), ("rank", P_RANK), ("lg", P_LG))
MA_FIRST = order(("qk", F_QK), ("t", F_T), ("v", F_V))
MB_LAST = order(("nat", L_NAT), ("at", L_AT), ("proj", L_PROJ))
MC_LAST = order(("bias", L_BIAS), ("xn", L_XN), ("rank", L_RANK), ("lg", L_LG))
N_MA, N_MB, N_MC = len(MA), len(MB), len(MC)


def at(positions, p):
    return [t for t in range(len(positions)) if positions[t] == p]


def wait_apart(eng, S, name, count):
    eng.wait_ge(S(name), count)
    eng.sem_inc(S("passed"), 1)


def pairs(b, u):
    return b * (NT // 2) + u + 1


def pair(u):
    return slice(2 * u, 2 * u + 2)


def tiles(b, t):
    return b * NT + t + 1


def attention_block(nc, a, S, keep):
    with ExitStack() as ctx:
        def sb(name, shape, dt):
            return ctx.enter_context(nc.sbuf_tensor(name, shape, dt))

        def ps(name, cols):
            return ctx.enter_context(nc.psum_tensor(name, [P, cols], F32))

        stage = sb("stage", [P, DC, 4 * D + NE], F32)
        chunk = stage[:, 0, 0:H]
        chunk_hl = stage[:, 1, 0:H].bitcast(F16)
        wqkv = sb("wqkv", [P, 2, DC, 3 * D], F16)
        wproj = sb("wproj", [P, 2, DC, D], F16)
        wrout = sb("wrout", [P, 2, DC, NE], F16)
        ident_f = sb("ident_f", [P, P], F32)
        ident_h = keep["ident"]
        ident_b = sb("ident_b", [P, P], BF16)
        mask_b = sb("mask_b", [P, P], BF16)
        tri_h = sb("tri_h", [P, P], F16)
        ones_h = sb("ones_h", [P, P], F16)
        iota_i = sb("iota_i", [P, 2, NE], I32)
        iota_e = sb("iota_e", [P, 2, NE], F32)
        trig = sb("trig", [P, NT, 2, HD // 2], F32)
        nw = sb("nw", [P, 2, HD], F32)
        ctab = sb("ctab", [P, NT, 2, HD], F32)
        stab = sb("stab", [P, NT, 2, HD], F32)
        ffn_nw = sb("ffn_nw", [P, D], F32)
        bias2 = sb("bias2", [NE + 1, D], F32)
        mhalf = sb("mhalf", [P, NH], F32)
        io_i = sb("io_i", [P, N_ROUTED + N_SHARED], I32)
        zeros_i = sb("zeros_i", [P, NE * REGION // P], I32)
        tokid = sb("tokid", [P, NTILE], I32)
        xTf = sb("xTf", [P, DC, T], F32)
        xTh = sb("xTh", [P, 2, DC, T], F16)
        sq = sb("sq", [P, 2 * D], F32)
        ms = sb("ms", [P, NT, 2 * NH], F32)
        rn = sb("rn", [P, NT, 2 * NH], F32)
        qk_raw = sb("qk_raw", [P, 2, 2 * D], F32)
        rot = sb("rot", [P, 2 * D], F32)
        rsum = sb("rsum", [P, 2, 2 * D], F32)
        nat = sb("nat", [P, NT, 2, 2 * D], F16)
        qkT = sb("qkT", [P, 8, T], F16)
        stk = sb("stk", [P, 2, 2, 8, T], F16)
        vst = sb("vst", [P, 2, NT, NH, 32], F32)
        prob = sb("prob", [P, 2, 4, PW], F32)
        raw = sb("raw", [P, 2, 4, T], F32)
        spent = iter(range(0, 8 * PW, PW))

        def scratch(rows, *shape):
            c = next(spent)
            n = int(np.prod(shape))
            assert n <= PW
            flat = prob[:].rearrange("p g h c -> p (g h c)")[0:rows, c:c + n]
            letters = "abc"[:len(shape)]
            return flat.rearrange(f"p ({' '.join(letters)}) -> p {' '.join(letters)}", **dict(zip(letters, shape)))

        ge = scratch(P, NE, N_SHARED)
        io_f = scratch(P, N_ROUTED + N_SHARED)
        cum = scratch(P, 3, NE)
        upto = scratch(P, 2, NE, NE)
        past = scratch(1, 2, N_ROUTED, NE)
        te = scratch(1, 4, N_ROUTED)
        xin = sb("xin", [P, NT, D], F32)
        rcp = sb("rcp", [P, NT, NH], F32)
        an = sb("an", [P, 2, D], F32)
        anh = sb("anh", [P, NT, 2, D], F16)
        aT = sb("aT", [P, 2, 2, 4, P], F16)
        y0 = sb("y0", [P, NT, D], F32)
        st6 = sb("st6", [P, NT, 6], F32)
        mv = sb("mv", [P, NT, 2], F32)
        vv = sb("vv", [P, NT, 6], F32)
        x1 = sb("x1", [P, NT, D], F32)
        xnf = sb("xnf", [P, 2, D], F32)
        xnh = sb("xnh", [P, NT, 2, D], F16)
        xnT = sb("xnT", [P, 2, 2, 4, P], F16)
        lg = sb("lg", [P, NT, NE], F32)
        mx = sb("mx", [P, NT, 8], F32)
        ix = sb("ix", [P, NT, 8], U32)
        ixf = sb("ixf", [P, NT, 2], F32)
        oh = sb("oh", [P, NT, 2, NE], F32)
        mh = sb("mh", [P, NT, NE], F16)
        msum = keep["msum"]
        ex = sb("ex", [P, NT, 2], F32)
        pr = sb("pr", [P, NT, 2], F32)
        pr1 = sb("pr1", [P, NT, 2], F32)
        tot = sb("tot", [P, NT, 2], F32)
        wt = sb("wt", [P, NT, 2], F32)
        comb = sb("comb", [P, NT, NE + 1], F32)
        cw = sb("cw", [P, NT, 2, NE], F32)
        combT = sb("combT", [NE + 1, NT, P], F32)
        sl = sb("sl", [P, NT, NE], F32)
        slm = sb("slm", [P, NT, 2, NE], F32)
        slf = sb("slf", [P, NT, 2], F32)
        sl_i = sb("sl_i", [P, NT, 2], I32)
        tok_i = sb("tok_i", [P, NT], I32)
        res = sb("res", [P, NT, D], F32)

        slots = (ps("slot0", 1024), ps("slot1", 1024))
        pv_bank = ps("pv_bank", T)
        ma = ps("ma", T)
        mb = ps("mb", T)
        mc = ps("mc", T)

        def turns(eng, turn):
            turn(-1, 1, True, False, False)
            turn(0, 0, True, True, False)
            with eng.Fori(0, (NB - 2) // 2) as it:
                turn(it * 2 + 1, 1, True, True, True)
                turn(it * 2 + 2, 0, True, True, True)
            turn(NB - 1, 1, False, True, True)
            turn(NB, 0, False, False, True)

        with nc.Block() as block:
            @block.sync
            def _(sp):
                w = 3 * D
                def load_weights(lo, hi, src):
                    sp.dma_start(stage[:, :, lo:hi], a[src].rearrange("(c p) n -> p c n", p=P)).then_inc(S("w_loaded"), 16)

                def load_xT(b):
                    sp.dma_start(xTf[:], a["xT"][bass.ds(b * D, D), :].rearrange("(c p) t -> p c t", p=P)
                                 ).then_inc(S("xT_loaded"), 16)

                load_weights(0, w, "wqkvT")
                sp.dma_start(trig[:], a["trig"].rearrange("(t p) s f -> p t s f", p=P)).then_inc(S("rope_loaded"), 16)
                sp.dma_start(nw[:, 0, :], a["qnw"].partition_broadcast(P)).then_inc(S("rope_loaded"), 16)
                sp.dma_start(nw[:, 1, :], a["knw"].partition_broadcast(P)).then_inc(S("rope_loaded"), 16)
                load_weights(w, w + D, "wprojT")
                load_weights(w + D, w + D + NE, "routT")
                load_xT(0)
                sp.dma_start(ffn_nw[:], a["ffn_nw"].partition_broadcast(P)).then_inc(S("c_loaded"), 16)
                sp.dma_start(bias2[:], a["b2all"]).then_inc(S("c_loaded"), 16)
                sp.wait_ge(S("const_ready"), 1)
                sp.dma_start(a["table"][0:SPARE, :].rearrange("(p c) o -> p (c o)", p=P),
                             zeros_i[:, :]).then_inc(S("table_init"), 16)
                sp.dma_start(a["table"][SPARE:N_ROWS, :].rearrange("(p c) o -> p (c o)", p=P),
                             zeros_i[:, 0:(N_ROWS - SPARE) // P]).then_inc(S("table_init"), 16)

                def turn(b, par, front, attend, back):
                    order_a, order_b, order_c = (MA, MB, MC) if attend else (MA_FIRST, MB_LAST, MC_LAST)
                    for p in range(POSITIONS):
                        if p == 1 and front and not (isinstance(b, int) and b + 2 >= NB):
                            wait_apart(sp, S, "xT_split", b + 2)
                            load_xT((b + 2) % NB)
                        for j in at(P_STORE, p):
                            if front and back:
                                k = (b - 1) * CHUNKS + j
                                wait_apart(sp, S, "chunk_lo", k + 1)
                                sp.dma_start(a["w_split"][bass.ds(k * P, P), :], chunk_hl).then_inc(S("chunk_stored"), 16)
                                sp.wait_ge(S("chunk_stored"), (k + 1) * 16)
                                sp.sem_inc(S("chunk_free"), 1)
                        for j in at(P_LOAD, p):
                            if front and back:
                                k = (b - 1) * CHUNKS + j
                                wait_apart(sp, S, "chunk_free", k + 1)
                                sp.dma_start(chunk, a["w_all"][bass.ds(k * P, P), :]).then_inc(S("chunk_in"), 16)
                        for u in at(P_BIAS if attend else L_BIAS, p):
                            if back:
                                wait_apart(sp, S, "res_ready", pairs(b - 1, u))
                                sp.dma_start(a["resid"][bass.ds((b - 1) * T + u * 2 * P, 2 * P), :]
                                             .rearrange("(t p) d -> p t d", p=P),
                                             res[:, pair(u), :]).then_inc(S("res_stored"), 16)
                        for u in at(P_XN if attend else L_XN, p):
                            if back:
                                wait_apart(sp, S, "xn_lo", pairs(b - 1, u))
                                sp.dma_start(a["xn_rows"][bass.ds((b - 1) * T + u * 2 * P, 2 * P), :]
                                             .rearrange("(t p) d -> p t d", p=P),
                                             xnh[:, pair(u), :, :].rearrange("p t h d -> p t (h d)")
                                             ).then_inc(S("xn_stored"), 16)
                        for t in at(P_T if attend else F_T, p):
                            if front and t % 2:
                                h0 = (t - 1) * P
                                half = slice(h0, h0 + 2 * P)
                                sp.wait_ge(S("ma_free"), (b + 1) * N_MA + order_a["t", t] + 2)
                                sp.dma_start(a["qk_dram"][:, :, :, half].rearrange("k s p t -> p (k s) t"),
                                             qkT[:, :, half]).then_inc(S("qk_out"), 16)
                                sp.wait_ge(S("qk_out"), ((b + 1) * 2 + (t // 2) + 1) * 16)
                                for cc in range(DC):
                                    for qk, r, hl, n in ((0, 0, 0, 2), (1, 0, 0, 2), (1, 2, 0, 2), (0, 2, 1, 1), (0, 3, 0, 1)):
                                        row = 64 * cc + HD * r
                                        k = qk * DC + cc
                                        sp.dma_start(
                                            stk[row:row + HD * n, 1 - par, qk, :, half],
                                            a["qk_dram"][k, hl:hl + n, :, half]
                                            .rearrange("s (d i) t -> (s d) i t", d=HD)).then_inc(S(f"stk_in{cc}"), 16)
                    if attend:
                        if back:
                            wait_apart(sp, S, "y0_done", b * NT)
                        sp.dma_start(xin[:], a["x"][bass.ds(b * T, T), :].rearrange("(t p) d -> p t d", p=P)
                                     ).then_inc(S("xin_loaded"), 16)
                    if back:
                        sp.wait_ge(S("xn_stored"), b * (NT // 2 * 16))
                        sp.wait_ge(S("res_stored"), b * (NT // 2 * 16))
                    sp.sem_inc(S("stores_out"), 1)

                turns(sp, turn)
                for cc in range(DC):
                    sp.wait_ge(S(f"stk_in{cc}"), 16 * 10 * NB)
                sp.wait_ge(S("xT_loaded"), 16 * (NB + 1))
                sp.wait_ge(S("chunk_stored"), 16 * N_CHUNKS)

            @block.gpsimd
            def _(pool):
                pool.memset(ident_f[:], 0.0).then_inc(S("made"), 1)
                pool.memset(mask_b[:], 0.0).then_inc(S("made"), 1)
                pool.memset(tri_h[:], 1.0).then_inc(S("made"), 1)
                pool.memset(zeros_i[:], 0).then_inc(S("made"), 1)
                pool.iota(tokid[:], pattern=[[P, NTILE]], base=0, channel_multiplier=1).then_inc(S("made"), 1)
                pool.memset(mhalf[:], -0.5).then_inc(S("made"), 1)
                pool.iota(iota_i[:, 0, :], pattern=[[1, NE]], base=0, channel_multiplier=0).then_inc(S("made"), 1)
                pool.iota(iota_i[:, 1, :], pattern=[[REGION, NE]], base=0, channel_multiplier=0).then_inc(S("made"), 1)
                pool.memset(ones_h[:], 1.0).then_inc(S("made"), 1)
                pool.iota(io_i[:, 0:N_ROUTED], pattern=[[1, N_ROUTED]], base=0, channel_multiplier=0).then_inc(S("made"), 1)
                pool.iota(io_i[:, N_ROUTED:], pattern=[[TT, N_SHARED]], base=0, channel_multiplier=0).then_inc(S("made"), 1)
                pool.wait_ge(S("made"), 11)
                pool.affine_select(out=ident_f[:], in_=ident_f[:], compare_op=ALU.not_equal, fill=1.0, base=0,
                                   pattern=[[-1, P]], channel_multiplier=1).then_inc(S("made"), 1)
                pool.affine_select(out=mask_b[:], in_=mask_b[:], compare_op=ALU.is_ge, fill=-1e30, base=0,
                                   pattern=[[1, P]], channel_multiplier=-1).then_inc(S("made"), 1)
                pool.affine_select(out=tri_h[:], in_=tri_h[:], compare_op=ALU.is_gt, fill=0.0, base=0,
                                   pattern=[[1, P]], channel_multiplier=-1).then_inc(S("made"), 1)
                pool.wait_ge(S("made"), 14)
                pool.tensor_copy(ident_h[:], ident_f[:]).then_inc(S("made"), 1)
                pool.tensor_copy(ident_b[:], ident_f[:]).then_inc(S("made"), 1)
                pool.wait_ge(S("made"), 16)
                pool.sem_inc(S("const_ready"), 1)
                pool.wait_ge(S("table_init"), 32)

                def turn(b, par, front, attend, back):
                    order_a, order_b, order_c = (MA, MB, MC) if attend else (MA_FIRST, MB_LAST, MC_LAST)
                    for p in range(POSITIONS):
                        for t in range(NT):
                            for q in range(4):
                                if front and p == (P_QK[t] + R_AFTER[q] if attend else F_QK[t]):
                                    pool.wait_ge(S("ms_ready"), tiles(b + 1, t))
                                    h = slice(q * NH // 2, (q + 1) * NH // 2)
                                    pool.tensor_tensor(rn[:, t, h], ms[:, t, h], mhalf[:, 0:NH // 2],
                                                       ALU.pow).then_inc(S("rn_ready"), 1)
                        for u in at(P_PROJ if attend else L_PROJ, p):
                            if back:
                                k = pairs(b - 1, u)
                                v = [vv[:, pair(u), c] for c in range(6)]
                                pool.wait_ge(S("var_ready"), k)
                                pool.tensor_tensor(v[1], v[0], mhalf[:, 0:2], ALU.pow).then_inc(S("rstd"), 1)
                                pool.wait_ge(S("rstd"), k)
                                pool.tensor_tensor(v[2], v[1], v[1], ALU.mult).then_inc(S("rstd_sq"), 1)
                                pool.wait_ge(S("rstd_sq"), k)
                                pool.tensor_tensor(v[3], v[2], mv[:, pair(u), 1], ALU.mult).then_inc(S("msq"), 1)
                                wait_apart(pool, S, "msq", k)
                                pool.tensor_scalar(v[4], v[3], FFN_EPS, None, ALU.add).then_inc(S("msq_eps"), 1)
                                pool.wait_ge(S("msq_eps"), k)
                                pool.tensor_tensor(v[5], v[4], mhalf[:, 0:2], ALU.pow).then_inc(S("norms_ready"), 1)
                        for u in at(P_BIAS if attend else L_BIAS, p):
                            if back:
                                wait_apart(pool, S, "slots_ready", pairs(b - 1, u))
                                for t in range(2 * u, 2 * u + 2):
                                    for k in range(TOPK):
                                        pool.indirect_dma_start(
                                            a["table"], bass.IndirectOffsetOnAxis(ap=sl_i[:, t, k:k + 1], axis=0),
                                            tok_i[:, t:t + 1], None).then_inc(S("scattered"), 16)
                    if back:
                        pool.wait_ge(S("scattered"), b * (NT * TOPK * 16))
                    pool.sem_inc(S("ids_out"), 1)

                turns(pool, turn)

            @block.scalar
            def _(act):
                act.wait_ge(S("w_loaded"), 16 * 3)
                w = 3 * D
                act.activation(wqkv[:, 0, :, :], stage[:, :, 0:w], ACT.Copy, scale=WS).then_inc(S("w_hi"), 1)
                act.activation(wproj[:, 0, :, :], stage[:, :, w:w + D], ACT.Copy, scale=WS).then_inc(S("w_hi"), 1)
                act.activation(wrout[:, 0, :, :], stage[:, :, w + D:], ACT.Copy, scale=RS).then_inc(S("w_hi"), 1)
                act.wait_ge(S("vst_one"), 1)

                def attended(b, par, p):
                    g = p // 4
                    s = b * 4 + g
                    act.wait_ge(S("pv_done"), s)
                    act.activation(raw[:, (1 - par) if p == 0 else par, (g - 1) % 4, :], pv_bank[:, :],
                                   ACT.Copy).then_inc(S("raw_done"), 1)

                def turn(b, par, front, attend, back):
                    order_a, order_b, order_c = (MA, MB, MC) if attend else (MA_FIRST, MB_LAST, MC_LAST)
                    if front:
                        act.wait_ge(S("xT_loaded"), (b + 2) * 16)
                        if not isinstance(b, int) or b >= 0:
                            act.wait_ge(S("v_done"), pairs(b, 1))
                        act.activation(xTh[:, 0, :, :], xTf[:, :, :], ACT.Copy).then_inc(S("xT_hi"), 1)
                    for p in range(POSITIONS):
                        g = p // 4
                        if p == 0 and back:
                            attended(b, par, 0)
                        if attend and p < 16:
                            for u in ((0, 1), (2,), (3,), (4, 5))[p % 4]:
                                act.wait_ge(S("unit_ready"), b * 24 + g * 6 + u + 1)
                                if u == 0 and (not isinstance(b, int) or b * 4 + g >= 2):
                                    act.wait_ge(S("pv_done"), b * 4 + g - 1)
                                slot = slots[u % 2]
                                pp = prob[:, g % 2]
                                if u in (2, 5):
                                    r = 0 if u == 2 else 2
                                    act.activation(pp[:, r:r + 2, 1024:PW],
                                                   slot[:, 0:512].rearrange("p (r q) -> p r q", r=2),
                                                   ACT.Exp, scale=ATT_SCALE).then_inc(S("exp_done"), 1)
                                else:
                                    r = (0, 1, None, 2, 3)[u]
                                    act.activation(pp[:, r, 0:1024], slot[:, 0:1024], ACT.Exp,
                                                   scale=ATT_SCALE).then_inc(S("exp_done"), 1)
                        if 0 < p < 16 and p % 4 == 0 and attend:
                            attended(b, par, p)
                        for t in at(P_QK if attend else F_QK, p):
                            if front:
                                k = tiles(b + 1, t)
                                act.wait_ge(S("qk_done"), k)
                                if not isinstance(b, int) or k > 2:
                                    act.wait_ge(S("rot_done"), (k - 2) * 3)
                                act.activation(qk_raw[:, t % 2, :], ma[:, :], ACT.Copy).then_inc(S("ma_free"), 1)
                                if not isinstance(b, int) or k > 1:
                                    act.wait_ge(S("ss_done"), k - 1)
                                act.wait_ge(S("ma_free"), (b + 1) * N_MA + order_a["qk", t] + 2)
                                act.activation(sq[:], qk_raw[:, t % 2, :], ACT.Square).then_inc(S("sq_ready"), 1)
                        for t in at(P_T if attend else F_T, p):
                            if front:
                                act.wait_ge(S("t_done"), tiles(b + 1, t))
                                act.activation(qkT[:, :, t * P:(t + 1) * P],
                                               ma[:, :].bitcast(F16).rearrange("p (k t) -> p k t", k=8),
                                               ACT.Copy).then_inc(S("ma_free"), 1)
                        for u in at(P_V if attend else F_V, p):
                            if front:
                                act.wait_ge(S("v_done"), pairs(b + 1, u))
                                act.activation(vst[:, 1 - par, pair(u), :, 0:HD],
                                               ma[:, :].rearrange("p (t h d) -> p t h d", t=2, d=HD), ACT.Copy,
                                               scale=1.0 / WS).then_inc(S("ma_free"), 1)
                        for u in at(P_AT if attend else L_AT, p):
                            if back:
                                act.wait_ge(S("at_done"), pairs(b - 1, u))
                                act.activation(aT[:, u].rearrange("p t k q -> p (t k q)"),
                                               mb[:, :].bitcast(F16), ACT.Copy).then_inc(S("mb_free"), 1)
                        for u in at(P_XN if attend else L_XN, p):
                            if back:
                                act.wait_ge(S("xnT_done"), pairs(b - 1, u))
                                act.activation(xnT[:, u].rearrange("p t k q -> p (t k q)"),
                                               mc[:, :].bitcast(F16), ACT.Copy).then_inc(S("mc_free"), 1)
                        for u in at(P_LG if attend else L_LG, p):
                            if back:
                                act.wait_ge(S("top_ready"), tiles(b - 1, 2 * u + 1))
                                act.activation(ex[:, pair(u), :], mx[:, pair(u), 0:2], ACT.Exp, scale=-1.0).then_inc(S("ex_ready"), 1)
                        for j in at(P_SPLIT, p):
                            if front and back:
                                k = (b - 1) * CHUNKS + j
                                act.wait_ge(S("chunk_in"), (k + 1) * 16)
                                act.activation(chunk_hl[:, 0:H], chunk, ACT.Copy, scale=WS).then_inc(S("chunk_hi"), 1)

                turns(act, turn)

            @block.vector
            def _(dve):
                def then(ins, name, count):
                    ins.then_inc(S(name), 1)
                    dve.wait_ge(S(name), count)

                def then_apart(ins, name, count):
                    ins.then_inc(S(name), 1)
                    wait_apart(dve, S, name, count)

                for bank in ("ma_free", "mb_free", "mc_free"):
                    dve.sem_inc(S(bank), 1)
                dve.memset(vst[:].rearrange("p a t h d -> p (a t h d)"), 0.0).then_inc(S("vst_zero"), 1)
                dve.memset(comb[:], 1.0).then_inc(S("vst_zero"), 1)
                dve.memset(msum[:], 0.0).then_inc(S("msum_free"), 1)
                dve.wait_ge(S("vst_zero"), 2)
                dve.memset(vst[:].rearrange("p a t h d -> p (a t h) d")[:, :, HD:HD + 1], 1.0).then_inc(S("vst_one"), 1)
                hh = HD // 2
                dve.wait_ge(S("rope_loaded"), 48)
                hh = HD // 2
                for qk in range(2):
                    for half in range(2):
                        here = slice(half * hh, half * hh + hh)
                        other = slice(hh - half * hh, HD - half * hh)
                        wb = nw[:, qk, here].unsqueeze(1).broadcast_to([P, NT, hh])
                        wo = nw[:, qk, other].unsqueeze(1).broadcast_to([P, NT, hh])
                        dve.scalar_tensor_tensor(ctab[:, :, qk, here], trig[:, :, 0, :], 1.0 / WS, wb,
                                                 ALU.mult, ALU.mult).then_inc(S("rope_made"), 1)
                        dve.scalar_tensor_tensor(stab[:, :, qk, here], trig[:, :, 1, :], (2 * half - 1) / WS, wo,
                                                 ALU.mult, ALU.mult).then_inc(S("rope_made"), 1)
                dve.wait_ge(S("w_hi"), 3)
                w = 3 * D
                for k, (dst, lo, hi, scale) in enumerate(((wqkv, 0, w, WS), (wproj, w, w + D, WS),
                                                          (wrout, w + D, w + D + NE, RS))):
                    dve.scalar_tensor_tensor(dst[:, 1, :, :], stage[:, :, lo:hi], scale, dst[:, 0, :, :],
                                             ALU.mult, ALU.subtract).then_inc(S("w_lo"), 1)
                dve.wait_ge(S("const_ready"), 1)
                dve.tensor_copy(iota_e[:], iota_i[:]).then_inc(S("vst_one"), 1)
                dve.wait_ge(S("c_loaded"), 32)
                dve.wait_ge(S("rope_made"), 8)
                dve.wait_ge(S("vst_one"), 2)
                dve.wait_ge(S("w_lo"), 3)
                dve.sem_inc(S("tables_ready"), 1)
                dve.sem_inc(S("chunk_free"), 1)

                def turn(b, par, front, attend, back):
                    order_a, order_b, order_c = (MA, MB, MC) if attend else (MA_FIRST, MB_LAST, MC_LAST)
                    if front:
                        dve.wait_ge(S("xT_hi"), b + 2)
                        dve.tensor_tensor(xTh[:, 1, :, :], xTf[:, :, :], xTh[:, 0, :, :],
                                          ALU.subtract).then_inc(S("xT_split"), 1)
                    for p in range(POSITIONS):
                        for u in at(P_XN if attend else L_XN, p):
                            if back:
                                k = pairs(b - 1, u)
                                dve.wait_ge(S("norms_ready"), k)
                                for t in range(2 * u, 2 * u + 2):
                                    dve.tensor_scalar(x1[:, t, :], y0[:, t, :], mv[:, t, 0:1], vv[:, t, 1:2],
                                                      ALU.subtract, ALU.mult).then_inc(S("x1_done"), 1)
                                for t in range(2 * u, 2 * u + 2):
                                    dve.wait_ge(S("x1_done"), tiles(b - 1, t))
                                    dve.scalar_tensor_tensor(xnf[:, t % 2, :], x1[:, t, :], vv[:, t, 5:6], ffn_nw[:],
                                                             ALU.mult, ALU.mult).then_inc(S("xnf_done"), 1)
                                dve.wait_ge(S("xnf_done"), tiles(b - 1, 2 * u + 1))
                                dve.wait_ge(S("stores_out"), b + 1)
                                then(dve.tensor_copy(xnh[:, pair(u), 0, :], xnf[:]), "xn_hi", k)
                                then(dve.tensor_tensor(xnh[:, pair(u), 1, :], xnf[:], xnh[:, pair(u), 0, :],
                                                       ALU.subtract), "xn_lo", k)
                        for u in at(P_W if attend else L_W, p):
                            if back:
                                k = pairs(b - 1, u)
                                q = pair(u)
                                dve.wait_ge(S("ex_ready"), k)
                                then(dve.tensor_scalar(pr1[:, q, :], ex[:, q, :], 1.0, None, ALU.add), "sig_den", k)
                                then(dve.reciprocal(pr[:, q, :], pr1[:, q, :]), "sig", k)
                                then(dve.scalar_tensor_tensor(tot[:, q, 0:1], pr[:, q, 0:1], 1e-6, pr[:, q, 1:2],
                                                              ALU.add, ALU.add), "sig_sum", k)
                                then(dve.reciprocal(tot[:, q, 1:2], tot[:, q, 0:1]), "sig_rcp", k)
                                then(dve.tensor_tensor(wt[:, q, :], pr[:, q, :], tot[:, q, 1:2].broadcast_to([P, 2, 2]),
                                                       ALU.mult), "wt_done", k)
                                dve.tensor_copy(keep["weights"][:, bass.ds(((b - 1) * NT + 2 * u) * 2, 4)],
                                                wt[:, q, :].rearrange("p t k -> p (t k)")).then_inc(S("kept"), 1)
                                then(dve.tensor_tensor(cw[:, q].rearrange("p t k e -> p (t k) e"),
                                                       oh[:, q].rearrange("p t k e -> p (t k) e"),
                                                       wt[:, q, :].rearrange("p t k -> p (t k)").unsqueeze(2)
                                                       .broadcast_to([P, 4, NE]), ALU.mult), "cw_done", k)
                                dve.tensor_tensor(comb[:, q, 0:NE], cw[:, q, 0, :], cw[:, q, 1, :],
                                                  ALU.add).then_inc(S("comb_ready"), 1)
                        for t in at(P_QN if attend else F_QN, p):
                            if front:
                                k = tiles(b + 1, t)
                                dve.wait_ge(S("rn_ready"), k * 4)
                                then(dve.tensor_tensor(rot[:].rearrange("p (c d i) -> p c i d", c=2 * DC, d=HD),
                                                       rsum[:, t % 2, :].rearrange("p (c i d) -> p c i d", c=2 * DC, d=HD),
                                                       rn[:, t, :].rearrange("p (c i) -> p c i", c=2 * DC).unsqueeze(3)
                                                       .broadcast_to([P, 2 * DC, NH // DC, HD]), ALU.mult), "qn_done", k)
                                then(dve.tensor_copy(nat[:, t, 0, :], rot[:]), "nat_hi", k)
                                then(dve.tensor_tensor(nat[:, t, 1, :], rot[:], nat[:, t, 0, :],
                                                       ALU.subtract), "nat_ready", k)
                        for t in at(P_NAT if attend else L_NAT, p):
                            if back:
                                k = tiles(b - 1, t)
                                dve.wait_ge(S("nat_done"), k)
                                o3 = mb[:, :].rearrange("p (h d) -> p h d", d=32)
                                then(dve.reciprocal(rcp[:, t, :], o3[:, :, HD]), "rcp_done", k)
                                dve.tensor_tensor(an[:, t % 2, :].rearrange("p (h d) -> p h d", d=HD), o3[:, :, 0:HD],
                                                  rcp[:, t, :].unsqueeze(2).broadcast_to([P, NH, HD]),
                                                  ALU.mult).then_inc(S("mb_free"), 1)
                                dve.wait_ge(S("mb_free"), (b - 1) * N_MB + order_b["nat", t] + 2)
                                if t % 2:
                                    u = t // 2
                                    k = pairs(b - 1, u)
                                    then(dve.tensor_copy(anh[:, pair(u), 0, :], an[:]), "an_hi", k)
                                    then(dve.tensor_tensor(anh[:, pair(u), 1, :], an[:], anh[:, pair(u), 0, :],
                                                           ALU.subtract), "an_ready", k)
                        for u in at(P_LG if attend else L_LG, p):
                            if back:
                                k = pairs(b - 1, u)
                                q = pair(u)
                                dve.wait_ge(S("lg_done"), k)
                                dve.tensor_scalar(lg[:, q, :], mc[:, 0:2 * NE].rearrange("p (t e) -> p t e", t=2), 1.0 / RS,
                                                  None, ALU.mult).then_inc(S("mc_free"), 1)
                                wait_apart(dve, S, "mc_free", (b - 1) * N_MC + order_c["lg", u] + 2)
                                for t in range(2 * u, 2 * u + 2):
                                    dve.max(mx[:, t, :], lg[:, t, :]).then_inc(S("top_ready"), 1)
                                for t in range(2 * u, 2 * u + 2):
                                    wait_apart(dve, S, "top_ready", tiles(b - 1, t))
                                    dve.max_index(ix[:, t, :], mx[:, t, :], lg[:, t, :]).then_inc(S("ix_done"), 1)
                                dve.wait_ge(S("ix_done"), tiles(b - 1, 2 * u + 1))
                                then(dve.tensor_copy(ixf[:, q, :], ix[:, q, 0:2]), "ixf_done", k)
                                then(dve.tensor_tensor(oh[:, q].rearrange("p t k e -> p (t k) e"),
                                                       iota_e[:, 0, :].unsqueeze(1).broadcast_to([P, 4, NE]),
                                                       ixf[:, q, :].rearrange("p t k -> p (t k)").unsqueeze(2)
                                                       .broadcast_to([P, 4, NE]), ALU.is_equal), "oh_done", k)
                                dve.tensor_tensor(mh[:, q, :], oh[:, q, 0, :], oh[:, q, 1, :], ALU.add).then_inc(S("mh_ready"), 1)
                        for t in at(P_QK if attend else F_QK, p):
                            if front:
                                k = tiles(b + 1, t)
                                dve.wait_ge(S("ma_free"), (b + 1) * N_MA + order_a["qk", t] + 2)
                                q4 = qk_raw[:, t % 2, :].rearrange("p (k h d) -> p k h d", k=2, d=HD)
                                r0 = rot[:].rearrange("p (k h d) -> p k h d", k=2, d=HD)
                                r1 = rsum[:, t % 2, :].rearrange("p (k h d) -> p k h d", k=2, d=HD)
                                dve.tensor_tensor(r0, q4, ctab[:, t].unsqueeze(2).broadcast_to([P, 2, NH, HD]),
                                                  ALU.mult).then_inc(S("rot_done"), 1)
                                dve.tensor_tensor(r1[:, :, :, 0:hh], q4[:, :, :, hh:HD],
                                                  stab[:, t, :, 0:hh].unsqueeze(2).broadcast_to([P, 2, NH, hh]),
                                                  ALU.mult).then_inc(S("rot_done"), 1)
                                dve.tensor_tensor(r1[:, :, :, hh:HD], q4[:, :, :, 0:hh],
                                                  stab[:, t, :, hh:HD].unsqueeze(2).broadcast_to([P, 2, NH, hh]),
                                                  ALU.mult).then_inc(S("rot_done"), 1)
                                dve.wait_ge(S("sq_ready"), k)
                                then(dve.tensor_reduce(ms[:, t, :], sq[:].rearrange("p (h d) -> p h d", d=HD),
                                                       AX.X, ALU.add), "ss_done", k)
                                dve.tensor_scalar(ms[:, t, :], ms[:, t, :], 1.0 / (HD * WS * WS), RMS_EPS,
                                                  ALU.mult, ALU.add).then_inc(S("ms_ready"), 1)
                                dve.wait_ge(S("rot_done"), k * 3)
                                then(dve.tensor_tensor(rsum[:, t % 2, :], rot[:], rsum[:, t % 2, :], ALU.add), "rsum_done", k)
                        for u in at(P_PROJ if attend else L_PROJ, p):
                            if back:
                                dve.wait_ge(S("proj_done"), pairs(b - 1, u))
                                dve.wait_ge(S("xin_loaded"), b * 16)
                                dve.scalar_tensor_tensor(y0[:, pair(u), :].rearrange("p t d -> p (t d)"), mb[:, :], 1.0 / WS,
                                                         xin[:, pair(u), :].rearrange("p t d -> p (t d)"),
                                                         ALU.mult, ALU.add).then_inc(S("mb_free"), 1)
                                dve.wait_ge(S("mb_free"), (b - 1) * N_MB + order_b["proj", u] + 2)
                                for t in range(2 * u, 2 * u + 2):
                                    dve.bn_stats(st6[:, t, :], y0[:, t, :]).then_inc(S("y0_done"), 1)
                                for t in range(2 * u, 2 * u + 2):
                                    wait_apart(dve, S, "y0_done", tiles(b - 1, t))
                                    dve.bn_aggr(mv[:, t, :], st6[:, t, :]).then_inc(S("mv_done"), 1)
                                dve.wait_ge(S("mv_done"), tiles(b - 1, 2 * u + 1))
                                dve.tensor_scalar(vv[:, pair(u), 0], mv[:, pair(u), 1], LN_EPS, None,
                                                  ALU.add).then_inc(S("var_ready"), 1)
                        for u in at(P_RANK if attend else L_RANK, p):
                            if back:
                                k = pairs(b - 1, u)
                                q = pair(u)
                                dve.wait_ge(S("rank_done"), k)
                                dve.tensor_tensor(sl[:, q, :], mc[:, 0:2 * NE].rearrange("p (t e) -> p t e", t=2),
                                                  iota_e[:, 1, :].unsqueeze(1).broadcast_to([P, 2, NE]), ALU.add
                                                  ).then_inc(S("sl_done"), 1)
                                dve.tensor_copy(combT[:, q, :], mc[0:NE + 1, P:3 * P].rearrange("p (t q) -> p t q", t=2)
                                                ).then_inc(S("mc_free"), 1)
                                for t in range(2 * u, 2 * u + 2):
                                    dve.wait_ge(S("msum_free"), tiles(b - 1, t))
                                    dve.tensor_tensor(msum[:], msum[:], mh[:, t, :], ALU.add).then_inc(S("msum_free"), 1)
                                dve.wait_ge(S("sl_done"), k)
                                for t in range(2 * u, 2 * u + 2):
                                    dve.tensor_tensor(slm[:, t, :, :], oh[:, t, :, :],
                                                      sl[:, t, :].unsqueeze(1).broadcast_to([P, 2, NE]),
                                                      ALU.mult).then_inc(S("slm_done"), 1)
                                dve.wait_ge(S("slm_done"), tiles(b - 1, 2 * u + 1))
                                then(dve.tensor_reduce(slf[:, q, :], slm[:, q, :, :], AX.X, ALU.add), "slf_done", k)
                                dve.tensor_copy(keep["slots"][:, bass.ds(((b - 1) * NT + 2 * u) * 2, 4)],
                                                slf[:, q, :].rearrange("p t k -> p (t k)")).then_inc(S("kept"), 1)
                                dve.wait_ge(S("ids_out"), b + 1)
                                dve.tensor_copy(tok_i[:, q], tokid[:, bass.ds((b - 1) * NT + 2 * u, 2)]
                                                ).then_inc(S("tok_ready"), 1)
                                dve.wait_ge(S("tok_ready"), k)
                                dve.tensor_copy(sl_i[:, q, :], slf[:, q, :]).then_inc(S("slots_ready"), 1)
                        for u in at(P_BIAS if attend else L_BIAS, p):
                            if back:
                                dve.wait_ge(S("bias_done"), pairs(b - 1, u))
                                dve.tensor_tensor(res[:, pair(u), :].rearrange("p t d -> p (t d)"), mc[:, :],
                                                  x1[:, pair(u), :].rearrange("p t d -> p (t d)"), ALU.add
                                                  ).then_inc(S("mc_free"), 1)
                                dve.wait_ge(S("mc_free"), (b - 1) * N_MC + order_c["bias", u] + 2)
                                dve.sem_inc(S("res_ready"), 1)
                        for j in at(P_SPLIT, p):
                            if front and back:
                                k = (b - 1) * CHUNKS + j
                                dve.wait_ge(S("chunk_hi"), k + 1)
                                dve.scalar_tensor_tensor(chunk_hl[:, H:2 * H], chunk, WS, chunk_hl[:, 0:H],
                                                         ALU.mult, ALU.subtract).then_inc(S("chunk_lo"), 1)

                turns(dve, turn)
                dve.wait_ge(S("pv_done"), 4 * NB)
                then(dve.tensor_copy(io_f, io_i[:]), "io_f_made", 1)
                then(dve.tensor_tensor(upto[:, 0], io_f[:, 0:NE].unsqueeze(2).broadcast_to([P, NE, NE]),
                                       io_f[:, 0:NE].unsqueeze(1).broadcast_to([P, NE, NE]), ALU.is_ge), "upto_made", 1)
                dve.wait_ge(S("counted"), 1)
                then(dve.tensor_copy(cum[:, 0, :], ma[:, 0:NE]), "tb", 1)
                then(dve.tensor_tensor(ge, cum[:, 0, :].unsqueeze(2).broadcast_to([P, NE, N_SHARED]),
                                       io_f[:, N_ROUTED:].unsqueeze(1).broadcast_to([P, NE, N_SHARED]), ALU.is_gt), "tb", 2)
                then(dve.tensor_reduce(cum[:, 1, :], ge, AX.X, ALU.add), "tb", 3)
                then(dve.tensor_tensor(upto[:, 1], upto[:, 0], cum[:, 1, :].unsqueeze(1).broadcast_to([P, NE, NE]),
                                       ALU.mult), "tb", 4)
                then(dve.tensor_reduce(cum[:, 2, :], upto[:, 1], AX.X, ALU.add), "tb", 5)
                ks = io_f[0:1, 0:N_ROUTED]
                then(dve.tensor_tensor(past[:, 0], ks.unsqueeze(2).broadcast_to([1, N_ROUTED, NE]),
                                       cum[0:1, 2, :].unsqueeze(1).broadcast_to([1, N_ROUTED, NE]), ALU.is_ge), "tb", 6)
                dve.tensor_reduce(te[:, 0, :], past[:, 0], AX.X, ALU.add).then_inc(S("tb"), 1)
                then(dve.tensor_tensor(past[:, 1], past[:, 0],
                                       cum[0:1, 1, :].unsqueeze(1).broadcast_to([1, N_ROUTED, NE]), ALU.mult), "tb", 8)
                then(dve.tensor_reduce(te[:, 1, :], past[:, 1], AX.X, ALU.add), "tb", 9)
                then(dve.tensor_tensor(te[:, 2, :], ks, te[:, 1, :], ALU.subtract), "tb", 10)
                then(dve.tensor_scalar(te[:, 2, :], te[:, 2, :], float(TT), None, ALU.mult), "tb", 11)
                then(dve.scalar_tensor_tensor(te[:, 3, :], te[:, 0, :], float(REGION), te[:, 2, :], ALU.mult, ALU.add), "tb", 12)
                tab = keep["tab"]
                dve.tensor_copy(tab[:, 0, 0:N_ROUTED], te[:, 0, :]).then_inc(S("tb"), 1)
                dve.tensor_copy(tab[:, 1, 0:N_ROUTED], te[:, 3, :]).then_inc(S("tb"), 1)
                dve.tensor_scalar(tab[:, 0, N_ROUTED:], io_f[0:1, 0:N_SHARED], 0.0, float(SHARED),
                                  ALU.mult, ALU.add).then_inc(S("tb"), 1)
                dve.tensor_scalar(keep["shift"][:], cum[:, 1, :], float(TT), float(-REGION), ALU.mult, ALU.add).then_inc(S("tb"), 1)
                dve.wait_ge(S("tb"), 16)

            @block.tensor
            def _(pe):
                pe.wait_ge(S("tables_ready"), 1)
                pe.wait_ge(S("const_ready"), 1)

                def scores(b, par, g, u):
                    i = b * 24 + g * 6 + u
                    if not isinstance(b, int) or i >= 2:
                        pe.wait_ge(S("exp_done"), i - 1)
                    slot = slots[u % 2]
                    if u in (2, 5):
                        jobs = [(4 * g + (0 if u == 2 else 2) + r, 2, 256 * r, r == 0) for r in range(2)]
                    else:
                        h = 4 * g + (0, 1, None, 2, 3)[u]
                        jobs = [(h, 0, 0, True), (h, 1, 512, True), (h, 3, 896, False)]
                    for h, j, col, first in jobs:
                        rows = slice(64 * (h // 8), 64 * (h // 8) + 64)
                        pe.matmul(slot[:, col:col + T - P * j],
                                  stk[rows, par, 1, h % 8, P * j:P * j + P],
                                  stk[rows, par, 0, h % 8, P * j:T], start=first, stop=False, skip_group_check=True)
                    for h, j, col, first in jobs:
                        last = pe.matmul(slot[:, col:col + P], ident_b[:], mask_b[:], start=False, stop=True,
                                         skip_group_check=True)
                    last.then_inc(S("unit_ready"), 1)

                def attended(b, par, p):
                    g = p // 4
                    s = b * 4 + g
                    pe.wait_ge(S("exp_done"), s * 6)
                    pe.wait_ge(S("ma_free"), (b + (0 if p == 0 else 1)) * N_MA + 1)
                    if not isinstance(b, int) or s >= 2:
                        pe.wait_ge(S("raw_done"), s - 1)
                    vp = (1 - par) if p == 0 else par
                    gg = (g - 1) % 4
                    for j in range(NT):
                        for r in range(4):
                            last = pe.matmul(pv_bank[32 * r:32 * r + 32, P * j:T],
                                             vst[:, vp, j, 4 * gg + r, :],
                                             prob[:, (g - 1) % 2, r, SEG[j]:SEG[j] + T - P * j],
                                             start=(j == 0), stop=(j == NT - 1), skip_group_check=True)
                    last.then_inc(S("pv_done"), 1)

                def turn(b, par, front, attend, back):
                    order_a, order_b, order_c = (MA, MB, MC) if attend else (MA_FIRST, MB_LAST, MC_LAST)
                    for p in range(POSITIONS):
                        g = p // 4
                        if p == 0 and back:
                            attended(b, par, 0)
                        if attend and p < 16:
                            if p % 8 == 0:
                                pe.wait_ge(S(f"stk_in{p // 8}"), (b + 1) * (10 * 16))
                            for u in ((0, 1), (2,), (3,), (4, 5))[p % 4]:
                                scores(b, par, g, u)
                        if 0 < p < 16 and p % 4 == 0 and attend:
                            attended(b, par, p)
                        for u in at(P_BIAS if attend else L_BIAS, p):
                            if back:
                                pe.wait_ge(S("mc_free"), (b - 1) * N_MC + max(order_c["bias", u], order_c["rank", u] + 1) + 1)
                                for j in range(2):
                                    last = pe.matmul(mc[:, j * D:(j + 1) * D], combT[:, 2 * u + j, :], bias2[:], start=True, stop=True)
                                last.then_inc(S("bias_done"), 1)
                        for t in at(P_QK if attend else F_QK, p):
                            if front:
                                pe.wait_ge(S("xT_split"), b + 2)
                                pe.wait_ge(S("ma_free"), (b + 1) * N_MA + order_a["qk", t] + 1)
                                product(ma[:, 0:2 * D], xTh, t, wqkv, slice(0, 2 * D)).then_inc(S("qk_done"), 1)
                        for t in at(P_NAT if attend else L_NAT, p):
                            if back:
                                pe.wait_ge(S("raw_done"), b * 4)
                                pe.wait_ge(S("mb_free"), (b - 1) * N_MB + order_b["nat", t] + 1)
                                for q in range(4):
                                    last = pe.transpose(mb[:, P * q:P * q + P], raw[:, 1 - par, q, P * t:P * t + P],
                                                        ident_f[:])
                                last.then_inc(S("nat_done"), 1)
                        for t in at(P_T if attend else F_T, p):
                            if front:
                                pe.wait_ge(S("nat_ready"), tiles(b + 1, t))
                                pe.wait_ge(S("ma_free"), (b + 1) * N_MA + order_a["t", t] + 1)
                                for k in range(8):
                                    last = pe.transpose(ma[:, 64 * k:64 * k + 64].bitcast(F16),
                                                        nat[:, t, k % 2, P * (k // 2):P * (k // 2) + P], ident_h[:])
                                last.then_inc(S("t_done"), 1)
                        for u in at(P_AT if attend else L_AT, p):
                            if back:
                                pe.wait_ge(S("an_ready"), pairs(b - 1, u))
                                pe.wait_ge(S("mb_free"), (b - 1) * N_MB + order_b["at", u] + 1)
                                for j in range(2):
                                    for k in range(4):
                                        c = 64 * (4 * j + k)
                                        last = pe.transpose(mb[:, c:c + 64].bitcast(F16),
                                                            anh[:, 2 * u + j, k // 2, P * (k % 2):P * (k % 2) + P], ident_h[:])
                                last.then_inc(S("at_done"), 1)
                        for u in at(P_V if attend else F_V, p):
                            if front:
                                pe.wait_ge(S("ma_free"), (b + 1) * N_MA + order_a["v", u] + 1)
                                for j in range(2):
                                    last = product(ma[:, j * D:(j + 1) * D], xTh, 2 * u + j, wqkv, slice(2 * D, 3 * D))
                                last.then_inc(S("v_done"), 1)
                        for u in at(P_PROJ if attend else L_PROJ, p):
                            if back:
                                pe.wait_ge(S("mb_free"), (b - 1) * N_MB + max(order_b["proj", u], order_b["at", u] + 1) + 1)
                                pieces = [(x, w, c) for c in range(DC) for x, w in ((0, 0), (0, 1), (1, 0))]
                                for j in range(2):
                                    for n, (x, w, c) in enumerate(pieces):
                                        last = pe.matmul(mb[:, j * D:(j + 1) * D], aT[:, u, j, x * DC + c, :], wproj[:, w, c, :],
                                                         start=(n == 0), stop=(n == len(pieces) - 1))
                                last.then_inc(S("proj_done"), 1)
                        for u in at(P_XN if attend else L_XN, p):
                            if back:
                                pe.wait_ge(S("xn_lo"), pairs(b - 1, u))
                                pe.wait_ge(S("mc_free"), (b - 1) * N_MC + order_c["xn", u] + 1)
                                for j in range(2):
                                    for k in range(4):
                                        c = 64 * (4 * j + k)
                                        last = pe.transpose(mc[:, c:c + 64].bitcast(F16),
                                                            xnh[:, 2 * u + j, k // 2, P * (k % 2):P * (k % 2) + P], ident_h[:])
                                last.then_inc(S("xnT_done"), 1)
                        for u in at(P_RANK if attend else L_RANK, p):
                            if back:
                                pe.wait_ge(S("comb_ready"), pairs(b - 1, u))
                                pe.wait_ge(S("mh_ready"), pairs(b - 1, u))
                                pe.wait_ge(S("msum_free"), tiles(b - 1, 2 * u))
                                pe.wait_ge(S("mc_free"), (b - 1) * N_MC + order_c["rank", u] + 1)
                                for j in range(2):
                                    pe.transpose(mc[0:NE + 1, (j + 1) * P:(j + 2) * P], comb[:, 2 * u + j, :], ident_f[:])
                                for j in range(2):
                                    cols = slice(j * NE, (j + 1) * NE)
                                    pe.matmul(mc[:, cols], tri_h[:], mh[:, 2 * u + j, :], start=True, stop=False)
                                    if j:
                                        pe.matmul(mc[:, cols], ones_h[:], mh[:, 2 * u, :], start=False, stop=False)
                                    last = pe.matmul(mc[:, cols], ones_h[:], msum[:], start=False, stop=True)
                                last.then_inc(S("rank_done"), 1)
                        for u in at(P_LG if attend else L_LG, p):
                            if back:
                                pe.wait_ge(S("mc_free"), (b - 1) * N_MC + max(order_c["lg", u], order_c["xn", u] + 1) + 1)
                                pieces = [(x, w, c) for c in range(DC) for x in range(2) for w in range(2)]
                                for j in range(2):
                                    for n, (x, w, c) in enumerate(pieces):
                                        last = pe.matmul(mc[:, j * NE:(j + 1) * NE], xnT[:, u, j, x * DC + c, :], wrout[:, w, c, :],
                                                         start=(n == 0), stop=(n == len(pieces) - 1))
                                last.then_inc(S("lg_done"), 1)

                def product(out, xh, t, w, cols):
                    pieces = [(x, y, c) for c in range(DC) for x, y in ((0, 0), (0, 1), (1, 0))]
                    for n, (x, y, c) in enumerate(pieces):
                        last = pe.matmul(out, xh[:, x, c, P * t:P * t + P], w[:, y, c, cols],
                                         start=(n == 0), stop=(n == len(pieces) - 1))
                    return last

                turns(pe, turn)
                pe.wait_ge(S("msum_free"), NTILE + 1)
                pe.matmul(ma[:, 0:NE], ones_h[:], msum[:], start=True, stop=True).then_inc(S("counted"), 1)


N_CHUNKS = 4 * (NE + 1)
CH = H
EW = 4 * 2 * CH
R_LAST = N_ROUTED - 1
assert N_ROUTED % 2 == 1 and N_SHARED % 2 == 0


def expert_block(nc, a, S, keep):
    with ExitStack() as ctx:
        def sb(name, shape, dt):
            return ctx.enter_context(nc.sbuf_tensor(name, shape, dt))

        def ps(name, cols):
            return ctx.enter_context(nc.psum_tensor(name, [P, cols], F32))

        tab = keep["tab"]
        wts = sb("wts", [P, (NE + 1) * EW], F16)
        b1 = sb("b1", [P, (NE + 1) * HC], F32)
        ident = sb("ident2", [P, P], F16)
        idx = sb("idx", [P, 2, 2], I32)
        xg = sb("xg", [P, 2, 2, 2 * D], F16)
        xgT = sb("xgT", [P, 2, 4, TT], F16)
        hf = sb("hf", [P, HC, TT], F32)
        hh = sb("hh", [P, 2, 2, HC, TT], F16)
        yb = sb("yb", [P, 2, 2, D], F32)
        yrow = sb("yrow", [P, 2, 2 * NTILE], F32)
        yidx = sb("yidx", [P, 2, 2, TOPK], I32)
        yk = sb("yk", [P, 2, TOPK, 2, D], F32)
        rs = sb("rs", [P, 2, 2, D], F32)
        acc = sb("acc", [P, 2, 2, D], F32)
        ob = sb("ob", [P, 2, 2, D], F32)
        st = sb("st", [P, 2, 2, 6], F32)
        mean_var = sb("mean_var", [P, 2, 2, 2], F32)
        var_eps = sb("var_eps", [P, 2, 2], F32)
        rstd = sb("rstd_f", [P, 2, 2], F32)
        half = sb("half_f", [P, 2], F32)
        tr = [ps(f"tr{i}", 512) for i in range(2)]
        hb = [ps(f"hb{i}", 512) for i in range(4)]
        ybank = [ps(f"yb{i}", 512) for i in range(2)]

        def first(par):
            return (R_LAST + 1 + 1 - par) // 2

        def tiles_of(eng, step):
            step(0, 0, 0)
            step(0, 1, 1)
            with eng.Fori(1, (R_LAST - 4) // 2) as h:
                step(h, 0, None)
                step(h, 1, None)
            for i in range(R_LAST - 4, R_LAST + 4):
                step(i // 2, i % 2, i)
            with eng.Fori((R_LAST + 4) // 2, (N_TILES - 3) // 2) as h:
                step(h, 0, R_LAST + 4)
                step(h, 1, R_LAST + 5)
            for i in range(N_TILES - 3, N_TILES):
                step(i // 2, i % 2, i)

        def shared(i):
            return i is not None and i > R_LAST

        with nc.Block() as block:
            @block.gpsimd
            def _(pool):
                pool.memset(half[:], -0.5).then_inc(S("half_made"), 1)

                def gather(h, par):
                    wait_apart(pool, S, f"idx_loaded{par}", (h + 1) * 16)
                    if not isinstance(h, int) or h >= 1:
                        wait_apart(pool, S, "tr_done", h * 2 + par - 1)
                    for j in range(2):
                        pool.indirect_dma_start(xg[:, par, j, :], None, a["xn_rows"],
                                                bass.IndirectOffsetOnAxis(ap=idx[:, par, j:j + 1], axis=0)
                                                ).then_inc(S(f"gathered{par}"), 16)

                def gather_routed(h, par):
                    wait_apart(pool, S, "yidx_ready", h * 2 + par - R_LAST)
                    for k in range(TOPK):
                        for j in range(2):
                            pool.indirect_dma_start(yk[:, par, k, j, :], None, a["y_rows"],
                                                    bass.IndirectOffsetOnAxis(ap=yidx[:, par, j, k:k + 1], axis=0)
                                                    ).then_inc(S(f"y_gathered{par}"), 16)

                def root(h, par):
                    pool.wait_ge(S("f_var"), h * 2 + par - R_LAST)
                    pool.tensor_tensor(rstd[:, par, :], var_eps[:, par, :], half[:], ALU.pow).then_inc(S("f_rstd"), 1)

                gather(0, 0)
                gather(0, 1)
                with pool.Fori(1, R_LAST // 2) as h:
                    gather(h, 0)
                    gather(h, 1)
                gather(R_LAST // 2, 0)
                wait_apart(pool, S, "y_stored0", 16 * ((N_ROUTED + 1) // 2))
                wait_apart(pool, S, "y_stored1", 16 * (N_ROUTED // 2))
                pool.wait_ge(S("half_made"), 1)
                h0 = R_LAST // 2
                gather_routed(h0, 1)
                with pool.Fori(h0 + 1, N_TILES // 2) as h:
                    gather_routed(h, 0)
                    root(h - 1, 1)
                    gather_routed(h, 1)
                    root(h, 0)
                gather_routed(N_TILES // 2, 0)
                root(N_TILES // 2 - 1, 1)
                root(N_TILES // 2, 0)

            @block.sync
            def _(sp):
                sp.dma_start(b1[:], a["b1"]).then_inc(S("b1_in"), 16)

                for u in range(2 * (NE + 1)):
                    sp.dma_start(wts[:, u * EW // 2:(u + 1) * EW // 2].rearrange("p (c f) -> p c f", c=2),
                                 a["w_split"][u * 2 * P:(u + 1) * 2 * P, :].rearrange("(c p) f -> p c f", p=P)
                                 ).then_inc(S("w_in"), 16)
                    if u != 0:
                        sp.wait_ge(S("w_in"), 16 * (u + 1))
                    if u % 2:
                        sp.sem_inc(S("experts_in"), 1)

                def load_shared(h, par):
                    tok = (h * 2 + par - N_ROUTED) * TT
                    wait_apart(sp, S, "tr_done", h * 2 + par - 1)
                    sp.dma_start(xg[:, par, :, :], a["xn_rows"][bass.ds(tok, TT), :].rearrange("(j p) d -> p j d", p=P)
                                 ).then_inc(S(f"rows_in{par}"), 16)

                def load_rest(h, par):
                    tok = (h * 2 + par - N_ROUTED) * TT
                    if not isinstance(h, int) or h > first(par):
                        wait_apart(sp, S, "routed_added", h * 2 + par - R_LAST - 2)
                    sp.dma_start(rs[:, par, :, :], a["resid"][bass.ds(tok, TT), :].rearrange("(j p) d -> p j d", p=P)
                                 ).then_inc(S(f"res_in{par}"), 16)

                def store(h, par):
                    tok = (h * 2 + par - N_ROUTED) * TT
                    wait_apart(sp, S, "out_ready", h * 2 + par - R_LAST)
                    sp.dma_start(a["out"][bass.ds(tok, TT), :].rearrange("(j p) d -> p j d", p=P), ob[:, par, :, :]
                                 ).then_inc(S(f"out_stored{par}"), 16)

                h0, h1 = R_LAST // 2, N_TILES // 2
                load_shared(h0, 1)
                load_rest(h0, 1)
                load_shared(h0 + 1, 0)
                load_rest(h0 + 1, 0)
                load_shared(h0 + 1, 1)
                load_shared(h0 + 2, 0)
                with sp.Fori(h0 + 1, h1 - 1) as h:
                    load_shared(h + 1, 1)
                    load_rest(h, 1)
                    store(h - 1, 1)
                    load_shared(h + 2, 0)
                    load_rest(h + 1, 0)
                    store(h, 0)
                h = h1 - 1
                load_rest(h, 1)
                store(h - 1, 1)
                load_rest(h + 1, 0)
                store(h, 0)
                store(h, 1)
                store(h + 1, 0)
                for par in range(2):
                    sp.wait_ge(S(f"out_stored{par}"), 16 * (N_SHARED // 2))

            @block.scalar
            def _(act):
                def load_ids(h, par):
                    row = act.value_load(tab[0:1, 1, bass.ds(h * 2 + par, 1)], min_val=0, max_val=N_ROWS - TT)
                    if not isinstance(h, int) or h >= 1:
                        act.wait_ge(S(f"gathered{par}"), h * 32)
                    act.dma_start(idx[:, par, :], a["table"][bass.ds(row, TT), :].rearrange("(p j) o -> p (j o)", j=2)
                                  ).then_inc(S(f"idx_loaded{par}"), 16)

                def store(h, par):
                    i = h * 2 + par
                    act.wait_ge(S("y_ready"), i + 1)
                    act.dma_start(a["y_rows"][bass.ds(i * TT, TT), :].rearrange("(p j) d -> p j d", j=2), yb[:, par, :, :]
                                  ).then_inc(S(f"y_stored{par}"), 16)

                def hidden(h, par):
                    i = h * 2 + par
                    e = act.value_load(tab[0:1, 0, bass.ds(i, 1)], min_val=0, max_val=NE)
                    if not isinstance(h, int) or h >= 1:
                        act.wait_ge(S("h_lo"), i * 2)
                        act.wait_ge(S("y_done"), i - 1)
                    elif par == 1:
                        act.wait_ge(S("h_lo"), i * 2)
                    for c in range(HC):
                        if c % 2 == 0:
                            act.wait_ge(S("h_done"), i * (HC // 2) + c // 2 + 1)
                        act.activation(hf[:, c, :], hb[c // 2][:, (c % 2) * TT:(c % 2) * TT + TT], ACT.Relu,
                                       bias=b1[:, bass.ds(e * HC + c, 1)], scale=1.0 / WS).then_inc(S("relu_done"), 1)
                        if c % (HC // 2) == HC // 2 - 1:
                            cs = slice(c + 1 - HC // 2, c + 1)
                            act.wait_ge(S("relu_done"), i * HC + c + 1)
                            act.activation(hh[:, par, 0, cs, :], hf[:, cs, :], ACT.Copy).then_inc(S("h_hi"), 1)

                for i in range(4):
                    load_ids(i // 2, i % 2)
                act.wait_ge(S("b1_in"), 16)
                hidden(0, 0)

                def step(h, par, i):
                    if i is None or i + 4 <= R_LAST:
                        load_ids(h + 2, par)
                    if i == R_LAST + 1:
                        store(h - 1 + par, 1 - par)
                    if i is None or i + 1 < N_TILES:
                        hidden(h + par, 1 - par)
                    if i is None or 1 <= i <= R_LAST:
                        store(h - 1 + par, 1 - par)

                tiles_of(act, step)
                act.wait_ge(S("y_stored0"), 16 * ((N_ROUTED + 1) // 2))
                act.wait_ge(S("y_stored1"), 16 * (N_ROUTED // 2))

            @block.vector
            def _(dve):
                def then(ins, name, count):
                    ins.then_inc(S(name), 1)
                    dve.wait_ge(S(name), count)

                def then_apart(ins, name, count):
                    ins.then_inc(S(name), 1)
                    wait_apart(dve, S, name, count)

                dve.tensor_copy(ident[:], keep["ident"][:]).then_inc(S("ident_copied"), 1)
                then(dve.tensor_copy(yrow[:, 0, :], keep["slots"][:]), "yr", 1)
                for e in range(1, NE):
                    then(dve.tensor_scalar(yrow[:, 1, :], keep["slots"][:], float(e * REGION), keep["shift"][:, e - 1:e],
                                           ALU.is_ge, ALU.mult), "yr", 2 * e)
                    then(dve.tensor_tensor(yrow[:, 0, :], yrow[:, 0, :], yrow[:, 1, :], ALU.add), "yr", 1 + 2 * e)
                then(dve.tensor_copy(keep["rows"][:], yrow[:, 0, :]), "yr", 2 * NE)

                def turned(h, par):
                    dve.wait_ge(S("tr_done"), h * 2 + par + 1)
                    dve.tensor_copy(xgT[:, par].rearrange("p k t -> p (k t)"),
                                    tr[par][:, :].bitcast(F16)).then_inc(S("xgT_ready"), 1)

                def split_hidden(h, par):
                    i = h * 2 + par
                    for half in range(2):
                        cs = slice(half * HC // 2, (half + 1) * HC // 2)
                        dve.wait_ge(S("h_hi"), i * 2 + half + 1)
                        dve.tensor_tensor(hh[:, par, 1, cs, :], hf[:, cs, :], hh[:, par, 0, cs, :],
                                          ALU.subtract).then_inc(S("h_lo"), 1)

                def output(h, par):
                    i = h * 2 + par
                    dve.wait_ge(S("y_done"), i + 1)
                    if not isinstance(h, int) or h >= 1:
                        dve.wait_ge(S(f"y_stored{par}"), h * 16)
                    dve.tensor_scalar(yb[:, par].rearrange("p j d -> p (j d)"), ybank[par][:, :], 1.0 / WS, None,
                                      ALU.mult).then_inc(S("y_ready"), 1)

                def pick(h, par):
                    s = h * 2 + par - N_ROUTED
                    dve.tensor_copy(yidx[:, par, :, :].rearrange("p j k -> p (j k)"),
                                    keep["rows"][:, bass.ds(s * 2 * TOPK, 2 * TOPK)]).then_inc(S("yidx_ready"), 1)

                def add_routed(h, par):
                    n = h * 2 + par - R_LAST
                    r = h - first(par) + 1
                    dve.wait_ge(S(f"y_gathered{par}"), r * (2 * TOPK * 16))
                    dve.wait_ge(S(f"res_in{par}"), r * 16)
                    for k in range(TOPK):
                        for j in range(2):
                            w = keep["weights"][:, bass.ds((n - 1) * 2 * TOPK + j * TOPK + k, 1)]
                            dve.scalar_tensor_tensor(acc[:, par, j, :], yk[:, par, k, j, :], w,
                                                     (rs if k == 0 else acc)[:, par, j, :],
                                                     ALU.mult, ALU.add).then_inc(S("weighted"), 1)
                        dve.wait_ge(S("weighted"), n * 4 - 2 + 2 * k)
                    dve.sem_inc(S("routed_added"), 1)

                def combine(h, par):
                    i, n = h * 2 + par, h * 2 + par - R_LAST
                    dve.wait_ge(S("y_done"), i + 1)
                    flat = acc[:, par].rearrange("p j d -> p (j d)")
                    then_apart(dve.scalar_tensor_tensor(flat, ybank[par][:, :], 1.0 / WS, flat, ALU.mult, ALU.add),
                               "y_ready", i + 1)
                    for j in range(2):
                        dve.bn_stats(st[:, par, j, :], acc[:, par, j, :]).then_inc(S("f_st"), 1)
                    for j in range(2):
                        wait_apart(dve, S, "f_st", n * 2 - 1 + j)
                        dve.bn_aggr(mean_var[:, par, j, :], st[:, par, j, :]).then_inc(S("f_mv"), 1)
                    dve.wait_ge(S("f_mv"), n * 2)
                    dve.tensor_scalar(var_eps[:, par, :], mean_var[:, par, :, 1], LN_EPS, None, ALU.add).then_inc(S("f_var"), 1)

                def finish(h, par):
                    dve.wait_ge(S("f_rstd"), h * 2 + par - R_LAST)
                    if not isinstance(h, int) or h > first(par):
                        dve.wait_ge(S(f"out_stored{par}"), (h - first(par)) * 16)
                    for j in range(2):
                        ins = dve.tensor_scalar(ob[:, par, j, :], acc[:, par, j, :], mean_var[:, par, j, 0:1],
                                                rstd[:, par, j:j + 1], ALU.subtract, ALU.mult).then_inc(S("f_out"), 1)
                    dve.wait_ge(S("f_out"), (h * 2 + par - R_LAST) * 2)
                    dve.sem_inc(S("out_ready"), 1)

                def step(h, par, i):
                    if i is None or i + 2 < N_TILES:
                        turned(h + 1, par)
                    if i is None or i + 1 < N_TILES:
                        split_hidden(h + par, 1 - par)
                    if shared(i):
                        if i < N_TILES - 1:
                            pick(h + par, 1 - par)
                        add_routed(h, par)
                        if i > R_LAST + 1:
                            finish(h - 1 + par, 1 - par)
                        combine(h, par)
                    else:
                        output(h, par)
                        if i == R_LAST:
                            pick(h, 1)

                turned(0, 0)
                turned(0, 1)
                split_hidden(0, 0)
                tiles_of(dve, step)
                finish(N_TILES // 2, 0)

            @block.tensor
            def _(pe):
                pe.wait_ge(S("ident_copied"), 1)

                def turn_rows(h, par, i):
                    if shared(i):
                        pe.wait_ge(S(f"rows_in{par}"), (h - first(par) + 1) * 16)
                    else:
                        pe.wait_ge(S(f"gathered{par}"), (h + 1) * 32)
                    if not isinstance(h, int) or h >= 1:
                        pe.wait_ge(S("xgT_ready"), h * 2 + par - 1)
                    for k in range(4):
                        for j in range(2):
                            c = (2 * k + j) * 64
                            last = pe.transpose(tr[par][:, c:c + 64].bitcast(F16), xg[:, par, j, P * k:P * k + P], ident[:])
                    last.then_inc(S("tr_done"), 1)

                PIECES = ((0, 0), (0, 1), (1, 0))

                def weights(e, chunk, w, col, n):
                    return wts[:, bass.ds(e * EW + (chunk * 2 * CH + w * CH + col), n)]

                def hidden(h, par):
                    i = h * 2 + par
                    e = pe.value_load(tab[0:1, 0, bass.ds(i, 1)], min_val=0, max_val=NE)
                    pe.wait_ge(S("experts_in"), e + 1)
                    pe.wait_ge(S("xgT_ready"), i + 1)
                    for hc in range(HC):
                        if hc % 2 == 0 and (not isinstance(h, int) or i >= 1):
                            pe.wait_ge(S("relu_done"), (i - 1) * HC + hc + 2)
                        n = 0
                        for c in range(DC):
                            for x, w in PIECES:
                                last = pe.matmul(hb[hc // 2][:, (hc % 2) * TT:(hc % 2) * TT + TT],
                                                 weights(e, c, w, hc * P, P), xgT[:, par, x * DC + c, :],
                                                 start=(n == 0), stop=(n == 5))
                                n += 1
                        if hc % 2:
                            last.then_inc(S("h_done"), 1)

                def output(h, par):
                    i = h * 2 + par
                    e = pe.value_load(tab[0:1, 0, bass.ds(i, 1)], min_val=0, max_val=NE)
                    pe.wait_ge(S("h_lo"), (i + 1) * 2)
                    if not isinstance(h, int) or h >= 1:
                        pe.wait_ge(S("y_ready"), i - 1)
                    for j in range(2):
                        n = 0
                        for hc in range(HC):
                            for x, w in PIECES:
                                last = pe.matmul(ybank[par][:, j * D:(j + 1) * D],
                                                 hh[:, par, x, hc, P * j:P * j + P],
                                                 weights(e, DC + hc * D // CH, w, hc * D % CH, D),
                                                 start=(n == 0), stop=(n == 3 * HC - 1))
                                n += 1
                    last.then_inc(S("y_done"), 1)

                turn_rows(0, 0, 0)
                turn_rows(0, 1, 1)
                hidden(0, 0)

                def step(h, par, i):
                    if i is None or i + 2 < N_TILES:
                        turn_rows(h + 1, par, None if i is None else i + 2)
                    if i is None or i + 1 < N_TILES:
                        hidden(h + par, 1 - par)
                    output(h, par)

                tiles_of(pe, step)


def layer(nc, a):
    with ExitStack() as ctx:
        named = {}

        def S(name):
            if name not in named:
                named[name] = ctx.enter_context(nc.semaphore(name))
            return named[name]

        keep = {
            "slots": ctx.enter_context(nc.sbuf_tensor("keep_slots", [P, 2 * NTILE], F32)),
            "rows": ctx.enter_context(nc.sbuf_tensor("keep_rows", [P, 2 * NTILE], I32)),
            "weights": ctx.enter_context(nc.sbuf_tensor("keep_weights", [P, 2 * NTILE], F32)),
            "msum": ctx.enter_context(nc.sbuf_tensor("keep_msum", [P, NE], F16)),
            "tab": ctx.enter_context(nc.sbuf_tensor("keep_tab", [1, 2, N_TILES], I32)),
            "shift": ctx.enter_context(nc.sbuf_tensor("keep_shift", [P, NE], F32)),
            "ident": ctx.enter_context(nc.sbuf_tensor("keep_ident", [P, P], F16)),
        }
        attention_block(nc, a, S, keep)
        expert_block(nc, a, S, keep)


def kernel(**inputs):
    import concourse.bacc as _bacc
    from concourse import mybir as _mybir
    from concourse.bass_utils import run_bass_kernel_spmd as _run

    v = {k.replace("L0_", ""): np.asarray(x) for k, x in inputs.items()}
    cat = lambda routed, shared: np.concatenate([v[routed], v[shared][None]], axis=0)
    w1 = cat("ffn_ew1", "ffn_sw1").reshape(NE + 1, DC, P, H)
    w2 = cat("ffn_ew2", "ffn_sw2").reshape(NE + 1, 2, HC // 2, P, D).transpose(0, 1, 3, 2, 4).reshape(NE + 1, 2, P, H)
    arrays = {
        "x": v["attn_x"].reshape(NTOK, D),
        "xT": v["attn_x"].transpose(0, 2, 1).reshape(NB * D, T),
        "wqkvT": v["attn_w_qkv"].T,
        "wprojT": v["attn_w_proj"].T,
        "qnw": v["attn_q_norm_w"],
        "knw": v["attn_k_norm_w"],
        "ffn_nw": v["ffn_norm_weight"],
        "routT": v["ffn_router_w"].T,
        "w_all": np.concatenate([w1, w2], axis=1).reshape(N_CHUNKS * P, H),
        "b1": cat("ffn_eb1", "ffn_sb1").reshape(NE + 1, HC, P).transpose(2, 0, 1).reshape(P, (NE + 1) * HC),
        "b2all": cat("ffn_eb2", "ffn_sb2"),
        "trig": rope_tables(),
    }
    arrays = {k: np.ascontiguousarray(x) for k, x in arrays.items()}
    nc = _bacc.Bacc("TRN2", target_bir_lowering=False, num_devices=1)
    a = {k: nc.dram_tensor("in_" + k, x.shape, _mybir.dt.from_np(x.dtype), kind="ExternalInput").ap()
         for k, x in arrays.items()}
    for name, shape, dt in (("qk_dram", (2 * DC, 2, P, T), F16), ("xn_rows", (NTOK, 2 * D), F16), ("resid", (NTOK, D), F32),
                            ("table", (N_ROWS, 1), I32), ("y_rows", (N_ROUTED * TT, D), F32), ("w_split", (N_CHUNKS * P, 2 * H), F16)):
        a[name] = nc.dram_tensor(name, shape, dt, kind="Internal").ap()
    a["out"] = nc.dram_tensor("out", (NTOK, D), F32, kind="ExternalOutput").ap()
    layer(nc, a)
    r = _run(nc, [{"in_" + k: x for k, x in arrays.items()}], core_ids=[0])
    return r.results[0]["out"].reshape(NB, T, D)
```
